# Optimizing a Trainium2 kernel written in Bass

```python
import numpy as np
import jax
import jax.numpy as jnp

def _softmax(x, axis=-1):
    return jax.nn.softmax(x, axis=axis)

def _gelu(x):
    return jax.nn.gelu(x, approximate=True)

def _silu(x):
    return jax.nn.silu(x)

def _sigmoid(x):
    return jax.nn.sigmoid(x)

def _layernorm(x, axis=-1, eps=1e-05):
    m = jnp.mean(x, axis=axis, keepdims=True)
    v = jnp.var(x, axis=axis, keepdims=True)
    return (x - m) / jnp.sqrt(v + eps)

def _scatter_add(tgt, idx, src, axis=0):
    return tgt.at[idx].add(src)

def _segment_sum(src, seg, n):
    return jax.ops.segment_sum(src, seg, n)
kernel_name = 'mk_decoder_preln_d2_seqx_r8_92af5b'

def setup_inputs(seed: int=0):
    np.random.seed(seed)
    _w = jnp.asarray

    def _rec_inputs():
        import jax
        import jax.numpy as jnp
        _rk = jax.random.key(seed)
        x = 7.22e-05 + 1 * jax.random.normal(jax.random.fold_in(_rk, 1), (16, 64, 128), jnp.float32)
        _lenS = 64 - jax.random.randint(jax.random.fold_in(_rk, 7), (16,), 0, max(1, 64 // 4) + 1, jnp.int32)
        _lenS2 = 64 - jax.random.randint(jax.random.fold_in(_rk, 8), (16,), 0, max(1, 64 // 4) + 1, jnp.int32)
        _ctx_768P = jax.random.normal(jax.random.fold_in(_rk, 11), (16, 16, 96), jnp.float32)
        _ctx_768c = jax.random.dirichlet(jax.random.fold_in(_rk, 511), 0.3 * jnp.ones((16,), jnp.float32), (16, 64))
        _ctx_768t = jnp.einsum('bsk,bkd->bsd', _ctx_768c, _ctx_768P)
        _ctx_768t = _ctx_768t * jax.lax.rsqrt(jnp.mean(jnp.square(_ctx_768t)) + 1e-12) * 0.953939
        ctx_768 = -0.000191848 + 0.999787 * (_ctx_768t + 0.3 * jax.random.normal(jax.random.fold_in(_rk, 611), (16, 64, 96), jnp.float32))
        return (x, ctx_768)
    x, ctx_768 = _rec_inputs()

    def _L0_attn_setup():
        import jax, jax.numpy as jnp
        import numpy as np
        B, T, D = (2, 256, 128)
        H = 16
        HD = D // H
        DL = 64
        NR = 64
        EPS = 1.1920929e-07

        def _rms_norm(x, w):
            ms = jnp.mean(jnp.square(x), axis=-1, keepdims=True)
            return x * jax.lax.rsqrt(ms + EPS) * w
        key = jax.random.key(seed)
        ks = jax.random.split(key, 10)
        s = 0.02
        return {'x': jax.random.normal(ks[0], (B, T, D), dtype=jnp.float32), 'W_DQ': jax.random.normal(ks[1], (DL, HD), dtype=jnp.float32) * s, 'W_UQ': jax.random.normal(ks[2], (HD, DL), dtype=jnp.float32) * s, 'W_DKV': jax.random.normal(ks[3], (2 * DL, HD), dtype=jnp.float32) * s, 'W_UKV': jax.random.normal(ks[4], (2 * HD, 2 * DL), dtype=jnp.float32) * s, 'W_QR': jax.random.normal(ks[5], (NR, HD), dtype=jnp.float32) * s, 'W_KR': jax.random.normal(ks[6], (NR, HD), dtype=jnp.float32) * s, 'W_O': jax.random.normal(ks[7], (HD, HD), dtype=jnp.float32) * s, 'q_norm_w': jnp.ones((HD,), dtype=jnp.float32), 'k_norm_w': jnp.ones((HD,), dtype=jnp.float32)}
    _L0_attn_all = _L0_attn_setup()
    _L0_attn_in = {k: v for k, v in _L0_attn_all.items() if k in ('W_DQ', 'W_UQ', 'W_DKV', 'W_UKV', 'W_QR', 'W_KR', 'W_O', 'q_norm_w', 'k_norm_w')}
    del _L0_attn_all

    def _L0_xattn_setup():
        import jax, jax.numpy as jnp
        import numpy as np
        B, LQ, LK = (4, 256, 256)
        D1, D2, H = (128, 96, 128)
        key = jax.random.key(seed)
        ks = jax.random.split(key, 9)
        s1, s2, sh = (1.0 / np.sqrt(D1), 1.0 / np.sqrt(D2), 1.0 / np.sqrt(H))
        return {'query': jax.random.normal(ks[0], (B, LQ, D1), jnp.float32), 'key': jax.random.normal(ks[1], (B, LK, D2), jnp.float32), 'value': jax.random.normal(ks[2], (B, LK, D2), jnp.float32), 'Wq': jax.random.normal(ks[3], (D1, H), jnp.float32) * s1, 'bq': jax.random.normal(ks[4], (H,), jnp.float32) * s1, 'Wk': jax.random.normal(ks[5], (D2, H), jnp.float32) * s2, 'bk': jax.random.normal(ks[6], (H,), jnp.float32) * s2, 'Wv': jax.random.normal(ks[7], (D2, H), jnp.float32) * s2, 'bv': jax.random.normal(ks[8], (H,), jnp.float32) * s2}
    _L0_xattn_all = _L0_xattn_setup()
    _L0_xattn_in = {k: v for k, v in _L0_xattn_all.items() if k in ('Wq', 'bq', 'Wk', 'bk', 'Wv', 'bv')}
    del _L0_xattn_all

    def _L0_ffn_setup():
        import jax, jax.numpy as jnp
        import numpy as np
        B, S, D, H, M, E, K = (8, 256, 128, 256, 64, 8, 2)
        EH = H // 2

        def _layernorm(x, g, b, eps=1e-05):
            mu = jnp.mean(x, axis=-1, keepdims=True)
            var = jnp.var(x, axis=-1, keepdims=True)
            return (x - mu) * jax.lax.rsqrt(var + eps) * g + b
        key = jax.random.key(seed)
        ks = jax.random.split(key, 16)
        sc = lambda *shape: 1.0 / np.sqrt(shape[0])
        return {'inputs_embeds': jax.random.normal(ks[0], (B, S, D), jnp.float32), 'W_enc': jax.random.normal(ks[1], (D, H), jnp.float32) * sc(D), 'b_enc': jnp.zeros((H,), jnp.float32), 'W_s2c': jax.random.normal(ks[2], (H, M), jnp.float32) * sc(H), 'b_s2c': jnp.zeros((M,), jnp.float32), 'Wr': jax.random.normal(ks[3], (M, E), jnp.float32) * sc(M), 'br': jnp.zeros((E,), jnp.float32), 'W1': jax.random.normal(ks[4], (E, M, EH), jnp.float32) * sc(M), 'b1': jnp.zeros((E, EH), jnp.float32), 'W2': jax.random.normal(ks[5], (E, EH, M), jnp.float32) * sc(EH), 'b2': jnp.zeros((E, M), jnp.float32), 'W_c2s': jax.random.normal(ks[6], (M, H), jnp.float32) * sc(M), 'b_c2s': jnp.zeros((H,), jnp.float32), 'W_dec': jax.random.normal(ks[7], (H, D), jnp.float32) * sc(H), 'b_dec': jnp.zeros((D,), jnp.float32), 'ln_g': jnp.ones((D,), jnp.float32), 'ln_b': jnp.zeros((D,), jnp.float32)}
    _L0_ffn_all = _L0_ffn_setup()
    _L0_ffn_in = {k: v for k, v in _L0_ffn_all.items() if k in ('W_enc', 'b_enc', 'W_s2c', 'b_s2c', 'Wr', 'br', 'W1', 'b1', 'W2', 'b2', 'W_c2s', 'b_c2s', 'W_dec', 'b_dec', 'ln_g', 'ln_b')}
    del _L0_ffn_all

    def _L1_attn_setup():
        import jax, jax.numpy as jnp
        import numpy as np
        import math
        DIM = 128
        NUM_HEADS = 16
        BATCH = 2
        SEQ = 256

        def _get_attention_slopes(n):

            def pow2_slopes(n):
                start = 2 ** (-2 ** (-(math.log2(n) - 3)))
                return [start * start ** i for i in range(n)]
            if math.log2(n).is_integer():
                return pow2_slopes(n)
            c = 2 ** math.floor(math.log2(n))
            return pow2_slopes(c) + _get_attention_slopes(2 * c)[0::2][:n - c]
        key = jax.random.key(seed)
        k1, k2, k3 = jax.random.split(key, 3)
        x = jax.random.normal(k1, (BATCH, SEQ, DIM), dtype=jnp.float32)
        w_qkv = jax.random.normal(k2, (DIM, 3 * DIM), dtype=jnp.float32) / np.sqrt(DIM)
        w_proj = jax.random.normal(k3, (DIM, DIM), dtype=jnp.float32) / np.sqrt(DIM)
        return {'x': x, 'w_qkv': w_qkv, 'w_proj': w_proj}
    _L1_attn_all = _L1_attn_setup()
    _L1_attn_in = {k: v for k, v in _L1_attn_all.items() if k in ('w_qkv', 'w_proj')}
    del _L1_attn_all

    def _L1_xattn_setup():
        import jax, jax.numpy as jnp
        import numpy as np
        HEADS = 8
        DIM_HEAD = 64
        SCALE = DIM_HEAD ** (-0.5)
        key = jax.random.key(seed)
        ks = jax.random.split(key, 7)
        B, Nq, Nc = (4, 256, 256)
        Dq, Dc = (128, 96)
        inner = HEADS * DIM_HEAD
        x = jax.random.normal(ks[0], (B, Nq, Dq), dtype=jnp.float32)
        context = jax.random.normal(ks[1], (B, Nc, Dc), dtype=jnp.float32)
        Wq = jax.random.normal(ks[2], (Dq, inner), dtype=jnp.float32) * Dq ** (-0.5)
        Wk = jax.random.normal(ks[3], (Dc, inner), dtype=jnp.float32) * Dc ** (-0.5)
        Wv = jax.random.normal(ks[4], (Dc, inner), dtype=jnp.float32) * Dc ** (-0.5)
        Wo = jax.random.normal(ks[5], (inner, Dq), dtype=jnp.float32) * inner ** (-0.5)
        bo = jax.random.normal(ks[6], (Dq,), dtype=jnp.float32) * 0.01
        return {'x': x, 'context': context, 'Wq': Wq, 'Wk': Wk, 'Wv': Wv, 'Wo': Wo, 'bo': bo}
    _L1_xattn_all = _L1_xattn_setup()
    _L1_xattn_in = {k: v for k, v in _L1_xattn_all.items() if k in ('Wq', 'Wk', 'Wv', 'Wo', 'bo')}
    del _L1_xattn_all

    def _L1_ffn_setup():
        import jax, jax.numpy as jnp
        import numpy as np
        N_EXPERTS = 16
        TOP_K = int(N_EXPERTS * 0.2)
        EPS = 1e-12
        key = jax.random.key(seed)
        ks = jax.random.split(key, 6)
        B, T, D, H, E = (4, 128, 128, 256, N_EXPERTS)
        x = jax.random.normal(ks[0], (B, T, D), dtype=jnp.float32)
        gate = jax.random.normal(ks[1], (D, E), dtype=jnp.float32)
        W1 = jax.random.normal(ks[2], (E, D, H), dtype=jnp.float32) * (1.0 / np.sqrt(D))
        b1 = jax.random.normal(ks[3], (E, H), dtype=jnp.float32) * 0.02
        W2 = jax.random.normal(ks[4], (E, H, D), dtype=jnp.float32) * (1.0 / np.sqrt(H))
        b2 = jax.random.normal(ks[5], (E, D), dtype=jnp.float32) * 0.02
        return {'x': x, 'gate': gate, 'W1': W1, 'b1': b1, 'W2': W2, 'b2': b2}
    _L1_ffn_all = _L1_ffn_setup()
    _L1_ffn_in = {k: v for k, v in _L1_ffn_all.items() if k in ('gate', 'W1', 'b1', 'W2', 'b2')}
    del _L1_ffn_all
    return {'x': x, 'ctx_768': ctx_768, 'L0_attn_W_DQ': _L0_attn_in['W_DQ'], 'L0_attn_W_UQ': _L0_attn_in['W_UQ'], 'L0_attn_W_DKV': _L0_attn_in['W_DKV'], 'L0_attn_W_UKV': _L0_attn_in['W_UKV'], 'L0_attn_W_QR': _L0_attn_in['W_QR'], 'L0_attn_W_KR': _L0_attn_in['W_KR'], 'L0_attn_W_O': _L0_attn_in['W_O'], 'L0_attn_q_norm_w': _L0_attn_in['q_norm_w'], 'L0_attn_k_norm_w': _L0_attn_in['k_norm_w'], 'L0_xattn_Wq': _L0_xattn_in['Wq'], 'L0_xattn_bq': _L0_xattn_in['bq'], 'L0_xattn_Wk': _L0_xattn_in['Wk'], 'L0_xattn_bk': _L0_xattn_in['bk'], 'L0_xattn_Wv': _L0_xattn_in['Wv'], 'L0_xattn_bv': _L0_xattn_in['bv'], 'L0_ffn_W_enc': _L0_ffn_in['W_enc'], 'L0_ffn_b_enc': _L0_ffn_in['b_enc'], 'L0_ffn_W_s2c': _L0_ffn_in['W_s2c'], 'L0_ffn_b_s2c': _L0_ffn_in['b_s2c'], 'L0_ffn_Wr': _L0_ffn_in['Wr'], 'L0_ffn_br': _L0_ffn_in['br'], 'L0_ffn_W1': _L0_ffn_in['W1'], 'L0_ffn_b1': _L0_ffn_in['b1'], 'L0_ffn_W2': _L0_ffn_in['W2'], 'L0_ffn_b2': _L0_ffn_in['b2'], 'L0_ffn_W_c2s': _L0_ffn_in['W_c2s'], 'L0_ffn_b_c2s': _L0_ffn_in['b_c2s'], 'L0_ffn_W_dec': _L0_ffn_in['W_dec'], 'L0_ffn_b_dec': _L0_ffn_in['b_dec'], 'L0_ffn_ln_g': _L0_ffn_in['ln_g'], 'L0_ffn_ln_b': _L0_ffn_in['ln_b'], 'L1_attn_w_qkv': _L1_attn_in['w_qkv'], 'L1_attn_w_proj': _L1_attn_in['w_proj'], 'L1_xattn_Wq': _L1_xattn_in['Wq'], 'L1_xattn_Wk': _L1_xattn_in['Wk'], 'L1_xattn_Wv': _L1_xattn_in['Wv'], 'L1_xattn_Wo': _L1_xattn_in['Wo'], 'L1_xattn_bo': _L1_xattn_in['bo'], 'L1_ffn_gate': _L1_ffn_in['gate'], 'L1_ffn_W1': _L1_ffn_in['W1'], 'L1_ffn_b1': _L1_ffn_in['b1'], 'L1_ffn_W2': _L1_ffn_in['W2'], 'L1_ffn_b2': _L1_ffn_in['b2']}

def reference(x, ctx_768, L0_attn_W_DQ, L0_attn_W_UQ, L0_attn_W_DKV, L0_attn_W_UKV, L0_attn_W_QR, L0_attn_W_KR, L0_attn_W_O, L0_attn_q_norm_w, L0_attn_k_norm_w, L0_xattn_Wq, L0_xattn_bq, L0_xattn_Wk, L0_xattn_bk, L0_xattn_Wv, L0_xattn_bv, L0_ffn_W_enc, L0_ffn_b_enc, L0_ffn_W_s2c, L0_ffn_b_s2c, L0_ffn_Wr, L0_ffn_br, L0_ffn_W1, L0_ffn_b1, L0_ffn_W2, L0_ffn_b2, L0_ffn_W_c2s, L0_ffn_b_c2s, L0_ffn_W_dec, L0_ffn_b_dec, L0_ffn_ln_g, L0_ffn_ln_b, L1_attn_w_qkv, L1_attn_w_proj, L1_xattn_Wq, L1_xattn_Wk, L1_xattn_Wv, L1_xattn_Wo, L1_xattn_bo, L1_ffn_gate, L1_ffn_W1, L1_ffn_b1, L1_ffn_W2, L1_ffn_b2):
    import jax
    import jax.numpy as jnp

    def _L0_attn_ref(x, W_DQ, W_UQ, W_DKV, W_UKV, W_QR, W_KR, W_O, q_norm_w, k_norm_w):
        import jax, jax.numpy as jnp
        import numpy as np
        B, T, D = (2, 256, 128)
        H = 16
        HD = D // H
        DL = 64
        NR = 64
        EPS = 1.1920929e-07

        def _rms_norm(x, w):
            ms = jnp.mean(jnp.square(x), axis=-1, keepdims=True)
            return x * jax.lax.rsqrt(ms + EPS) * w
        b, t, d = x.shape
        scale = HD ** (-0.5)
        xh = x.reshape(b, t, H, HD).transpose(0, 2, 1, 3)
        c_q = jnp.einsum('bhtd,ld->bhtl', xh, W_DQ)
        q_c = jnp.einsum('bhtl,dl->bhtd', c_q, W_UQ)
        q_c_norm = _rms_norm(q_c, q_norm_w)
        q_r = jnp.einsum('bhtd,rd->bhtr', q_c_norm, W_QR)
        q = jnp.concatenate([q_c_norm, q_r], axis=-1)
        c_kv = jnp.einsum('bhtd,ld->bhtl', xh, W_DKV)
        kv = jnp.einsum('bhtl,dl->bhtd', c_kv, W_UKV)
        k_c, v_c = (kv[..., :HD], kv[..., HD:])
        k_c_norm = _rms_norm(k_c, k_norm_w)
        k_r = jnp.einsum('bhtd,rd->bhtr', xh, W_KR)
        k = jnp.concatenate([k_c_norm, k_r], axis=-1)
        scores = jnp.einsum('bhqd,bhkd->bhqk', q, k) * scale
        causal = jnp.triu(jnp.full((t, t), -jnp.inf, dtype=scores.dtype), k=1)
        attn = jax.nn.softmax(scores + causal, axis=-1)
        ctx = jnp.einsum('bhqk,bhkd->bhqd', attn, v_c)
        out = jnp.einsum('bhtd,od->bhto', ctx, W_O)
        return out.transpose(0, 2, 1, 3).reshape(b, t, d)

    def _L0_xattn_ref(query, key, value, Wq, bq, Wk, bk, Wv, bv):
        import jax, jax.numpy as jnp
        import numpy as np
        B, LQ, LK = (4, 256, 256)
        D1, D2, H = (128, 96, 128)
        q = jnp.einsum('bqd,dh->bqh', query, Wq) + bq
        k = jnp.einsum('bkd,dh->bkh', key, Wk) + bk
        v = jnp.einsum('bkd,dh->bkh', value, Wv) + bv
        scores = jnp.einsum('bqh,bkh->bqk', q, k)
        weights = jax.nn.softmax(scores, axis=-1)
        return jnp.einsum('bqk,bkh->bqh', weights, v)

    def _L0_ffn_ref(inputs_embeds, W_enc, b_enc, W_s2c, b_s2c, Wr, br, W1, b1, W2, b2, W_c2s, b_c2s, W_dec, b_dec, ln_g, ln_b):
        import jax, jax.numpy as jnp
        import numpy as np
        B, S, D, H, M, E, K = (8, 256, 128, 256, 64, 8, 2)
        EH = H // 2

        def _layernorm(x, g, b, eps=1e-05):
            mu = jnp.mean(x, axis=-1, keepdims=True)
            var = jnp.var(x, axis=-1, keepdims=True)
            return (x - mu) * jax.lax.rsqrt(var + eps) * g + b
        b, s, d = inputs_embeds.shape
        spikes_enc = jax.nn.sigmoid(inputs_embeds @ W_enc + b_enc)
        flat = spikes_enc.reshape(b * s, -1)
        cont = flat @ W_s2c + b_s2c
        probs = jax.nn.softmax(cont @ Wr + br, axis=-1)
        topk_w, topk_idx = jax.lax.top_k(probs, K)
        topk_w = topk_w / jnp.sum(topk_w, axis=-1, keepdims=True)
        gate = jnp.sum(jax.nn.one_hot(topk_idx, E, dtype=cont.dtype) * topk_w[..., None], axis=1)
        h = jax.nn.relu(jnp.einsum('tm,emh->eth', cont, W1) + b1[:, None, :])
        y = jnp.einsum('eth,ehm->etm', h, W2) + b2[:, None, :]
        expert_out = jnp.einsum('etm,te->tm', y, gate)
        spikes_moe = jax.nn.sigmoid(expert_out @ W_c2s + b_c2s)
        spikes_moe = spikes_moe.reshape(b, s, -1)
        decoded = spikes_moe @ W_dec + b_dec
        return _layernorm(decoded, ln_g, ln_b)

    def _L1_attn_ref(x, w_qkv, w_proj):
        import jax, jax.numpy as jnp
        import numpy as np
        import math
        DIM = 128
        NUM_HEADS = 16
        BATCH = 2
        SEQ = 256

        def _get_attention_slopes(n):

            def pow2_slopes(n):
                start = 2 ** (-2 ** (-(math.log2(n) - 3)))
                return [start * start ** i for i in range(n)]
            if math.log2(n).is_integer():
                return pow2_slopes(n)
            c = 2 ** math.floor(math.log2(n))
            return pow2_slopes(c) + _get_attention_slopes(2 * c)[0::2][:n - c]
        B, N, D = x.shape
        H = NUM_HEADS
        Dh = D // H
        qkv = x @ w_qkv
        q, k, v = jnp.split(qkv, 3, axis=-1)
        split_heads = lambda t: t.reshape(B, N, H, Dh).transpose(0, 2, 1, 3)
        q, k, v = (split_heads(q), split_heads(k), split_heads(v))
        scale = Dh ** (-0.5)
        att = jnp.einsum('bhnd,bhmd->bhnm', q, k) * scale
        slopes = jnp.asarray(_get_attention_slopes(H), dtype=att.dtype)
        pos_bias = slopes[None, :, None, None] * jnp.arange(N, dtype=att.dtype)[None, None, None, :]
        att = att + pos_bias
        big_neg = jnp.finfo(att.dtype).min
        causal = jnp.tril(jnp.ones((N, N), dtype=bool))[None, None]
        att = jnp.where(causal, att, big_neg)
        att = jax.nn.softmax(att, axis=-1)
        out = jnp.einsum('bhnm,bhmd->bhnd', att, v)
        out = out.transpose(0, 2, 1, 3).reshape(B, N, D)
        return out @ w_proj

    def _L1_xattn_ref(x, context, Wq, Wk, Wv, Wo, bo):
        import jax, jax.numpy as jnp
        import numpy as np
        HEADS = 8
        DIM_HEAD = 64
        SCALE = DIM_HEAD ** (-0.5)
        B, Nq, _ = x.shape
        q = (x @ Wq).reshape(B, Nq, HEADS, DIM_HEAD)
        k = (context @ Wk).reshape(B, context.shape[1], HEADS, DIM_HEAD)
        v = (context @ Wv).reshape(B, context.shape[1], HEADS, DIM_HEAD)
        sim = jnp.einsum('bihd,bjhd->bhij', q, k) * SCALE
        attn = jax.nn.softmax(sim, axis=-1)
        out = jnp.einsum('bhij,bjhd->bihd', attn, v)
        out = out.reshape(B, Nq, HEADS * DIM_HEAD)
        return out @ Wo + bo

    def _L1_ffn_ref(x, gate, W1, b1, W2, b2):
        import jax, jax.numpy as jnp
        import numpy as np
        N_EXPERTS = 16
        TOP_K = int(N_EXPERTS * 0.2)
        EPS = 1e-12
        raw_gate = jax.nn.softmax(jnp.einsum('btd,de->bte', x, gate), axis=-1)
        _, topk_idx = jax.lax.top_k(raw_gate, TOP_K)
        mask = jax.nn.one_hot(topk_idx, raw_gate.shape[-1], dtype=raw_gate.dtype).sum(axis=2)
        gate_topk = mask * raw_gate
        gate_topk = gate_topk / jnp.maximum(jnp.sum(jnp.abs(gate_topk), axis=-1, keepdims=True), EPS)
        hidden = jax.nn.relu(jnp.einsum('btd,edh->bteh', x, W1) + b1)
        expert_out = jnp.einsum('bteh,ehd->bted', hidden, W2) + b2
        return jnp.einsum('bte,bted->btd', gate_topk, expert_out)
    x = x + _L0_attn_ref(_layernorm(x, axis=-1), L0_attn_W_DQ, L0_attn_W_UQ, L0_attn_W_DKV, L0_attn_W_UKV, L0_attn_W_QR, L0_attn_W_KR, L0_attn_W_O, L0_attn_q_norm_w, L0_attn_k_norm_w)
    x = x + _L0_xattn_ref(_layernorm(x, axis=-1), ctx_768, ctx_768, L0_xattn_Wq, L0_xattn_bq, L0_xattn_Wk, L0_xattn_bk, L0_xattn_Wv, L0_xattn_bv)
    x = x + _L0_ffn_ref(_layernorm(x, axis=-1), L0_ffn_W_enc, L0_ffn_b_enc, L0_ffn_W_s2c, L0_ffn_b_s2c, L0_ffn_Wr, L0_ffn_br, L0_ffn_W1, L0_ffn_b1, L0_ffn_W2, L0_ffn_b2, L0_ffn_W_c2s, L0_ffn_b_c2s, L0_ffn_W_dec, L0_ffn_b_dec, L0_ffn_ln_g, L0_ffn_ln_b)
    x = x + _L1_attn_ref(_layernorm(x, axis=-1), L1_attn_w_qkv, L1_attn_w_proj)
    x = x + _L1_xattn_ref(_layernorm(x, axis=-1), ctx_768, L1_xattn_Wq, L1_xattn_Wk, L1_xattn_Wv, L1_xattn_Wo, L1_xattn_bo)
    x = x + _L1_ffn_ref(_layernorm(x, axis=-1), L1_ffn_gate, L1_ffn_W1, L1_ffn_b1, L1_ffn_W2, L1_ffn_b2)
    return x

_drawn_inputs = setup_inputs


def setup_inputs(seed=0):
    import zlib

    import numpy as np

    out = dict(_drawn_inputs(seed))
    spreads = {'L0_attn_q_norm_w': (1.0, 0.6),
     'L0_attn_k_norm_w': (1.0, 0.6),
     'L0_ffn_b_enc': (0.0, 0.499),
     'L0_ffn_b_s2c': (0.0, 0.1),
     'L0_ffn_br': (0.0, 0.1),
     'L0_ffn_b1': (0.0, 0.496),
     'L0_ffn_b2': (0.0, 0.364),
     'L0_ffn_b_c2s': (0.0, 0.1),
     'L0_ffn_b_dec': (0.0, 0.1),
     'L0_ffn_ln_g': (1.0, 0.2),
     'L0_ffn_ln_b': (0.0, 0.1)}
    factors = {'L0_attn_W_DQ': 8.0,
     'L0_attn_W_UQ': 8.0,
     'L0_attn_W_DKV': 8.0,
     'L0_attn_W_UKV': 8.0,
     'L0_attn_W_QR': 8.0,
     'L0_attn_W_KR': 8.0,
     'L0_attn_W_O': 8.0,
     'L0_xattn_bk': 8.0,
     'L1_xattn_bo': 6.207,
     'L1_ffn_b1': 8.0,
     'L1_ffn_b2': 6.209}
    for name, (base, spread) in spreads.items():
        noise = np.random.default_rng([zlib.crc32(name.encode()), seed]).standard_normal(out[name].shape)
        drawn = base * np.exp(spread * noise) if base else spread * noise
        out[name] = jnp.asarray(drawn.astype(out[name].dtype))
    for name, factor in factors.items():
        out[name] = (out[name] * factor).astype(out[name].dtype)
    return out
```

```python
import numpy as np

B, S, D, DC = 16, 64, 128, 96
P = 128
TOK = B * S
TILES = TOK // P
HALVES = 2
TPH = TILES // HALVES
HT = TOK // HALVES
PAIR = P // S
LN_EPS = 1e-5
RMS_EPS = 1.1920929e-07
NH, HD = 16, 8
GRP = 4
NG = NH // GRP
XH, XD = 8, 64
XC = XH // 2
E0, K0, M0, F0H = 8, 2, 64, 128
E1, K1, F1H = 16, 3, 256
GW = 96
EXPERT = F1H + 2 * D + 2
MASKED = -1e30


def _pack_layout(parts):
    at, out = 0, {}
    for name, rows, cols in parts:
        out[name] = (rows, at, cols)
        at += cols
    return out, at


PACKS = {
    "l0": [("ident", P, P), ("blocks", P, P), ("heads", P, GRP), ("eps", P, 1), ("qnw", P, 1), ("knw", P, 1),
           ("dq", 64, P), ("uqT", 64, P), ("dkv", P, P), ("ukT", P, P), ("uvT", P, HD), ("kr", 64, P),
           ("qr", 64, P), ("oT", HD, P)],
    "ctx": [("ctxT", DC, TOK), ("wk0", DC, P), ("wv0", DC, P), ("bk0", P, 1), ("bv0", P, P), ("wq0", P, P),
            ("bq0", P, 1), ("xk", DC, XH * XD), ("xv", DC, XH * XD)],
    "f0": [("enc", P, 256), ("benc", P, 2), ("s2c", P, 2 * P), ("bs2c", P, 1), ("wr", M0, E0), ("br", P, E0),
           ("iota", P, E1), ("w1", P, (E0 // 2) * F0H), ("b1", P, E0), ("w2", P, E0 * M0), ("b2", GW, M0),
           ("c2s", P, 256), ("bc2s", P, 2), ("dec", P, 2 * P), ("bdec", P, P), ("lng", P, P), ("lnb", P, P)],
    "l1": [("qkv", P, 3 * P), ("proj", P, P), ("xq", P, XH * XD), ("xo", P, XC * P), ("xbo", P, P),
           ("gate", P, E1), ("fb2", GW, P)],
}
LAYOUT = {k: _pack_layout(v)[0] for k, v in PACKS.items()}
WIDTH = {k: _pack_layout(v)[1] for k, v in PACKS.items()}


def bank_plan():
    held, counts, plan = {}, {}, {}

    def lend(name, *banks):
        before = []
        for b in banks:
            if b in held and held[b] not in before:
                before.append(held[b])
        counts[banks[0]] = counts.get(banks[0], 0) + 1
        for b in banks:
            held[b] = (banks[0], counts[banks[0]])
        plan[name] = (banks[0], counts[banks[0]], before)

    for n, w in enumerate(("dq", "dk", "dm", "c")):
        lend(("fold", w), n)
    lend(("fold", "v"), 4)
    for h in range(HALVES):
        ln(lend, 0, h, 6)
        lend(("q0", h), 7)
        lend(("k0", h), 6)
        lend(("sq", h), 5)
        lend(("sk", h), 4)
        lend(("m0", h), 3)
        lend(("v0", h), 2)
    attention_banks(lend, 0)
    for h in range(HALVES):
        ln(lend, 1, h, 6)
        lend(("xq0", h), 7)
        lend(("xs0", h), h)
    for h in range(HALVES):
        lend(("xt0", h), 2)
        lend(("xo0", h, 0), 3 + 0)
        lend(("xo0", h, 1), 5)
    for h in range(HALVES):
        ln(lend, 2, h, 6)
        for c in range(2):
            lend(("enc", h, c), c)
        lend(("s2c", h), 2)
        lend(("rt0", h), 3)
    for h in range(HALVES):
        lend(("g0", h), 7)
    for h in range(HALVES):
        for p in range(E0 // 2):
            for q in range(2):
                lend(("z0", h, p, q), q)
                lend(("G0", h, p, q), 2 + q)
            if p == 0:
                lend(("y0", h), 4 + h)
    for h in range(HALVES):
        for c in range(2):
            lend(("c2s", h, c), c)
        lend(("dec", h), 2 + h)
    for h in range(HALVES):
        ln(lend, 3, h, 6)
        lend(("q1", h), 7)
        lend(("k1", h), 6)
        lend(("v1", h), 5)
    attention_banks(lend, 1)
    for h in range(HALVES):
        lend(("oT", h), 6)
        lend(("pr", h), 7)
    for h in range(HALVES):
        ln(lend, 4, h, 6)
        for c in range(XC):
            lend(("xq1", h, c), 7 - c % 2)
    for t in range(TILES + 2):
        if t < TILES:
            lend(("xs1", t), 0, 1)
        if 2 <= t:
            lend(("xo1", t - 2), 3, 4)
        if 1 <= t <= TILES:
            lend(("xt1", t - 1), 2)
    for h in range(HALVES):
        lend(("xp1", h), 5 + h)
    for h in range(HALVES):
        ln(lend, 5, h, 6)
        lend(("rt1", h), 7)
    for h in range(HALVES):
        lend(("g1", h), 5)
    lend(("experts",), 0, 1, 2, 3, 4, 5, 6, 7)
    for h in range(HALVES):
        lend(("fin", h), h)
    return plan


def ln(lend, k, h, bank):
    lend(("lnT", k, h), bank)


def fillers(layer):
    if layer == 0:
        work = [("ck0", h) for h in range(HALVES)] + [("cv0", h) for h in range(HALVES)] \
            + [("ck1", c, h) for c in range(XC) for h in range(HALVES)]
    else:
        work = [("cv1", n) for n in range(B // 2)]
    steps = [[] for _ in range(TILES)]
    for n, w in enumerate(work):
        steps[n * TILES // len(work)].append(w)
    return steps


def attention_banks(lend, layer):
    n = 0
    for t in range(TILES + 2):
        if t < TILES:
            lend(("s", layer, t), 0, 1, 2, 3)
            for w in fillers(layer)[t]:
                lend(w, 6 + n % 2)
                n += 1
        if 2 <= t:
            lend(("o", layer, t - 2), 5)
        if 1 <= t <= TILES:
            for g in range(2):
                lend(("t", layer, t - 1, g), 4)


def build(nc, dram, out):
    import concourse.bass as bass
    from concourse import mybir
    from contextlib import ExitStack

    f32, bf16, u32 = mybir.dt.float32, mybir.dt.bfloat16, mybir.dt.uint32
    ALU, ACT, AX = mybir.AluOpType, mybir.ActivationFunctionType, mybir.AxisListType
    plan = bank_plan()

    with ExitStack() as ctx:
        def sb(name, shape, dt=f32):
            return ctx.enter_context(nc.sbuf_tensor(name, shape, dt))

        def sem(name):
            return ctx.enter_context(nc.semaphore(name))

        PS = ctx.enter_context(nc.psum_tensor("banks", [P, 8, 512], f32))

        x = sb("x", [P, TILES, D])
        xn = sb("xn", [P, TILES, D])
        xnT = sb("xnT", [P, TOK])
        packs = {k: sb(f"pack_{k}", [P, WIDTH[k]]) for k in PACKS}
        masks = sb("masks", [P, 2, NH * S])

        def piece(pack, name):
            rows, at, cols = LAYOUT[pack][name]
            return packs[pack][0:rows, at:at + cols]

        stats = sb("stats", [P, TILES, 6])
        mv = sb("mv", [P, TILES, 2])
        veps = sb("veps", [P, TILES])
        half_neg = sb("half_neg", [P, TPH])
        rstd = sb("rstd", [P, TILES])

        fold = sb("fold", [P, 4, P])
        fold_c = sb("fold_c", [HD, P])
        rawq = sb("rawq", [P, TOK])
        rawk = sb("rawk", [P, TOK])
        hid = sb("hid", [P, 2, 2, HT])
        sqq, rms = hid[:, 0, :, :], hid[:, 1, :, :]
        qT = sb("qT", [P, TOK])
        kf = sb("kf", [P, TOK])
        kexp = sb("kexp", [P, GRP, TOK])
        vx = sb("vx", [P, B, NH // 2, 2 * (HD + 1)])
        sc = sb("sc", [P, 3, NH * S])
        pT = sb("pT", [P, 2, NH // 2, P])
        top = sb("top", [P, 3, NH])
        orec = sb("orec", [P, NH])
        oh = sb("oh", [P, TILES, D])

        k0T = sb("k0T", [P, TOK])
        v0 = sb("v0", [P, TILES // 2, PAIR, D])
        k1T = sb("k1T", [P, XC, TOK])
        v1 = sb("v1", [P, B, XC, XD])
        xs = sb("xs", [P, TILES, S])
        xtop = sb("xtop", [P, TILES])
        xrec = sb("xrec", [P, TILES])
        q1T = kexp

        halfb = sb("halfb", [P, 4])
        spk = sb("spk", [P, 2, HT])
        contT = rawk
        rl = sb("rl", [P, TILES, E1])
        r8 = sb("r8", [P, TILES, 8])
        i8 = sb("i8", [P, TILES, 8], u32)
        i8f = sb("i8f", [P, TILES, 8])
        eq = sb("eq", [P, TILES, K1, E1])
        pick = sb("pick", [P, TILES, E1])
        rsum = sb("rsum", [P, TILES])
        ghi = sb("ghi", [P, TILES, GW], bf16)
        g3T = sb("g3T", [P, TOK], bf16)
        sel = sb("sel", [P, E1, P], bf16)
        identb = sb("identb", [P, P], bf16)
        b2s = sb("b2s", [GW, 2, 3, P], bf16)
        b2r = sb("b2r", [GW, P])
        relu = sb("relu", [P, 2, 2, HT])
        ws = sb("ws", [P, 2, EXPERT])
        accT = kf

        spm = [relu[:, h, :, :] for h in range(HALVES)]

        bank_full = [sem(f"bank_full{b}") for b in range(8)]
        bank_read = [sem(f"bank_read{b}") for b in range(8)]
        x_loaded, masks_loaded = sem("x_loaded"), sem("masks_loaded")
        pack_loaded = {k: sem(f"pack_{k}_loaded") for k in PACKS}
        consts_set = sem("consts_set")
        stats_ready, rstd_ready, xn_ready = sem("stats_ready"), sem("rstd_ready"), sem("xn_ready")
        q_ready, k_ready, k_normed = sem("q_ready"), sem("k_ready"), sem("k_normed")
        top_ready, shifted, probs_ready = sem("top_ready"), sem("shifted"), sem("probs_ready")
        xprobs, xnorm = sem("xprobs"), sem("xnorm")
        spikes_ready, hid0_used = sem("spikes_ready"), sem("hid0_used")
        logits_shifted, exp_ready, gates_ready = sem("logits_shifted"), sem("exp_ready"), sem("gates_ready")
        dve_step, act_step, pool_step = sem("dve_step"), sem("act_step"), sem("pool_step")
        w_loaded = [sem(f"w_loaded{n}") for n in range(2)]
        z_full, relu_ready, G_full, hid_ready, acc_done = (sem(n) for n in ("z_full", "relu_ready", "G_full", "hid_ready", "acc_done"))
        out_ready, stored = sem("out_ready"), sem("stored")

        def filled(ins, name):
            ins.then_inc(bank_full[plan[name][0]], 1)

        def await_bank(eng, name):
            key, count, _ = plan[name]
            eng.wait_ge(bank_full[key], count)

        def read_out(ins, name):
            ins.then_inc(bank_read[plan[name][0]], 1)

        def await_read(eng, name):
            key, count, _ = plan[name]
            eng.wait_ge(bank_read[key], count)

        def chain(eng, signal):
            n = [0]

            def link(ins):
                n[0] += 1
                ins.then_inc(signal, 1)
                eng.wait_ge(signal, n[0])
            return link

        def tok(t, j=None):
            return slice(P * t, P * t + P) if j is None else slice(P * t + S * j, P * t + S * j + S)

        def rows(j):
            return slice(S * j, S * j + S)

        def half(h):
            return slice(HT * h, HT * h + HT)

        def tiles(h):
            return range(TPH * h, TPH * h + TPH)

        def th(h):
            return slice(TPH * h, TPH * h + TPH)

        def bank(b, a, n):
            return PS[:, b, :].rearrange("p (a n) -> p a n", a=a)[:, :, 0:n]

        def bc(ap, shape):
            return ap.broadcast_to(shape)

        block = ctx.enter_context(nc.Block())

        @block.sync
        def _(sp):
            sp.dma_start(x[:, 0:TPH, :], dram["x"].rearrange("(t p) d -> p t d", p=P)[:, 0:TPH, :]).then_inc(x_loaded, 16)
            sp.dma_start(packs["l0"][:], dram["l0"]).then_inc(pack_loaded["l0"], 16)
            sp.dma_start(x[:, TPH:, :], dram["x"].rearrange("(t p) d -> p t d", p=P)[:, TPH:, :]).then_inc(x_loaded, 16)
            sp.dma_start(masks[:], dram["masks"]).then_inc(masks_loaded, 16)
            for k in ("ctx", "f0", "l1"):
                sp.dma_start(packs[k][:], dram[k]).then_inc(pack_loaded[k], 16)

            def load_expert(e, slot):
                sp.dma_start(ws[:, slot, :], dram["experts"][e, :, :]).then_inc(w_loaded[slot], 16)

            for e in range(2):
                load_expert(e, e)
            with sp.Fori(1, E1 // 2) as i:
                for n in range(2):
                    sp.wait_ge(acc_done, i * 4 - 2 + 2 * n)
                    load_expert(i * 2 + n, n)
            o = out.rearrange("(t p) d -> p t d", p=P)
            for h in range(HALVES):
                sp.wait_ge(out_ready, h + 1)
                sp.dma_start(o[:, th(h), :], x[:, th(h), :]).then_inc(stored, 16)
            sp.wait_ge(stored, 16 * HALVES)

        @block.gpsimd
        def _(pool):
            link = chain(pool, pool_step)
            link(pool.memset(half_neg[:], -0.5))
            link(pool.memset(vx[:], 0.0))
            for q in range(2):
                link(pool.memset(vx[rows(q), :, :, 9 * q + 8:9 * q + 9], 1.0))
            link(pool.memset(ghi[:], 0.0))
            link(pool.memset(g3T[:], 0.0))
            link(pool.memset(sel[:], 0.0))
            for part in range(3):
                link(pool.affine_select(out=sel[:], in_=sel[:], compare_op=ALU.not_equal, fill=1.0, base=-32 * part,
                                        pattern=[[-1, E1], [0, P]], channel_multiplier=1))
            pool.memset(xs[:], 0.0).then_inc(consts_set, 1)

            def rsqrt(k, h):
                pool.wait_ge(stats_ready, HALVES * k + h + 1)
                link(pool.tensor_scalar(veps[:, th(h)], mv[:, th(h), 1], LN_EPS, None, ALU.add))
                pool.tensor_tensor(rstd[:, th(h)], veps[:, th(h)], half_neg[:], ALU.pow).then_inc(rstd_ready, 1)

            def shift(layer, t):
                n = TILES * layer + t
                pool.wait_ge(top_ready, n + 1)
                s = sc[:, t % 3, :].rearrange("p (h k) -> p h k", h=NH)
                pool.tensor_tensor(s, s, bc(top[:, t % 3, :].unsqueeze(2), [P, NH, S]), ALU.subtract).then_inc(shifted, 1)

            order = ln_order()
            for item in order:
                if item[0] == "ln":
                    rsqrt(item[1], item[2])
                else:
                    for t in range(TILES):
                        shift(item[1], t)

        @block.tensor
        def _(pe):
            def claim(name):
                for key, count in plan[name][2]:
                    pe.wait_ge(bank_read[key], count)
                return plan[name][0]

            def mm(o, w, m, start=True, stop=True, **kw):
                return pe.matmul(o, w, m, start=start, stop=stop, **kw)

            ident = piece("l0", "ident")

            def turn_xn(k, h, n):
                b = claim(("lnT", k, h))
                pe.wait_ge(xn_ready, n)
                for i, t in enumerate(tiles(h)):
                    last = pe.transpose(PS[:, b, P * i:P * i + P], xn[:, t, :], ident)
                filled(last, ("lnT", k, h))

            def product(name, w, m, wait=None):
                b = claim(name)
                rows_out = w.shape[1]
                filled(mm(PS[0:rows_out, b, :], w, m), name)

            def fold_weights():
                pe.wait_ge(pack_loaded["l0"], 16)
                for name, a, c in (("dq", "dq", "uqT"), ("dk", "dkv", "ukT"), ("dm", "kr", "qr"), ("c", "uvT", "dkv")):
                    b = claim(("fold", name))
                    w, m = piece("l0", a), piece("l0", c)
                    filled(mm(PS[0:w.shape[1], b, 0:P], w, m), ("fold", name))
                b = claim(("fold", "v"))
                await_read(pe, ("fold", "c"))
                filled(mm(PS[:, b, 0:P], fold_c[:], piece("l0", "oT")), ("fold", "v"))

            def values(name, h, w):
                b = claim(name)
                wv = w.rearrange("p (c q d) -> p q c d", q=2, d=HD)
                for n in range(B // HALVES):
                    for q in range(2):
                        last = mm(PS[rows(q), b, 64 * n:64 * n + 64], xnT[:, HT * h + S * n:HT * h + S * n + S], wv[:, q, :, :])
                filled(last, name)

            def qkv0(h):
                await_read(pe, ("lnT", 0, h))
                if h == 0:
                    await_read(pe, ("fold", "v"))
                product(("q0", h), fold[:, 0, :], xnT[:, half(h)])
                product(("k0", h), fold[:, 1, :], xnT[:, half(h)])
                await_read(pe, ("q0", h))
                product(("sq", h), piece("l0", "blocks"), sqq[:, 0, :])
                await_read(pe, ("k0", h))
                product(("sk", h), piece("l0", "blocks"), sqq[:, 1, :])
                product(("m0", h), fold[:, 2, :], xnT[:, half(h)])
                values(("v0", h), h, fold[:, 3, :])

            def qkv1(h):
                await_read(pe, ("lnT", 3, h))
                pe.wait_ge(pack_loaded["l1"], 16)
                w = piece("l1", "qkv")
                product(("q1", h), w[:, 0:P], xnT[:, half(h)])
                product(("k1", h), w[:, P:2 * P], xnT[:, half(h)])
                values(("v1", h), h, w[:, 2 * P:3 * P])

            def context(name):
                pe.wait_ge(pack_loaded["ctx"], 16)
                ctxT = piece("ctx", "ctxT")
                if name[0] == "ck0":
                    product(name, piece("ctx", "wk0"), ctxT[:, half(name[1])])
                elif name[0] == "ck1":
                    product(name, piece("ctx", "xk")[:, P * name[1]:P * name[1] + P], ctxT[:, half(name[2])])
                elif name[0] == "cv0":
                    b = claim(name)
                    for a in range(2):
                        for j in range(PAIR):
                            for u in range(2):
                                last = mm(PS[rows(u), b, P * (2 * a + j):P * (2 * a + j) + P],
                                          ctxT[:, tok(TPH * name[1] + 2 * a + u, j)], piece("ctx", "wv0"))
                    filled(last, name)
                else:
                    b = claim(name)
                    w = piece("ctx", "xv").rearrange("p (c q d) -> p q c d", q=2, d=XD)
                    for n in range(2):
                        for q in range(2):
                            s0 = S * (2 * name[1] + n)
                            last = mm(PS[rows(q), b, 256 * n:256 * n + 256], ctxT[:, s0:s0 + S], w[:, q, :, :])
                    filled(last, name)

            def attention(layer):
                for t in range(TILES + 2):
                    if t < TILES:
                        claim(("s", layer, t))
                        if layer == 0:
                            pe.wait_ge(q_ready, t // TPH + 1)
                        else:
                            await_read(pe, ("q1", t // TPH))
                        pe.wait_ge(k_ready, HALVES * layer + t // TPH + 1)
                        for i in range(NG):
                            g = slice(32 * i, 32 * i + 32)
                            for j in range(PAIR):
                                last = mm(PS[rows(j), i, 0:GRP * S], qT[g, tok(t, j)], kexp[g, :, tok(t, j)])
                        filled(last, ("s", layer, t))
                        for w in fillers(layer)[t]:
                            context(w)
                    if 2 <= t:
                        u = t - 2
                        b = claim(("o", layer, u))
                        await_read(pe, ("v%d" % layer, u // TPH))
                        await_read(pe, ("t", layer, u, 1))
                        for c in range(NH // 2):
                            for j in range(PAIR):
                                last = mm(PS[rows(j), b, 18 * c:18 * c + 18], pT[:, u % 2, c, rows(j)], vx[:, 2 * u + j, c, :])
                        filled(last, ("o", layer, u))
                    if 1 <= t <= TILES:
                        u = t - 1
                        pe.wait_ge(probs_ready, TILES * layer + u + 1)
                        for g in range(2):
                            b = claim(("t", layer, u, g))
                            for c in range(4):
                                k0 = P * (4 * g + c)
                                last = pe.transpose(PS[:, b, P * c:P * c + P], sc[:, u % 3, k0:k0 + P], ident)
                            filled(last, ("t", layer, u, g))

            def cross0():
                for h in range(HALVES):
                    turn_xn(1, h, HALVES + h + 1)
                    await_read(pe, ("lnT", 1, h))
                    product(("xq0", h), piece("ctx", "wq0"), xnT[:, half(h)])
                    b = claim(("xs0", h))
                    await_read(pe, ("xq0", h))
                    for i, t in enumerate(tiles(h)):
                        for j in range(PAIR):
                            last = mm(PS[rows(j), b, S * i:S * i + S], rawq[:, tok(t, j)], k0T[:, tok(t, j)])
                    filled(last, ("xs0", h))
                for h in range(HALVES):
                    b = claim(("xt0", h))
                    pe.wait_ge(xprobs, h + 1)
                    for a in range(2):
                        t = TPH * h + 2 * a
                        last = pe.transpose(PS[:, b, P * a:P * a + P], xs[:, t:t + 2, :], ident)
                    filled(last, ("xt0", h))
                    await_read(pe, ("xt0", h))
                    for u in range(2):
                        b = claim(("xo0", h, u))
                        for a in range(2):
                            for j in range(PAIR):
                                last = mm(PS[rows(j), b, P * a:P * a + P], pT[rows(u), h, a, rows(j)],
                                          v0[rows(u), 2 * h + a, j, :])
                        filled(last, ("xo0", h, u))

            def gates_turned(layer, h):
                b = claim(("g%d" % layer, h))
                pe.wait_ge(gates_ready, HALVES * layer + h + 1)
                view = PS[:, b, :].bitcast(bf16)
                for i, t in enumerate(tiles(h)):
                    last = pe.transpose(view[0:GW, P * i:P * i + P], ghi[:, t, :], identb[:])
                filled(last, ("g%d" % layer, h))

            def moe0():
                pe.wait_ge(pack_loaded["f0"], 16)
                enc, s2c, w2 = piece("f0", "enc"), piece("f0", "s2c"), piece("f0", "w2")
                for h in range(HALVES):
                    turn_xn(2, h, 2 * HALVES + h + 1)
                    await_read(pe, ("lnT", 2, h))
                    for c in range(2):
                        product(("enc", h, c), enc[:, P * c:P * c + P], xnT[:, half(h)])
                    b = claim(("s2c", h))
                    for c in range(2):
                        pe.wait_ge(spikes_ready, 2 * h + c + 1)
                        last = mm(PS[:, b, :], s2c[:, P * c:P * c + P], spk[:, c, :], start=(c == 0), stop=(c == 1))
                    filled(last, ("s2c", h))
                    b = claim(("rt0", h))
                    await_read(pe, ("s2c", h))
                    for i, t in enumerate(tiles(h)):
                        last = mm(PS[:, b, E0 * i:E0 * i + E0], contT[0:M0, tok(t)], piece("f0", "wr"))
                    filled(last, ("rt0", h))
                pe.wait_ge(consts_set, 2)
                for h in range(HALVES):
                    gates_turned(0, h)
                w1 = piece("f0", "w1")
                for h in range(HALVES):
                    await_read(pe, ("g0", h))
                    for p in range(E0 // 2 + 1):
                        if p < E0 // 2:
                            for q in range(2):
                                b = claim(("z0", h, p, q))
                                filled(mm(PS[:, b, :], w1[rows(q), F0H * p:F0H * p + F0H], contT[rows(q), half(h)]),
                                       ("z0", h, p, q))
                                b = claim(("G0", h, p, q))
                                filled(mm(PS[:, b, :], sel[:, 2 * p + q, :], g3T[:, half(h)]), ("G0", h, p, q))
                        if p == 0:
                            yb = claim(("y0", h))
                            continue
                        for q in range(2):
                            e = 2 * (p - 1) + q
                            await_read(pe, ("G0", h, p - 1, q))
                            last = mm(PS[rows(q), yb, :], w2[:, M0 * e:M0 * e + M0], hid[:, q, 1, :],
                                      start=(p == 1), stop=(q == 1 and p == E0 // 2), skip_group_check=True)
                            last.then_inc(hid0_used, 1)
                    for n in range(3):
                        last = mm(PS[rows(0), yb, :], b2s[:, 0, n, 0:M0], g3T[0:GW, half(h)],
                                  start=False, stop=True, skip_group_check=True)
                    filled(last, ("y0", h))
                c2s, dec = piece("f0", "c2s"), piece("f0", "dec")
                for h in range(HALVES):
                    await_read(pe, ("y0", h))
                    for c in range(2):
                        product(("c2s", h, c), c2s[:, P * c:P * c + P], accT[:, half(h)])
                    b = claim(("dec", h))
                    pe.wait_ge(spikes_ready, 2 * HALVES + 2 * h + 2)
                    for i in range(TPH):
                        for c in range(2):
                            last = mm(PS[:, b, P * i:P * i + P], spm[h][:, c, P * i:P * i + P], dec[:, P * c:P * c + P],
                                      start=(c == 0), stop=(c == 1))
                    filled(last, ("dec", h))

            def project1():
                for h in range(HALVES):
                    b = claim(("oT", h))
                    await_read(pe, ("o", 1, TPH * h + TPH - 1))
                    for i, t in enumerate(tiles(h)):
                        last = pe.transpose(PS[:, b, P * i:P * i + P], oh[:, t, :], ident)
                    filled(last, ("oT", h))
                    b = claim(("pr", h))
                    await_read(pe, ("oT", h))
                    for i, t in enumerate(tiles(h)):
                        last = mm(PS[:, b, P * i:P * i + P], rawq[:, tok(t)], piece("l1", "proj"))
                    filled(last, ("pr", h))

            def cross1():
                for h in range(HALVES):
                    turn_xn(4, h, 5 * HALVES + h + 1)
                    await_read(pe, ("lnT", 4, h))
                    for c in range(XC):
                        product(("xq1", h, c), piece("l1", "xq")[:, P * c:P * c + P], xnT[:, half(h)])
                for t in range(TILES + 2):
                    if t < TILES:
                        claim(("xs1", t))
                        for c in range(XC):
                            await_read(pe, ("xq1", t // TPH, c))
                        for c in range(XC):
                            for q in range(2):
                                for j in range(PAIR):
                                    last = mm(PS[rows(j), q, S * c:S * c + S], q1T[rows(q), c, tok(t, j)],
                                              k1T[rows(q), c, tok(t, j)])
                        filled(last, ("xs1", t))
                    if 2 <= t:
                        u = t - 2
                        claim(("xo1", u))
                        await_read(pe, ("xt1", u))
                        for c in range(XC):
                            for q in range(2):
                                for j in range(PAIR):
                                    last = mm(PS[rows(q), 3 + q, P * c + S * j:P * c + S * j + S],
                                              v1[rows(q), 2 * u + j, c, :], pT[rows(q), u % 2, c, rows(j)])
                        filled(last, ("xo1", u))
                    if 1 <= t <= TILES:
                        u = t - 1
                        pe.wait_ge(xnorm, u + 1)
                        b = claim(("xt1", u))
                        for c in range(XC):
                            last = pe.transpose(PS[:, b, P * c:P * c + P], sc[:, u % 3, P * c:P * c + P], ident)
                        filled(last, ("xt1", u))
                xo = piece("l1", "xo")
                for h in range(HALVES):
                    b = claim(("xp1", h))
                    for i, t in enumerate(tiles(h)):
                        await_read(pe, ("xo1", t))
                        for c in range(XC):
                            last = mm(PS[:, b, P * i:P * i + P], q1T[:, c, tok(t)], xo[:, P * c:P * c + P],
                                      start=(c == 0), stop=(c == XC - 1))
                    filled(last, ("xp1", h))

            def moe1():
                for h in range(HALVES):
                    turn_xn(5, h, 6 * HALVES + h + 1)
                    await_read(pe, ("lnT", 5, h))
                    b = claim(("rt1", h))
                    for i, t in enumerate(tiles(h)):
                        last = mm(PS[:, b, E1 * i:E1 * i + E1], xnT[:, tok(t)], piece("l1", "gate"))
                    filled(last, ("rt1", h))
                for h in range(HALVES):
                    gates_turned(1, h)
                claim(("experts",))
                for h in range(HALVES):
                    await_read(pe, ("g1", h))

                def pair_of_experts(i, first):
                    for n in range(2):
                        if first:
                            pe.wait_ge(w_loaded[n], 16)
                        else:
                            pe.wait_ge(w_loaded[n], i * 16 + 16)
                        for h in range(HALVES):
                            u = 2 * n + h
                            ub = u % 2
                            fresh = first and u < 2
                            if not fresh:
                                pe.wait_ge(hid_ready, 2 * (u - 2) + 2 if first else i * 8 + (2 * (u - 2) + 2))
                            mm(PS[:, 4 + ub, :], sel[:, (n if first else i * 2 + n), :], g3T[:, half(h)]).then_inc(G_full, 1)
                            for c in range(2):
                                if not fresh:
                                    pe.wait_ge(relu_ready, 2 * (u - 2) + c + 1 if first else i * 8 + (2 * (u - 2) + c + 1))
                                mm(PS[:, 2 * ub + c, :], ws[:, n, P * c:P * c + P], xnT[:, half(h)]).then_inc(z_full, 1)
                            if not (first and u == 0):
                                down(i, u - 1, first)

                def down(i, u, first):
                    n, h, ub = (u % 4) // 2, u % 2, u % 2
                    for c in range(2):
                        pe.wait_ge(hid_ready, 2 * u + c + 1 if first else i * 8 + (2 * u + c + 1))
                        last = mm(PS[:, 6 + h, :], ws[:, n, F1H + P * c:F1H + P * c + P], hid[:, ub, c, :],
                                  start=(first and u < 2 and c == 0), stop=False, skip_group_check=True)
                    last.then_inc(acc_done, 1)

                pair_of_experts(0, True)
                with pe.Fori(1, E1 // 2) as i:
                    pair_of_experts(i, False)
                for c in range(2):
                    pe.wait_ge(hid_ready, 4 * E1 - 2 + c + 1)
                    mm(PS[:, 7, :], ws[:, 1, F1H + P * c:F1H + P * c + P], hid[:, 1, c, :], start=False, stop=False, skip_group_check=True)
                for h in range(HALVES):
                    for n in range(3):
                        last = mm(PS[:, 6 + h, :], b2s[:, 1, n, :], g3T[0:GW, half(h)],
                                  start=False, stop=True, skip_group_check=True)
                filled(last, ("experts",))
                for h in range(HALVES):
                    b = claim(("fin", h))
                    for i, t in enumerate(tiles(h)):
                        last = pe.transpose(PS[:, b, P * i:P * i + P], accT[:, tok(t)], ident)
                    filled(last, ("fin", h))

            pe.wait_ge(consts_set, 1)
            fold_weights()
            for h in range(HALVES):
                turn_xn(0, h, h + 1)
                qkv0(h)
            attention(0)
            cross0()
            moe0()
            for h in range(HALVES):
                turn_xn(3, h, 4 * HALVES + h + 1)
                qkv1(h)
            attention(1)
            project1()
            cross1()
            moe1()

        @block.scalar
        def _(act):
            link = chain(act, act_step)

            def evac(name, dst, b, src=None, func=ACT.Copy, **kw):
                await_bank(act, name)
                read_out(act.activation(dst, PS[:, b, :] if src is None else src, func, **kw), name)

            def turned(k, h):
                name = ("lnT", k, h)
                evac(name, xnT[:, half(h)], plan[name][0])

            def values(name, h):
                await_bank(act, name)
                src = PS[:, plan[name][0], :].rearrange("p (n d) -> p n d", d=HD)
                dst = vx[:, 8 * h:8 * h + 8, :, :].rearrange("p b c d -> p (b c) d")
                act.activation(dst[rows(0), :, 0:HD], src[rows(0), :, :], ACT.Copy)
                read_out(act.activation(dst[rows(1), :, HD + 1:2 * HD + 1], src[rows(1), :, :], ACT.Copy), name)

            def context(name):
                b = plan[name][0]
                if name[0] == "ck0":
                    evac(name, k0T[:, half(name[1])], b, func=ACT.Identity, bias=piece("ctx", "bk0"))
                elif name[0] == "ck1":
                    evac(name, k1T[:, name[1], half(name[2])], b)
                elif name[0] == "cv0":
                    evac(name, v0[:, 2 * name[1]:2 * name[1] + 2, :, :], b)
                else:
                    evac(name, v1[:, 2 * name[1]:2 * name[1] + 2, :, :], b)

            def attention(layer):
                for t in range(TILES + 1):
                    if t < TILES:
                        for w in fillers(layer)[t]:
                            context(w)
                    if 1 <= t:
                        u = t - 1
                        for g in range(2):
                            if g == 0 and u >= 2:
                                await_bank(act, ("o", layer, u - 2))
                            evac(("t", layer, u, g), pT[:, u % 2, 4 * g:4 * g + 4, :], 4)
                    if t < TILES:
                        act.wait_ge(shifted, TILES * layer + t + 1)
                        act.activation(sc[:, t % 3, :], sc[:, t % 3, :], ACT.Exp).then_inc(probs_ready, 1)

            def router_exp(layer, h):
                act.wait_ge(logits_shifted, HALVES * layer + h + 1)
                n = (E0, E1)[layer]
                act.activation(rl[:, th(h), 0:n], rl[:, th(h), 0:n], ACT.Exp).then_inc(exp_ready, 1)

            act.wait_ge(pack_loaded["l0"], 16)
            act.wait_ge(consts_set, 1)
            act.activation(identb[:], piece("l0", "ident"), ACT.Copy).then_inc(consts_set, 1)
            for h in range(HALVES):
                turned(0, h)
                if h == 1:
                    await_bank(act, ("sk", 0))
                for n, (name, raw) in enumerate((("q0", rawq), ("k0", rawk))):
                    await_bank(act, (name, h))
                    b = plan[(name, h)][0]
                    act.activation(sqq[:, n, :], PS[:, b, :], ACT.Square)
                    read_out(act.activation(raw[:, half(h)], PS[:, b, :], ACT.Copy), (name, h))
                for n, name in enumerate(("sq", "sk")):
                    if h == 1:
                        act.wait_ge((q_ready, k_normed)[n], 1)
                    evac((name, h), rms[:, n, :], plan[(name, h)][0], func=ACT.Sqrt, scale=1.0 / HD, bias=piece("l0", "eps"))
                values(("v0", h), h)
            act.wait_ge(pack_loaded["ctx"], 16)
            attention(0)
            for h in range(HALVES):
                turned(1, h)
                evac(("xq0", h), rawq[:, half(h)], 7, func=ACT.Identity, bias=piece("ctx", "bq0"))
                await_read(act, ("xs0", h))
                act.activation(xs[:, th(h), :], xs[:, th(h), :], ACT.Exp).then_inc(xprobs, 1)
            for h in range(HALVES):
                evac(("xt0", h), pT[:, h, 0:2, :], 2, src=PS[:, 2, 0:2 * P])
            act.wait_ge(pack_loaded["f0"], 16)
            act.activation(halfb[:, 0:2], piece("f0", "benc"), ACT.Copy, scale=0.5)
            link(act.activation(halfb[:, 2:4], piece("f0", "bc2s"), ACT.Copy, scale=0.5))
            for h in range(HALVES):
                turned(2, h)
                for c in range(2):
                    if h == 1:
                        await_bank(act, ("s2c", 0))
                    await_bank(act, ("enc", h, c))
                    read_out(act.activation(spk[:, c, :], PS[:, c, :], ACT.Tanh, scale=0.5, bias=halfb[:, c:c + 1]), ("enc", h, c))
                evac(("s2c", h), contT[:, half(h)], 2, func=ACT.Identity, bias=piece("f0", "bs2c"))
                router_exp(0, h)
            for h in range(HALVES):
                evac(("g0", h), g3T[0:GW, half(h)], 7, src=PS[:, 7, :].bitcast(bf16)[0:GW, 0:HT])
            for h in range(HALVES):
                for e in range(E0):
                    n = E0 * h + e
                    if n >= 2:
                        await_read(act, ("G0", (n - 2) // E0, (n - 2) % E0 // 2, e % 2))
                    name = ("z0", h, e // 2, e % 2)
                    evac(name, relu[:, e % 2, 0, :], plan[name][0], func=ACT.Relu, bias=piece("f0", "b1")[:, e:e + 1])
                evac(("y0", h), accT[:, half(h)], plan[("y0", h)][0])
            for h in range(HALVES):
                for c in range(2):
                    if h == 0 and c == 0:
                        await_read(act, ("G0", 1, E0 // 2 - 1, 1))
                    await_bank(act, ("c2s", h, c))
                    read_out(act.activation(spm[h][:, c, :], PS[:, c, :], ACT.Tanh, scale=0.5, bias=halfb[:, 2 + c:3 + c]), ("c2s", h, c))
            act.wait_ge(pack_loaded["l1"], 16)
            for h in range(HALVES):
                turned(3, h)
                evac(("q1", h), qT[:, half(h)], 7)
                evac(("k1", h), kf[:, half(h)], 6)
                values(("v1", h), h)
            attention(1)
            for h in range(HALVES):
                evac(("oT", h), rawq[:, half(h)], 6)
            for h in range(HALVES):
                turned(4, h)
                for c in range(XC):
                    evac(("xq1", h, c), q1T[:, c, half(h)], plan[("xq1", h, c)][0])
            for t in range(TILES + 2):
                if 2 <= t:
                    u = t - 2
                    await_bank(act, ("xo1", u))
                    for q in range(2):
                        last = act.activation(q1T[rows(q), :, tok(u)], PS[rows(q), 3 + q, :].rearrange("p (c k) -> p c k", c=XC), ACT.Copy)
                    read_out(last, ("xo1", u))
                if 1 <= t <= TILES:
                    u = t - 1
                    evac(("xt1", u), pT[:, u % 2, 0:XC, :], 2)
                if t < TILES:
                    await_read(act, ("xs1", t))
                    act.activation(sc[:, t % 3, 0:XH * S], sc[:, t % 3, 0:XH * S], ACT.Exp, scale=float(XD) ** -0.5).then_inc(xprobs, 1)
            for h in range(HALVES):
                turned(5, h)
                router_exp(1, h)
            for h in range(HALVES):
                evac(("g1", h), g3T[0:GW, half(h)], 5, src=PS[:, 5, :].bitcast(bf16)[0:GW, 0:HT])

            def pair_of_experts(i, first):
                for u in range(4):
                    for c in range(2):
                        fresh = first and u < 2
                        act.wait_ge(z_full, 2 * u + c + 1 if first else i * 8 + (2 * u + c + 1))
                        if not fresh:
                            act.wait_ge(hid_ready, 2 * (u - 2) + c + 1 if first else i * 8 + (2 * (u - 2) + c + 1))
                        bias = ws[:, u // 2, 2 * F1H + c:2 * F1H + c + 1]
                        act.activation(relu[:, u % 2, c, :], PS[:, 2 * (u % 2) + c, :], ACT.Relu, bias=bias).then_inc(relu_ready, 1)

            pair_of_experts(0, True)
            with act.Fori(1, E1 // 2) as i:
                pair_of_experts(i, False)
            await_bank(act, ("experts",))
            act.activation(accT[:, half(0)], PS[:, 6, :], ACT.Copy)
            read_out(act.activation(accT[:, half(1)], PS[:, 7, :], ACT.Copy), ("experts",))

        @block.vector
        def _(dve):
            link = chain(dve, dve_step)

            def layernorm(k, h, src=x, dst=xn, last_signal=True):
                n = HALVES * k + h
                for t in tiles(h):
                    last = dve.bn_stats(stats[:, t, :], src[:, t, :])
                link(last)
                for t in tiles(h):
                    last = dve.bn_aggr(mv[:, t, :], stats[:, t, :])
                last.then_inc(stats_ready, 1)
                dve.wait_ge(stats_ready, n + 1)
                dve.wait_ge(rstd_ready, n + 1)
                for t in tiles(h):
                    last = dve.tensor_scalar(dst[:, t, :], src[:, t, :], mv[:, t, 0:1], rstd[:, t:t + 1], ALU.subtract, ALU.mult)
                last.then_inc(xn_ready, 1)

            def expand_keys(h, n):
                for j in range(GRP):
                    last = dve.tensor_scalar(kexp[:, j, half(h)], kf[:, half(h)], piece("l0", "heads")[:, j:j + 1], None, ALU.mult)
                last.then_inc(k_ready, 1)

            def attention(layer):
                mask = masks[:, layer, :]
                for t in range(TILES + 2):
                    if t < TILES:
                        name = ("s", layer, t)
                        await_bank(dve, name)
                        s = sc[:, t % 3, :]
                        read_out(dve.scalar_tensor_tensor(s.rearrange("p (i n) -> p i n", i=NG), PS[:, 0:NG, 0:GRP * S],
                                                          float(HD) ** -0.5, mask.rearrange("p (i n) -> p i n", i=NG),
                                                          ALU.mult, ALU.add), name)
                        await_read(dve, name)
                        dve.reduce_max(top[:, t % 3, :], s.rearrange("p (h k) -> p h k", h=NH), AX.X).then_inc(top_ready, 1)
                    if 2 <= t:
                        u = t - 2
                        name = ("o", layer, u)
                        await_bank(dve, name)
                        o = PS[:, 5, 0:NH * (HD + 1)].rearrange("p (h d) -> p h d", h=NH)
                        link(dve.reciprocal(orec[:], o[:, :, HD]))
                        dst = oh[:, u, :].rearrange("p (h d) -> p h d", h=NH)
                        read_out(dve.tensor_tensor(dst, o[:, :, 0:HD], bc(orec[:].unsqueeze(2), [P, NH, HD]), ALU.mult), name)
                        if layer == 0:
                            await_read(dve, name)
                            last = dve.tensor_tensor(x[:, u, :], x[:, u, :], oh[:, u, :], ALU.add)
                            if u % TPH == TPH - 1:
                                link(last)

            def route(layer, h):
                n, k = ((E0, K0), (E1, K1))[layer]
                name = ("rt%d" % layer, h)
                b = plan[name][0]
                await_bank(dve, name)
                r, s4 = rl[:, th(h), 0:n], rsum[:, th(h)]
                src = PS[:, b, 0:TPH * n].rearrange("p (t e) -> p t e", e=n)
                if layer == 0:
                    read_out(dve.tensor_tensor(r, src, bc(piece("f0", "br").unsqueeze(1), [P, TPH, n]), ALU.add), name)
                else:
                    read_out(dve.tensor_copy(r, src), name)
                await_read(dve, name)
                link(dve.reduce_max(s4, r, AX.X))
                dve.tensor_tensor(r, r, bc(s4.unsqueeze(2), [P, TPH, n]), ALU.subtract).then_inc(logits_shifted, 1)
                dve.wait_ge(exp_ready, HALVES * layer + h + 1)
                link(dve.reduce_sum(s4, r, AX.X))
                link(dve.reciprocal(s4, s4))
                link(dve.tensor_tensor(r, r, bc(s4.unsqueeze(2), [P, TPH, n]), ALU.mult))
                for t in tiles(h):
                    last = dve.max(r8[:, t, :], rl[:, t, 0:n])
                link(last)
                for t in tiles(h):
                    last = dve.max_index(i8[:, t, :], r8[:, t, :], rl[:, t, 0:n])
                link(last)
                link(dve.tensor_copy(i8f[:, th(h), :], i8[:, th(h), :]))
                iota = piece("f0", "iota")
                for t in tiles(h):
                    last = dve.tensor_tensor(eq[:, t, 0:k, 0:n], bc(iota[:, 0:n].unsqueeze(1), [P, k, n]),
                                             bc(i8f[:, t, 0:k].unsqueeze(2), [P, k, n]), ALU.is_equal)
                link(last)
                link(dve.reduce_sum(pick[:, th(h), 0:n], eq[:, th(h), 0:k, 0:n].rearrange("p t k e -> p t e k"), AX.X))
                link(dve.tensor_tensor(r, r, pick[:, th(h), 0:n], ALU.mult))
                link(dve.reduce_sum(s4, r, AX.X))
                if layer == 1:
                    link(dve.tensor_scalar(s4, s4, 1e-12, None, ALU.max))
                link(dve.reciprocal(s4, s4))
                link(dve.tensor_tensor(r, r, bc(s4.unsqueeze(2), [P, TPH, n]), ALU.mult))
                link(dve.tensor_copy(ghi[:, th(h), 0:n], r))
                link(dve.tensor_tensor(r, r, ghi[:, th(h), 0:n], ALU.subtract))
                link(dve.tensor_copy(ghi[:, th(h), 32:32 + n], r))
                link(dve.tensor_tensor(r, r, ghi[:, th(h), 32:32 + n], ALU.subtract))
                dve.tensor_copy(ghi[:, th(h), 64:64 + n], r).then_inc(gates_ready, 1)

            def bias_parts(layer, src, n):
                link(dve.tensor_copy(b2s[:, layer, 0, 0:n], src))
                link(dve.tensor_tensor(b2r[:, 0:n], src, b2s[:, layer, 0, 0:n], ALU.subtract))
                link(dve.tensor_copy(b2s[:, layer, 1, 0:n], b2r[:, 0:n]))
                link(dve.tensor_tensor(b2r[:, 0:n], b2r[:, 0:n], b2s[:, layer, 1, 0:n], ALU.subtract))
                link(dve.tensor_copy(b2s[:, layer, 2, 0:n], b2r[:, 0:n]))

            dve.wait_ge(pack_loaded["l0"], 16)
            blocks = piece("l0", "blocks")
            for n, name in enumerate(("dq", "dk", "dm")):
                await_bank(dve, ("fold", name))
                ins = dve.tensor_tensor(fold[:, n, :], PS[:, plan[("fold", name)][0], 0:P], blocks, ALU.mult)
                read_out(ins, ("fold", name))
            await_bank(dve, ("fold", "c"))
            read_out(dve.tensor_copy(fold_c[:], PS[0:HD, plan[("fold", "c")][0], 0:P]), ("fold", "c"))
            await_bank(dve, ("fold", "v"))
            read_out(dve.tensor_tensor(fold[:, 3, :], PS[:, 4, 0:P], blocks, ALU.mult), ("fold", "v"))
            for h in range(HALVES):
                dve.wait_ge(x_loaded, 16 * h + 16)
                layernorm(0, h)
            for h in range(HALVES):
                for n, (name, raw, w, dst) in enumerate((("sq", rawq, "qnw", qT), ("sk", rawk, "knw", kf))):
                    await_read(dve, (name, h))
                    link(dve.reciprocal(rms[:, n, :], rms[:, n, :]))
                    ins = dve.scalar_tensor_tensor(dst[:, half(h)], raw[:, half(h)], piece("l0", w), rms[:, n, :], ALU.mult, ALU.mult)
                    ins.then_inc((q_ready, k_normed)[n], 1)
                dve.wait_ge(k_normed, h + 1)
                await_bank(dve, ("m0", h))
                read_out(dve.tensor_tensor(kf[:, half(h)], kf[:, half(h)], PS[:, 3, :], ALU.add), ("m0", h))
                await_read(dve, ("m0", h))
                expand_keys(h, 0)
            dve.wait_ge(masks_loaded, 16)
            attention(0)
            for h in range(HALVES):
                layernorm(1, h)
            for h in range(HALVES):
                name = ("xs0", h)
                await_bank(dve, name)
                s = PS[:, h, 0:TPH * S].rearrange("p (t k) -> p t k", k=S)
                link(dve.reduce_max(xtop[:, th(h)], s, AX.X))
                ins = dve.tensor_tensor(xs[:, th(h), :], s, bc(xtop[:, th(h)].unsqueeze(2), [P, TPH, S]), ALU.subtract)
                read_out(ins, name)
                await_read(dve, name)
                dve.wait_ge(xprobs, h + 1)
                link(dve.reduce_sum(xrec[:, th(h)], xs[:, th(h), :], AX.X))
                link(dve.reciprocal(xrec[:, th(h)], xrec[:, th(h)]))
                for t in tiles(h):
                    last = dve.tensor_tensor(x[:, t, :], x[:, t, :], piece("ctx", "bv0"), ALU.add)
                link(last)
            for h in range(HALVES):
                for u in range(2):
                    name = ("xo0", h, u)
                    await_bank(dve, name)
                    for a in range(2):
                        t = TPH * h + 2 * a + u
                        last = dve.scalar_tensor_tensor(x[:, t, :], PS[:, plan[name][0], P * a:P * a + P], xrec[:, t:t + 1], x[:, t, :], ALU.mult, ALU.add)
                    read_out(last, name)
                await_read(dve, ("xo0", h, 1))
                layernorm(2, h)
            dve.wait_ge(pack_loaded["f0"], 16)
            bias_parts(0, piece("f0", "b2"), M0)
            for h in range(HALVES):
                for c in range(2):
                    await_read(dve, ("enc", h, c))
                    dve.tensor_scalar(spk[:, c, :], spk[:, c, :], 0.5, 0.5, ALU.mult, ALU.add).then_inc(spikes_ready, 1)
                route(0, h)
            for h in range(HALVES):
                for e in range(E0):
                    n = E0 * h + e
                    name = ("G0", h, e // 2, e % 2)
                    await_read(dve, ("z0", h, e // 2, e % 2))
                    await_bank(dve, name)
                    if n >= 2:
                        dve.wait_ge(hid0_used, n - 1)
                    read_out(dve.tensor_tensor(hid[:, e % 2, 1, :], relu[:, e % 2, 0, :], PS[:, plan[name][0], :], ALU.mult), name)
            for h in range(HALVES):
                for c in range(2):
                    await_read(dve, ("c2s", h, c))
                    dve.tensor_scalar(spm[h][:, c, :], spm[h][:, c, :], 0.5, 0.5, ALU.mult, ALU.add).then_inc(spikes_ready, 1)
            for h in range(HALVES):
                name = ("dec", h)
                await_bank(dve, name)
                d4 = [P, TPH, D]
                read_out(dve.tensor_tensor(xn[:, th(h), :], PS[:, 2 + h, :].rearrange("p (t d) -> p t d", t=TPH),
                                           bc(piece("f0", "bdec").unsqueeze(1), d4), ALU.add), name)
                await_read(dve, name)
                layernorm(3, h, src=xn, dst=oh)
                dve.wait_ge(xn_ready, 3 * HALVES + h + 1)
                o = oh[:, th(h), :]
                link(dve.tensor_tensor(o, o, bc(piece("f0", "lng").unsqueeze(1), d4), ALU.mult))
                link(dve.tensor_tensor(o, o, bc(piece("f0", "lnb").unsqueeze(1), d4), ALU.add))
                link(dve.tensor_tensor(x[:, th(h), :], x[:, th(h), :], o, ALU.add))
            for h in range(HALVES):
                layernorm(4, h)
            for h in range(HALVES):
                await_read(dve, ("k1", h))
                expand_keys(h, 1)
            attention(1)
            dve.wait_ge(pack_loaded["l1"], 16)
            bias_parts(1, piece("l1", "fb2"), D)
            for h in range(HALVES):
                await_bank(dve, ("pr", h))
                read_out(dve.tensor_tensor(x[:, th(h), :], x[:, th(h), :], PS[:, 7, :].rearrange("p (t d) -> p t d", t=TPH), ALU.add), ("pr", h))
                await_read(dve, ("pr", h))
                layernorm(5, h)
            for t in range(TILES):
                name = ("xs1", t)
                await_bank(dve, name)
                s = PS[:, 0:2, 0:XC * S].rearrange("p q (c k) -> p q c k", c=XC)
                tp = top[:, t % 3, 0:XH].rearrange("p (q c) -> p q c", q=2)
                link(dve.reduce_max(tp, s, AX.X))
                w = sc[:, t % 3, 0:XH * S].rearrange("p (c q k) -> p q c k", q=2, k=S)
                for q in range(2):
                    last = dve.tensor_tensor(w[:, q, :, :], s[:, q, :, :], bc(tp[:, q, :].unsqueeze(2), [P, XC, S]), ALU.subtract)
                read_out(last, name)
                await_read(dve, name)
                dve.wait_ge(xprobs, HALVES + t + 1)
                e = sc[:, t % 3, 0:XH * S].rearrange("p (h k) -> p h k", h=XH)
                link(dve.reduce_sum(orec[:, 0:XH], e, AX.X))
                link(dve.reciprocal(orec[:, 0:XH], orec[:, 0:XH]))
                dve.tensor_tensor(e, e, bc(orec[:, 0:XH].unsqueeze(2), [P, XH, S]), ALU.mult).then_inc(xnorm, 1)
            for h in range(HALVES):
                d4 = [P, TPH, D]
                link(dve.tensor_tensor(x[:, th(h), :], x[:, th(h), :], bc(piece("l1", "xbo").unsqueeze(1), d4), ALU.add))
                name = ("xp1", h)
                await_bank(dve, name)
                read_out(dve.tensor_tensor(x[:, th(h), :], x[:, th(h), :], PS[:, 5 + h, :].rearrange("p (t d) -> p t d", t=TPH), ALU.add), name)
                await_read(dve, name)
                layernorm(6, h)
            for h in range(HALVES):
                route(1, h)

            def pair_of_experts(i, first):
                for u in range(4):
                    fresh = first and u < 2
                    dve.wait_ge(G_full, u + 1 if first else i * 4 + (u + 1))
                    if not fresh:
                        dve.wait_ge(acc_done, u - 1 if first else i * 4 + (u - 1))
                    for c in range(2):
                        dve.wait_ge(relu_ready, 2 * u + c + 1 if first else i * 8 + (2 * u + c + 1))
                        dve.tensor_tensor(hid[:, u % 2, c, :], relu[:, u % 2, c, :], PS[:, 4 + u % 2, :], ALU.mult).then_inc(hid_ready, 1)

            pair_of_experts(0, True)
            with dve.Fori(1, E1 // 2) as i:
                pair_of_experts(i, False)
            for h in range(HALVES):
                name = ("fin", h)
                await_bank(dve, name)
                ins = dve.tensor_tensor(x[:, th(h), :], x[:, th(h), :], PS[:, h, :].rearrange("p (t d) -> p t d", t=TPH), ALU.add)
                ins.then_inc(out_ready, 1)


def ln_order():
    seq = [("ln", 0, h) for h in range(HALVES)] + [("att", 0)]
    for k in (1, 2, 3, 4):
        seq += [("ln", k, h) for h in range(HALVES)]
    seq += [("att", 1)]
    for k in (5, 6):
        seq += [("ln", k, h) for h in range(HALVES)]
    return seq


def _tile_cols(a, n):
    return np.tile(a, (1, n))


def _host_pieces(v):
    heads = np.arange(P) // HD
    rep = P // HD
    w2 = v["L0_ffn_W2"]
    b2 = np.zeros((GW, M0), np.float32)
    fb2 = np.zeros((GW, D), np.float32)
    for n in range(3):
        b2[32 * n:32 * n + E0] = v["L0_ffn_b2"]
        fb2[32 * n:32 * n + E1] = v["L1_ffn_b2"]

    def row(a):
        return np.broadcast_to(a[None, :], (P, a.shape[0]))

    def col(a):
        return a.reshape(-1, P).T

    def cols2(w):
        return w.reshape(-1, P, w.shape[1]).transpose(1, 0, 2).reshape(P, -1)

    s2c = v["L0_ffn_W_s2c"].reshape(2, P, M0).transpose(1, 0, 2)
    return {
        "ident": np.eye(P, dtype=np.float32),
        "blocks": (heads[:, None] == heads[None, :]).astype(np.float32),
        "heads": (heads[:, None] % GRP == np.arange(GRP)[None, :]).astype(np.float32),
        "eps": np.full((P, 1), RMS_EPS, np.float32),
        "qnw": np.tile(v["L0_attn_q_norm_w"], rep)[:, None], "knw": np.tile(v["L0_attn_k_norm_w"], rep)[:, None],
        "dq": _tile_cols(v["L0_attn_W_DQ"], rep), "uqT": _tile_cols(v["L0_attn_W_UQ"].T, rep),
        "dkv": _tile_cols(v["L0_attn_W_DKV"], rep), "ukT": _tile_cols(v["L0_attn_W_UKV"][:HD].T, rep),
        "uvT": v["L0_attn_W_UKV"][HD:].T, "kr": _tile_cols(v["L0_attn_W_KR"], rep),
        "qr": _tile_cols(v["L0_attn_W_QR"], rep), "oT": _tile_cols(v["L0_attn_W_O"].T, rep),
        "ctxT": v["ctx_768"].reshape(TOK, DC).T, "wk0": v["L0_xattn_Wk"], "wv0": v["L0_xattn_Wv"],
        "bk0": col(v["L0_xattn_bk"]), "bv0": row(v["L0_xattn_bv"]), "wq0": v["L0_xattn_Wq"], "bq0": col(v["L0_xattn_bq"]),
        "xk": v["L1_xattn_Wk"], "xv": v["L1_xattn_Wv"],
        "enc": v["L0_ffn_W_enc"], "benc": col(v["L0_ffn_b_enc"]),
        "s2c": np.concatenate([s2c, s2c], axis=2).reshape(P, 2 * P),
        "bs2c": np.tile(v["L0_ffn_b_s2c"], 2)[:, None], "wr": v["L0_ffn_Wr"], "br": row(v["L0_ffn_br"]),
        "iota": row(np.arange(E1, dtype=np.float32)),
        "w1": v["L0_ffn_W1"].reshape(E0 // 2, P, F0H).transpose(1, 0, 2).reshape(P, -1),
        "b1": v["L0_ffn_b1"].T, "w2": w2.transpose(1, 0, 2).reshape(P, -1), "b2": b2,
        "c2s": np.concatenate([v["L0_ffn_W_c2s"]] * 2, axis=0), "bc2s": col(v["L0_ffn_b_c2s"]),
        "dec": cols2(v["L0_ffn_W_dec"]), "bdec": row(v["L0_ffn_b_dec"]), "lng": row(v["L0_ffn_ln_g"]), "lnb": row(v["L0_ffn_ln_b"]),
        "qkv": v["L1_attn_w_qkv"], "proj": v["L1_attn_w_proj"], "xq": v["L1_xattn_Wq"], "xo": cols2(v["L1_xattn_Wo"]),
        "xbo": row(v["L1_xattn_bo"]), "gate": v["L1_ffn_gate"],
        "fb2": fb2,
    }


def _expert_rows(w1, w2, b1):
    w2 = w2.reshape(E1, 2, P, D).transpose(0, 2, 1, 3).reshape(E1, P, 2 * D)
    return np.ascontiguousarray(np.concatenate([w1, w2, b1.reshape(E1, 2, P).transpose(0, 2, 1)], axis=2))


def _masks():
    q = (np.arange(P) % S)[:, None, None]
    k = np.arange(S)[None, None, :]
    first = 2.0 ** (-(2.0 ** -(np.log2(NH) - 3)))
    slopes = np.array([first * first ** n for n in range(NH)], np.float32)[None, :, None]
    keep = np.broadcast_to(k <= q, (P, NH, S))
    causal = np.where(keep, np.float32(0), np.float32(MASKED))
    alibi = np.where(keep, slopes * k.astype(np.float32), np.float32(MASKED))
    return np.stack([causal, alibi], axis=1).astype(np.float32).reshape(P, 2, NH * S)


def kernel(**inputs):
    import concourse.bacc as bacc
    from concourse import mybir
    from concourse.bass_utils import run_bass_kernel_spmd

    v = {k: np.asarray(a) for k, a in inputs.items()}
    pieces = _host_pieces(v)
    arrays = {"x": np.ascontiguousarray(v["x"].reshape(TOK, D)), "masks": _masks(),
              "experts": _expert_rows(v["L1_ffn_W1"], v["L1_ffn_W2"], v["L1_ffn_b1"])}
    for k, parts in PACKS.items():
        packed = np.zeros((P, WIDTH[k]), np.float32)
        for name, rows, cols in parts:
            r, at, c = LAYOUT[k][name]
            packed[:r, at:at + c] = pieces[name]
        arrays[k] = packed
    nc = bacc.Bacc("TRN2", target_bir_lowering=False, num_devices=1)
    dram = {k: nc.dram_tensor(f"in_{k}", a.shape, mybir.dt.float32, kind="ExternalInput").ap() for k, a in arrays.items()}
    out = nc.dram_tensor("out", (TOK, D), mybir.dt.float32, kind="ExternalOutput").ap()
    build(nc, dram, out)
    r = run_bass_kernel_spmd(nc, [{f"in_{k}": a for k, a in arrays.items()}], core_ids=[0])
    return r.results[0]["out"].reshape(B, S, D)
```

```python
import numpy as np

B, S, D, DC = 16, 64, 128, 96
P = 128
TOK = B * S
TILES = TOK // P
HALVES = 2
TPH = TILES // HALVES
HT = TOK // HALVES
PAIR = P // S
LN_EPS = 1e-5
RMS_EPS = 1.1920929e-07
NH, HD = 16, 8
GRP = 4
NG = NH // GRP
XH, XD = 8, 64
XC = XH // 2
E0, K0, M0, F0H = 8, 2, 64, 128
E1, K1, F1H = 16, 3, 256
GW = 96
EXPERT = F1H + 2 * D + 2
MASKED = -1e30


def _pack_layout(parts):
    at, out = 0, {}
    for name, rows, cols in parts:
        out[name] = (rows, at, cols)
        at += cols
    return out, at


PACKS = {
    "l0": [("ident", P, P), ("iota", P, E1), ("blocks", P, P), ("heads", P, GRP), ("eps", P, 1), ("qnw", P, 1), ("knw", P, 1),
           ("dq", 64, P), ("uqT", 64, P), ("dkv", P, P), ("ukT", P, P), ("uvT", P, HD), ("kr", 64, P),
           ("qr", 64, P), ("oT", HD, P)],
    "ctx": [("ctxT", DC, TOK), ("wk0", DC, P), ("wv0", DC, P), ("bk0", P, 1), ("bv0", P, P), ("wq0", P, P),
            ("bq0", P, 1), ("xk", DC, XH * XD), ("xv", DC, XH * XD)],
    "f0": [("enc", P, 256), ("benc", P, 2), ("s2c", P, 2 * P), ("bs2c", P, 1), ("wr", M0, E0), ("br", P, E0),
           ("w1", P, (E0 // 2) * F0H), ("b1", P, E0), ("w2", P, E0 * M0), ("b2", GW, M0),
           ("c2s", P, 256), ("bc2s", P, 2), ("dec", P, 2 * P), ("bdec", P, P), ("lng", P, P), ("lnb", P, P)],
    "l1": [("qkv", P, 3 * P), ("proj", P, P), ("xq", P, XH * XD), ("xo", P, XC * P), ("xbo", P, P),
           ("gate", P, E1), ("fb2", GW, P)],
}
LAYOUT = {k: _pack_layout(v)[0] for k, v in PACKS.items()}
WIDTH = {k: _pack_layout(v)[1] for k, v in PACKS.items()}


ORDER = """
    fold stats.0.0 turn.0.0 stats.0.1 qk0.0 turn.0.1 rms0.0 qk0.1 qkT0.0 rms0.1 expand.0.0 v.0.0 qkT0.1
    expand.0.1 scores.0.0 v.0.1 scores.0.4 exp.0.4 scores.0.5 scores.0.1 exp.0.0 weights.0.4 weights.0.0
    ck1.0.0 ck0.1 values.0.0 ck1.1.0 cv0.0 values.0.4 exp.0.5 ck1.0.1 ck0.0 exp.0.1 scores.0.2 weights.0.5
    weights.0.1 scores.0.6 cv0.1 ck1.1.1 values.0.1 scores.0.3 exp.0.2 weights.0.2 values.0.5 scores.0.7
    exp.0.6 weights.0.6 ck1.2.0 values.0.2 ck1.2.1 exp.0.3 values.0.6 exp.0.7 weights.0.3 weights.0.7
    ck1.3.0 values.0.3 stats.1.0 values.0.7 ck1.3.1 stats.1.1 turn.1.0 xq0.0 turn.1.1 xs0.0 xq0.1 xs0.1
    xo0.0 stats.2.0 xo0.1 turn.2.0 stats.2.1 enc.0 turn.2.1 s2c.0 enc.1 route.0.0 pick.0.0 s2c.1 route.0.1
    pick.0.1 gates.0.0 up0.0.0 gates.0.1 down0.0.0 up0.1.0 up0.0.1 down0.1.0 up0.1.1 down0.0.1 up0.0.2
    down0.1.1 up0.1.2 down0.0.2 up0.0.3 down0.1.2 down0.0.3 up0.1.3 c2s.0 down0.1.3 dec.0 c2s.1 stats.3.0
    dec.1 stats.3.1 inner.3.0 stats.4.0 inner.3.1 turn.4.0 qk1.0 stats.4.1 turn.4.1 qk1.1 expand.1.1 v.1.1
    expand.1.0 v.1.0 scores.1.4 scores.1.0 scores.1.1 scores.1.5 exp.1.4 exp.1.0 weights.1.0 cv1.0
    weights.1.4 values.1.0 exp.1.1 cv1.4 scores.1.2 values.1.4 exp.1.5 scores.1.6 weights.1.1 cv1.1
    weights.1.5 values.1.1 exp.1.2 cv1.5 scores.1.3 values.1.5 exp.1.6 scores.1.7 weights.1.2 cv1.2
    weights.1.6 values.1.2 exp.1.3 values.1.6 exp.1.7 weights.1.3 cv1.7 cv1.3 weights.1.7 values.1.3
    values.1.7 proj1.0 stats.5.0 proj1.1 cv1.6 stats.5.1 turn.5.0 xq1.0 turn.5.1 xs1.0 xq1.1 xexp1.0 xs1.4
    xs1.5 xs1.1 xw1.0 xexp1.4 xo1.0 xw1.4 xp1.0 xexp1.1 xo1.4 xs1.2 xw1.1 xp1.4 xexp1.5 xs1.6 xo1.1 xp1.1
    xexp1.2 xw1.5 xo1.5 xs1.3 xw1.2 xp1.5 xexp1.6 xs1.7 xo1.2 xw1.6 xp1.2 xexp1.3 xo1.6 xw1.3 xp1.6 xexp1.7
    xo1.3 xp1.3 stats.6.0 xw1.7 xo1.7 turn.6.0 xp1.7 stats.6.1 route.1.0 turn.6.1 pick.1.0 route.1.1
    gates.1.0 pick.1.1 gates.1.1 experts
"""


def schedule():
    return [tuple(int(a) if a.isdigit() else a for a in word.split(".")) for word in ORDER.split()]


def bank_plan(order):
    held, counts, plan, turn, kept = {}, {}, {}, list(range(4, 8)), set()

    def lend(name, *banks):
        before = []
        for b in banks:
            if b in held and held[b] not in before:
                before.append(held[b])
        counts[banks[0]] = counts.get(banks[0], 0) + 1
        for b in banks:
            held[b] = (banks[0], counts[banks[0]])
        plan[name] = (banks[0], counts[banks[0]], before, banks)

    def any_bank(name, keep=False):
        b = next(b for b in turn if b not in kept)
        turn.remove(b)
        turn.append(b)
        if keep:
            kept.add(b)
        lend(name, b)
        return b

    n = 0
    for step in order:
        kind = step[0]
        h = step[-1]
        if kind == "fold":
            for i, w in enumerate(("dq", "dk", "dm", "c")):
                lend(("fold", w), i)
            lend(("fold", "v"), 4)
        elif kind == "turn":
            any_bank(("lnT", step[1], h))
        elif kind in ("qk0", "qk1"):
            any_bank(("q" + kind[2], h))
            any_bank(("k" + kind[2], h))
        elif kind == "qkT0":
            for w in ("qT0", "kT0", "m0"):
                any_bank((w, h))
        elif kind == "v":
            any_bank(("v%d" % step[1], h))
        elif kind == "scores":
            lend(("s", step[1], h), 0, 1, 2, 3)
        elif kind == "weights":
            for g in range(2):
                any_bank(("t", step[1], h, g))
        elif kind == "values":
            any_bank(("o", step[1], h))
        elif kind in ("ck0", "cv0", "ck1", "cv1"):
            any_bank(step)
        elif kind in ("xq0", "xs0", "s2c", "dec", "xp1"):
            any_bank(step)
        elif kind == "xo0":
            any_bank(("xt0", h))
            for u in range(2):
                any_bank(("xo0", h, u))
        elif kind in ("enc", "c2s"):
            for c in range(2):
                any_bank((kind, h, c))
        elif kind == "route":
            any_bank(("rt%d" % step[1], h))
        elif kind == "gates":
            any_bank(("g%d" % step[1], h))
        elif kind == "up0":
            if h == 0:
                any_bank(("y0", step[1]), keep=True)
            for q in range(2):
                lend(("z0", step[1], h, q), n % 4)
                lend(("G0", step[1], h, q), (n + 1) % 4)
                n += 2
        elif kind == "down0" and h == E0 // 2 - 1:
            kept.discard(plan[("y0", step[1])][0])
        elif kind == "proj1":
            any_bank(("oT", h))
            any_bank(("pr", h))
        elif kind == "xq1":
            for c in range(XC):
                any_bank(("xq1", h, c))
        elif kind == "xs1":
            lend(("xs1", h), 2 * (h // TPH), 2 * (h // TPH) + 1)
        elif kind == "xw1":
            any_bank(("xt1", h))
        elif kind == "xo1":
            for q in range(2):
                any_bank(("xo1", h, q))
        elif kind == "experts":
            lend(("experts",), *range(8))
            for i in range(HALVES):
                lend(("fin", i), i)
    return plan


def build(nc, dram, out):
    import concourse.bass as bass
    from concourse import mybir
    from contextlib import ExitStack

    f32, f32r, bf16, u32 = mybir.dt.float32, mybir.dt.float32r, mybir.dt.bfloat16, mybir.dt.uint32
    ALU, ACT, AX = mybir.AluOpType, mybir.ActivationFunctionType, mybir.AxisListType
    order = schedule()
    plan = bank_plan(order)

    def nth(*step):
        return [s for s in order if s[0] == step[0]].index(step) + 1

    with ExitStack() as ctx:
        def sb(name, shape, dt=f32):
            return ctx.enter_context(nc.sbuf_tensor(name, shape, dt))

        def sem(name):
            return ctx.enter_context(nc.semaphore(name))

        PS = ctx.enter_context(nc.psum_tensor("banks", [P, 8, 512], f32))

        x = sb("x", [P, TILES, D])
        xn = sb("xn", [P, TILES, D])
        xnT = sb("xnT", [P, TOK])
        kf = sb("kf", [P, TOK])
        stats = sb("stats", [P, TILES, 6])
        mv = sb("mv", [P, TILES, 2])
        veps = sb("veps", [P, TILES])
        half_neg = sb("half_neg", [P, TPH])
        zero = sb("zero", [P, 1])
        rstd = sb("rstd", [P, TILES])
        rl = sb("rl", [P, TILES, E1])
        r8 = sb("r8", [P, TILES, 8])
        i8 = sb("i8", [P, TILES, 8], u32)
        i8f = sb("i8f", [P, TILES, 8])
        eq = sb("eq", [P, TILES, K1, E1])
        pick = sb("pick", [P, TILES, E1])
        rsum = sb("rsum", [P, TILES])
        ghi = sb("ghi", [P, TILES, GW], bf16)
        g3T = sb("g3T", [P, TOK], bf16)
        sel = sb("sel", [P, E1, P], bf16)
        identb = sb("identb", [P, P], bf16)
        b2s = sb("b2s", [GW, 2, 3, P], bf16)
        b2r = sb("b2r", [GW, P])
        ws = sb("ws", [P, 2, EXPERT])
        relu = sb("relu", [P, 2, 2, HT])
        packs = {k: sb(f"pack_{k}", [P, WIDTH[k]]) for k in ("l0", "l1")}

        early = ExitStack()

        def eb(name, shape, dt=f32):
            return early.enter_context(nc.sbuf_tensor(name, shape, dt))

        packs.update({k: eb(f"pack_{k}", [P, WIDTH[k]]) for k in ("ctx", "f0")})
        masks = eb("masks", [P, 2, NH * S])
        fold = eb("fold", [P, 4, P])
        fold_c = eb("fold_c", [HD, P])
        wide = eb("wide", [P, HALVES, 2, HT])
        ssum = eb("ssum", [P, HALVES, 2, TPH * NH])
        rawq = eb("rawq", [P, TOK])
        contT = eb("contT", [P, TOK])
        qT = eb("qT", [P, TOK])
        kexp = eb("kexp", [P, GRP, TOK])
        vx = eb("vx", [P, B, NH // 2, 2 * (HD + 1)])
        sc = eb("sc", [P, 2 * HALVES, NH * S])
        pT = eb("pT", [P, HALVES, NH // 2, P])
        top = eb("top", [P, 2 * HALVES, NH])
        orec = eb("orec", [P, 2 * HALVES, NH])
        oh = eb("oh", [P, TILES, D])
        k0T = eb("k0T", [P, TOK])
        v0 = eb("v0", [P, TILES // 2, PAIR, D])
        k1T = eb("k1T", [P, XC, TOK])
        v1 = eb("v1", [P, B, XC, XD])
        xs = eb("xs", [P, TILES, S])
        xtop = eb("xtop", [P, TILES])
        xrec = eb("xrec", [P, TILES])
        halfb = eb("halfb", [P, 4])
        spk = wide
        q1T = kexp
        early.close()
        hid = sb("hid", [P, 2, 2, HT])
        bias1 = sb("bias1", [P, 2, 2])
        w1r = sb("w1r", [P, 2, 2, F1H], f32r)
        w2r = sb("w2r", [P, 2, 2, 2 * D], f32r)
        xr = sb("xr", [P, 2, TOK], f32r)
        hr = sb("hr", [P, 4, 2, 2, HT], f32r)
        accT = kf

        def piece(pack, name):
            rows, at, cols = LAYOUT[pack][name]
            return packs[pack][0:rows, at:at + cols]

        bank_full = [sem(f"bank_full{b}") for b in range(8)]
        bank_read = [sem(f"bank_read{b}") for b in range(8)]
        x_loaded, masks_loaded = sem("x_loaded"), sem("masks_loaded")
        pack_loaded = {k: sem(f"pack_{k}_loaded") for k in PACKS}
        fill_set, identb_set, halfb_set, b2_split = sem("fill_set"), sem("identb_set"), sem("halfb_set"), sem("b2_split")
        stats_ready, rstd_ready, xn_ready = sem("stats_ready"), sem("rstd_ready"), sem("xn_ready")
        squares_ready, squares_summed, roots_ready, qk_normed = (sem(n) for n in ("squares_ready", "squares_summed", "roots_ready", "qk_normed"))
        k_ready = sem("k_ready")
        top_ready, shifted, probs_ready = sem("top_ready"), sem("shifted"), sem("probs_ready")
        xprobs0, xprobs1, xrec_ready, xnorm = sem("xprobs0"), sem("xprobs1"), sem("xrec_ready"), sem("xnorm")
        spikes_in, spikes_out, hid0_used = sem("spikes_in"), sem("spikes_out"), sem("hid0_used")
        logits_shifted, exp_ready, gates_ready = sem("logits_shifted"), sem("exp_ready"), sem("gates_ready")
        dve_step, act_step, pool_step = sem("dve_step"), sem("act_step"), sem("pool_step")
        w_loaded = [sem(f"w_loaded{n}") for n in range(2)]
        part_high = sem("part_high")
        w1_split, w2_split, x_split = sem("w1_split"), sem("w2_split"), sem("x_split")
        z_full, G_full, acc_done = sem("z_full"), sem("G_full"), sem("acc_done")
        relu_ready, hid_ready, high_ready, low_ready = (sem(n) for n in ("relu_ready", "hid_ready", "high_ready", "low_ready"))
        out_ready, stored = sem("out_ready"), sem("stored")

        def filled(ins, name):
            ins.then_inc(bank_full[plan[name][0]], 1)

        def await_bank(eng, name):
            eng.wait_ge(bank_full[plan[name][0]], plan[name][1])

        def read_out(ins, name):
            ins.then_inc(bank_read[plan[name][0]], 1)

        def await_read(eng, name):
            eng.wait_ge(bank_read[plan[name][0]], plan[name][1])

        def chain(eng, signal):
            n = [0]

            def link(ins):
                n[0] += 1
                ins.then_inc(signal, 1)
                eng.wait_ge(signal, n[0])
            return link

        def bank(name, i=0):
            return PS[:, plan[name][3][i], :]

        def tok(t, j=None):
            return slice(P * t, P * t + P) if j is None else slice(P * t + S * j, P * t + S * j + S)

        def rows(j):
            return slice(S * j, S * j + S)

        def half(h):
            return slice(HT * h, HT * h + HT)

        def tiles(h):
            return range(TPH * h, TPH * h + TPH)

        def th(h):
            return slice(TPH * h, TPH * h + TPH)

        def slot(t):
            return 2 * (t // TPH) + t % 2

        def before(t, n=1):
            return t - n if t - n >= TPH * (t // TPH) else None

        def bc(ap, shape):
            return ap.broadcast_to(shape)

        def by_tile(ap):
            return ap.rearrange("p (t d) -> p t d", t=TPH)

        block = ctx.enter_context(nc.Block())

        @block.sync
        def _(sp):
            xv = dram["x"].rearrange("(t p) d -> p t d", p=P)
            sp.dma_start(x[:, th(0), :], xv[:, th(0), :]).then_inc(x_loaded, 16)
            sp.dma_start(packs["l0"][:], dram["l0"]).then_inc(pack_loaded["l0"], 16)
            sp.dma_start(x[:, th(1), :], xv[:, th(1), :]).then_inc(x_loaded, 16)
            sp.dma_start(masks[:], dram["masks"]).then_inc(masks_loaded, 16)
            for k in ("ctx", "f0", "l1"):
                sp.dma_start(packs[k][:], dram[k]).then_inc(pack_loaded[k], 16)

            def load_expert(e, slot):
                sp.dma_start(ws[:, slot, :], dram["experts"][e, :, :]).then_inc(w_loaded[slot], 16)

            for e in range(2):
                load_expert(e, e)
            with sp.Fori(1, E1 // 2) as i:
                for n in range(2):
                    sp.wait_ge(w2_split, i * 2 + (n - 1))
                    load_expert(i * 2 + n, n)
            o = out.rearrange("(t p) d -> p t d", p=P)
            for h in range(HALVES):
                sp.wait_ge(out_ready, h + 1)
                sp.dma_start(o[:, th(h), :], x[:, th(h), :]).then_inc(stored, 16)
            sp.wait_ge(stored, 16 * HALVES)

        @block.gpsimd
        def _(pool):
            link = chain(pool, pool_step)
            link(pool.memset(half_neg[:], -0.5))
            link(pool.memset(zero[:], 0.0))

            def rsqrt(k, h):
                pool.wait_ge(stats_ready, nth("stats", k, h))
                link(pool.tensor_scalar(veps[:, th(h)], mv[:, th(h), 1], LN_EPS, None, ALU.add))
                pool.tensor_tensor(rstd[:, th(h)], veps[:, th(h)], half_neg[:], ALU.pow).then_inc(rstd_ready, 1)

            def fill():
                link(pool.memset(vx[:], 0.0))
                for q in range(2):
                    link(pool.memset(vx[rows(q), :, :, 9 * q + 8:9 * q + 9], 1.0))
                link(pool.memset(ghi[:], 0.0))
                link(pool.memset(g3T[:], 0.0))
                link(pool.memset(sel[:], 0.0))
                for part in range(3):
                    ins = pool.affine_select(out=sel[:], in_=sel[:], compare_op=ALU.not_equal, fill=1.0, base=-32 * part,
                                             pattern=[[-1, E1], [0, P]], channel_multiplier=1)
                    if part < 2:
                        link(ins)
                ins.then_inc(fill_set, 1)

            def copied(o, a):
                return pool.tensor_tensor(o, a, bc(zero[:, 0:1], [P, a.shape[1]]), ALU.add)

            def split_weights(i, n, first):
                pool.wait_ge(w_loaded[n], 16 if first else i * 16 + 16)
                if not first:
                    pool.wait_ge(relu_ready, i * 8 + (4 * n - 4))
                copied(bias1[:, n, :], ws[:, n, 2 * F1H:2 * F1H + 2])
                copied(w1r[:, n, 0, :], ws[:, n, 0:F1H]).then_inc(part_high, 1)
                pool.wait_ge(part_high, 2 * n + 1 if first else i * 4 + (2 * n + 1))
                pool.tensor_tensor(w1r[:, n, 1, :], ws[:, n, 0:F1H], w1r[:, n, 0, :].bitcast(f32), ALU.subtract).then_inc(w1_split, 1)
                if not first:
                    pool.wait_ge(acc_done, i * 4 + (2 * n - 2))
                copied(w2r[:, n, 0, :], ws[:, n, F1H:F1H + 2 * D]).then_inc(part_high, 1)
                pool.wait_ge(part_high, 2 * n + 2 if first else i * 4 + (2 * n + 2))
                pool.tensor_tensor(w2r[:, n, 1, :], ws[:, n, F1H:F1H + 2 * D], w2r[:, n, 0, :].bitcast(f32), ALU.subtract).then_inc(w2_split, 1)

            for step in order:
                kind, h = step[0], step[-1]
                if kind == "stats":
                    rsqrt(step[1], h)
                    if step == ("stats", 0, HALVES - 1):
                        fill()
                elif kind == "scores":
                    pool.wait_ge(top_ready, nth(*step))
                    s = sc[:, slot(h), :].rearrange("p (h k) -> p h k", h=NH)
                    pool.tensor_tensor(s, s, bc(top[:, slot(h), :].unsqueeze(2), [P, NH, S]), ALU.subtract).then_inc(shifted, 1)
                elif kind == "xexp1":
                    pool.wait_ge(xrec_ready, nth(*step))
                    e = sc[:, slot(h), 0:XH * S].rearrange("p (h k) -> p h k", h=XH)
                    pool.tensor_tensor(e, e, bc(orec[:, slot(h), 0:XH].unsqueeze(2), [P, XH, S]), ALU.mult).then_inc(xnorm, 1)
                elif kind == "experts":
                    for n in range(2):
                        split_weights(0, n, True)
                    with pool.Fori(1, E1 // 2) as i:
                        for n in range(2):
                            split_weights(i, n, False)

        @block.tensor
        def _(pe):
            def claim(name):
                for key, count in plan[name][2]:
                    pe.wait_ge(bank_read[key], count)
                return bank(name)

            def mm(o, w, m, start=True, stop=True, **kw):
                return pe.matmul(o, w, m, start=start, stop=stop, **kw)

            ident = piece("l0", "ident")

            def product(name, w, m):
                b = claim(name)
                filled(mm(b[0:w.shape[1], :], w, m), name)

            def turned(name, src, h, identity=ident):
                b = claim(name)
                for i in range(TPH):
                    last = pe.transpose(b[:, P * i:P * i + P], src[:, P * i:P * i + P], identity)
                filled(last, name)

            def fold_weights():
                pe.wait_ge(pack_loaded["l0"], 16)
                for name, a, c in (("dq", "dq", "uqT"), ("dk", "dkv", "ukT"), ("dm", "kr", "qr"), ("c", "uvT", "dkv")):
                    b = claim(("fold", name))
                    w, m = piece("l0", a), piece("l0", c)
                    filled(mm(b[0:w.shape[1], 0:P], w, m), ("fold", name))
                b = claim(("fold", "v"))
                await_read(pe, ("fold", "c"))
                filled(mm(b[:, 0:P], fold_c[:], piece("l0", "oT")), ("fold", "v"))
                await_read(pe, ("fold", "v"))

            def values(name, h, w):
                b = claim(name)
                wv = w.rearrange("p (c q d) -> p q c d", q=2, d=HD)
                for n in range(B // HALVES):
                    for q in range(2):
                        last = mm(b[rows(q), 64 * n:64 * n + 64], xnT[:, HT * h + S * n:HT * h + S * n + S], wv[:, q, :, :])
                filled(last, name)

            def context(name):
                pe.wait_ge(pack_loaded["ctx"], 16)
                ctxT = piece("ctx", "ctxT")
                if name[0] == "ck0":
                    product(name, piece("ctx", "wk0"), ctxT[:, half(name[1])])
                elif name[0] == "ck1":
                    product(name, piece("ctx", "xk")[:, P * name[1]:P * name[1] + P], ctxT[:, half(name[2])])
                elif name[0] == "cv0":
                    b = claim(name)
                    for a in range(2):
                        for j in range(PAIR):
                            for u in range(2):
                                last = mm(b[rows(u), P * (2 * a + j):P * (2 * a + j) + P],
                                          ctxT[:, tok(TPH * name[1] + 2 * a + u, j)], piece("ctx", "wv0"))
                    filled(last, name)
                else:
                    b = claim(name)
                    w = piece("ctx", "xv").rearrange("p (c q d) -> p q c d", q=2, d=XD)
                    for n in range(2):
                        for q in range(2):
                            s0 = S * (2 * name[1] + n)
                            last = mm(b[rows(q), 256 * n:256 * n + 256], ctxT[:, s0:s0 + S], w[:, q, :, :])
                    filled(last, name)

            def scores(layer, t):
                claim(("s", layer, t))
                if layer == 1:
                    await_read(pe, ("q1", t // TPH))
                else:
                    await_read(pe, ("qT0", t // TPH))
                pe.wait_ge(k_ready, nth("expand", layer, t // TPH))
                for i in range(NG):
                    g = slice(32 * i, 32 * i + 32)
                    for j in range(PAIR):
                        last = mm(PS[rows(j), i, 0:GRP * S], qT[g, tok(t, j)], kexp[g, :, tok(t, j)])
                filled(last, ("s", layer, t))

            def turn_weights(layer, t):
                pe.wait_ge(probs_ready, nth("exp", layer, t))
                for g in range(2):
                    b = claim(("t", layer, t, g))
                    for c in range(4):
                        k0 = P * (4 * g + c)
                        last = pe.transpose(b[:, P * c:P * c + P], sc[:, slot(t), k0:k0 + P], ident)
                    filled(last, ("t", layer, t, g))

            def heads(layer, t):
                b = claim(("o", layer, t))
                await_read(pe, ("v%d" % layer, t // TPH))
                for g in range(2):
                    await_read(pe, ("t", layer, t, g))
                for c in range(NH // 2):
                    for j in range(PAIR):
                        last = mm(b[rows(j), 18 * c:18 * c + 18], pT[:, t // TPH, c, rows(j)], vx[:, 2 * t + j, c, :])
                filled(last, ("o", layer, t))

            def experts():
                claim(("experts",))
                for h in range(HALVES):
                    await_read(pe, ("g1", h))

                def exact(o, w, m, start=False):
                    for n, (a, b) in enumerate(((0, 0), (0, 1), (1, 0))):
                        last = mm(o, w[:, a, :], m[:, b, :], start=(start and n == 0), stop=(start and n == 2), skip_group_check=not start)
                    return last

                def down(i, u, first):
                    n, h = (u % 4) // 2, u % 2
                    if h == 0:
                        pe.wait_ge(w2_split, u // 2 + 1 if first else i * 2 + (u // 2 + 1))
                    for c in range(2):
                        pe.wait_ge(low_ready, 2 * u + c + 1 if first else i * 8 + (2 * u + c + 1))
                        for k, (a, b) in enumerate(((0, 0), (0, 1), (1, 0))):
                            last = mm(PS[:, 6 + h, :], w2r[:, n, a, P * c:P * c + P], hr[:, u % 4, c, b, :],
                                      start=(first and u in (0, 1) and c == 0 and k == 0), stop=False, skip_group_check=True)
                    last.then_inc(acc_done, 1)

                def pair_of_experts(i, first):
                    for u in range(4):
                        n, h, ub = u // 2, u % 2, u % 2
                        fresh = first and u < 2
                        if not fresh:
                            pe.wait_ge(hid_ready, 2 * (u - 2) + 2 if first else i * 8 + (2 * (u - 2) + 2))
                        mm(PS[:, 4 + ub, :], sel[:, (n if first else i * 2 + n), :], g3T[:, half(h)]).then_inc(G_full, 1)
                        if h == 0:
                            pe.wait_ge(w1_split, n + 1 if first else i * 2 + (n + 1))
                        for c in range(2):
                            if not fresh:
                                pe.wait_ge(relu_ready, 2 * (u - 2) + c + 1 if first else i * 8 + (2 * (u - 2) + c + 1))
                            exact(PS[:, 2 * ub + c, :], w1r[:, n, :, P * c:P * c + P], xr[:, :, half(h)], start=True).then_inc(z_full, 1)
                        if not fresh:
                            down(i, u - 2, first)

                pe.wait_ge(x_split, HALVES)
                pair_of_experts(0, True)
                with pe.Fori(1, E1 // 2) as i:
                    pair_of_experts(i, False)
                for u in (2 * E1 - 2, 2 * E1 - 1):
                    down(0, u, True)
                pe.wait_ge(b2_split, 2)
                for h in range(HALVES):
                    for n in range(3):
                        last = mm(PS[:, 6 + h, :], b2s[:, 1, n, :], g3T[0:GW, half(h)],
                                  start=False, stop=True, skip_group_check=True)
                filled(last, ("experts",))
                await_read(pe, ("experts",))
                for h in range(HALVES):
                    turned(("fin", h), accT[:, half(h)], h)

            for step in order:
                kind, h = step[0], step[-1]
                if kind == "fold":
                    fold_weights()
                elif kind == "turn":
                    pe.wait_ge(xn_ready, nth(*step))
                    turned(("lnT", step[1], h), xn[:, th(h), :].rearrange("p t d -> p (t d)"), h)
                elif kind == "qk0":
                    await_read(pe, ("lnT", 0, h))
                    for n, name in enumerate(("q0", "k0")):
                        b = claim((name, h))
                        for i, t in enumerate(tiles(h)):
                            last = mm(b[:, P * i:P * i + P], xnT[:, tok(t)], fold[:, n, :])
                        filled(last, (name, h))
                elif kind == "qkT0":
                    for n, name in enumerate(("qT0", "kT0")):
                        pe.wait_ge(qk_normed, 2 * nth("rms0", h) - 1 + n)
                        turned((name, h), wide[:, h, n, :], h)
                    product(("m0", h), fold[:, 2, :], xnT[:, half(h)])
                elif kind == "v":
                    await_read(pe, ("lnT", (0, 4)[step[1]], h))
                    values(("v%d" % step[1], h), h, fold[:, 3, :] if step[1] == 0 else piece("l1", "qkv")[:, 2 * P:3 * P])
                elif kind == "scores":
                    scores(step[1], h)
                elif kind == "weights":
                    turn_weights(step[1], h)
                elif kind == "values":
                    heads(step[1], h)
                elif kind in ("ck0", "ck1", "cv0", "cv1"):
                    context(step)
                elif kind == "xq0":
                    await_read(pe, ("lnT", 1, h))
                    product(("xq0", h), piece("ctx", "wq0"), xnT[:, half(h)])
                elif kind == "xs0":
                    b = claim(("xs0", h))
                    await_read(pe, ("xq0", h))
                    await_read(pe, ("ck0", h))
                    for i, t in enumerate(tiles(h)):
                        for j in range(PAIR):
                            last = mm(b[rows(j), S * i:S * i + S], rawq[:, tok(t, j)], k0T[:, tok(t, j)])
                    filled(last, ("xs0", h))
                elif kind == "xo0":
                    b = claim(("xt0", h))
                    pe.wait_ge(xprobs0, nth("xs0", h))
                    for a in range(2):
                        t = TPH * h + 2 * a
                        last = pe.transpose(b[:, P * a:P * a + P], xs[:, t:t + 2, :], ident)
                    filled(last, ("xt0", h))
                    await_read(pe, ("xt0", h))
                    await_read(pe, ("cv0", h))
                    for u in range(2):
                        b = claim(("xo0", h, u))
                        for a in range(2):
                            for j in range(PAIR):
                                last = mm(b[rows(j), P * a:P * a + P], pT[rows(u), h, a, rows(j)],
                                          v0[rows(u), 2 * h + a, j, :])
                        filled(last, ("xo0", h, u))
                elif kind == "enc":
                    pe.wait_ge(pack_loaded["f0"], 16)
                    await_read(pe, ("lnT", 2, h))
                    for c in range(2):
                        product(("enc", h, c), piece("f0", "enc")[:, P * c:P * c + P], xnT[:, half(h)])
                elif kind == "s2c":
                    b = claim(("s2c", h))
                    for c in range(2):
                        pe.wait_ge(spikes_in, 2 * nth("enc", h) - 1 + c)
                        last = mm(b, piece("f0", "s2c")[:, P * c:P * c + P], spk[:, h, c, :], start=(c == 0), stop=(c == 1))
                    filled(last, ("s2c", h))
                elif kind == "route":
                    n = (E0, E1)[step[1]]
                    name = ("rt%d" % step[1], h)
                    b = claim(name)
                    await_read(pe, ("s2c", h) if step[1] == 0 else ("lnT", 6, h))
                    for i, t in enumerate(tiles(h)):
                        w, m = (contT[0:M0, tok(t)], piece("f0", "wr")) if step[1] == 0 else (xnT[:, tok(t)], piece("l1", "gate"))
                        last = mm(b[:, n * i:n * i + n], w, m)
                    filled(last, name)
                elif kind == "gates":
                    name = ("g%d" % step[1], h)
                    b = claim(name).bitcast(bf16)
                    pe.wait_ge(identb_set, 1)
                    pe.wait_ge(gates_ready, nth("pick", step[1], h))
                    for i, t in enumerate(tiles(h)):
                        last = pe.transpose(b[0:GW, P * i:P * i + P], ghi[:, t, :], identb[:])
                    filled(last, name)
                elif kind == "up0":
                    g, p = step[1], step[2]
                    if p == 0:
                        pe.wait_ge(fill_set, 1)
                        await_read(pe, ("g0", g))
                    for q in range(2):
                        product(("z0", g, p, q), piece("f0", "w1")[rows(q), F0H * p:F0H * p + F0H], contT[rows(q), half(g)])
                        product(("G0", g, p, q), sel[:, 2 * p + q, :], g3T[:, half(g)])
                elif kind == "down0":
                    g, p = step[1], step[2]
                    b = claim(("y0", g)) if p == 0 else bank(("y0", g))
                    for q in range(2):
                        e = 2 * p + q
                        await_read(pe, ("G0", g, p, q))
                        mm(b[rows(q), :], piece("f0", "w2")[:, M0 * e:M0 * e + M0], wide[:, g, q, :],
                           start=(p == 0), stop=(q == 1 and p == E0 // 2 - 1), skip_group_check=True).then_inc(hid0_used, 1)
                    if p == E0 // 2 - 1:
                        pe.wait_ge(b2_split, 1)
                        for n in range(3):
                            last = mm(b[rows(0), :], b2s[:, 0, n, 0:M0], g3T[0:GW, half(g)],
                                      start=False, stop=True, skip_group_check=True)
                        filled(last, ("y0", g))
                elif kind == "c2s":
                    await_read(pe, ("y0", h))
                    for c in range(2):
                        product(("c2s", h, c), piece("f0", "c2s")[:, P * c:P * c + P], accT[:, half(h)])
                elif kind == "dec":
                    b = claim(("dec", h))
                    pe.wait_ge(spikes_out, 2 * nth("c2s", h))
                    for i in range(TPH):
                        for c in range(2):
                            last = mm(b[:, P * i:P * i + P], relu[:, h, c, P * i:P * i + P], piece("f0", "dec")[:, P * c:P * c + P],
                                      start=(c == 0), stop=(c == 1))
                    filled(last, ("dec", h))
                elif kind == "qk1":
                    await_read(pe, ("lnT", 4, h))
                    pe.wait_ge(pack_loaded["l1"], 16)
                    product(("q1", h), piece("l1", "qkv")[:, 0:P], xnT[:, half(h)])
                    product(("k1", h), piece("l1", "qkv")[:, P:2 * P], xnT[:, half(h)])
                elif kind == "proj1":
                    await_read(pe, ("o", 1, TPH * h + TPH - 1))
                    turned(("oT", h), oh[:, th(h), :].rearrange("p t d -> p (t d)"), h)
                    b = claim(("pr", h))
                    await_read(pe, ("oT", h))
                    for i, t in enumerate(tiles(h)):
                        last = mm(b[:, P * i:P * i + P], rawq[:, tok(t)], piece("l1", "proj"))
                    filled(last, ("pr", h))
                elif kind == "xq1":
                    await_read(pe, ("lnT", 5, h))
                    for c in range(XC):
                        product(("xq1", h, c), piece("l1", "xq")[:, P * c:P * c + P], xnT[:, half(h)])
                elif kind == "xs1":
                    claim(("xs1", h))
                    for c in range(XC):
                        await_read(pe, ("xq1", h // TPH, c))
                        await_read(pe, ("ck1", c, h // TPH))
                    for c in range(XC):
                        for q in range(2):
                            for j in range(PAIR):
                                last = mm(bank(("xs1", h), q)[rows(j), S * c:S * c + S], q1T[rows(q), c, tok(h, j)],
                                          k1T[rows(q), c, tok(h, j)])
                    filled(last, ("xs1", h))
                elif kind == "xw1":
                    pe.wait_ge(xnorm, nth("xexp1", h))
                    b = claim(("xt1", h))
                    for c in range(XC):
                        last = pe.transpose(b[:, P * c:P * c + P], sc[:, slot(h), P * c:P * c + P], ident)
                    filled(last, ("xt1", h))
                elif kind == "xo1":
                    bs = [claim(("xo1", h, q)) for q in range(2)]
                    await_read(pe, ("xt1", h))
                    await_read(pe, ("cv1", h))
                    last = [None, None]
                    for c in range(XC):
                        for q in range(2):
                            for j in range(PAIR):
                                last[q] = mm(bs[q][rows(q), P * c + S * j:P * c + S * j + S],
                                             v1[rows(q), 2 * h + j, c, :], pT[rows(q), h // TPH, c, rows(j)])
                    for q in range(2):
                        filled(last[q], ("xo1", h, q))
                elif kind == "xp1":
                    b = claim(("xp1", h))
                    for q in range(2):
                        await_read(pe, ("xo1", h, q))
                    for c in range(XC):
                        last = mm(b[:, 0:P], q1T[:, c, tok(h)], piece("l1", "xo")[:, P * c:P * c + P],
                                  start=(c == 0), stop=(c == XC - 1))
                    filled(last, ("xp1", h))
                elif kind == "experts":
                    experts()

        @block.scalar
        def _(act):
            link = chain(act, act_step)

            def evac(name, dst, src=None, func=ACT.Copy, **kw):
                await_bank(act, name)
                read_out(act.activation(dst, bank(name) if src is None else src, func, **kw), name)

            def values(name, h):
                await_bank(act, name)
                src = bank(name).rearrange("p (n d) -> p n d", d=HD)
                dst = vx[:, 8 * h:8 * h + 8, :, :].rearrange("p b c d -> p (b c) d")
                act.activation(dst[rows(0), :, 0:HD], src[rows(0), :, :], ACT.Copy)
                read_out(act.activation(dst[rows(1), :, HD + 1:2 * HD + 1], src[rows(1), :, :], ACT.Copy), name)

            def experts():
                def pair_of_experts(i, first):
                    for u in range(4):
                        n, ub = u // 2, u % 2
                        fresh = first and u < 2
                        for c in range(2):
                            act.wait_ge(z_full, 2 * u + c + 1 if first else i * 8 + (2 * u + c + 1))
                            if not fresh:
                                act.wait_ge(hid_ready, 2 * (u - 2) + c + 1 if first else i * 8 + (2 * (u - 2) + c + 1))
                            act.activation(relu[:, ub, c, :], PS[:, 2 * ub + c, :], ACT.Relu, bias=bias1[:, n, c:c + 1]).then_inc(relu_ready, 1)
                        if not first:
                            act.wait_ge(acc_done, i * 4 + (u - 3))
                        for c in range(2):
                            act.wait_ge(hid_ready, 2 * u + c + 1 if first else i * 8 + (2 * u + c + 1))
                            act.activation(hr[:, u, c, 0, :], hid[:, ub, c, :], ACT.Copy).then_inc(high_ready, 1)

                pair_of_experts(0, True)
                with act.Fori(1, E1 // 2) as i:
                    pair_of_experts(i, False)
                await_bank(act, ("experts",))
                act.activation(accT[:, half(0)], PS[:, 6, :], ACT.Copy)
                read_out(act.activation(accT[:, half(1)], PS[:, 7, :], ACT.Copy), ("experts",))

            for step in order:
                kind, h = step[0], step[-1]
                if kind == "fold":
                    act.wait_ge(pack_loaded["l0"], 16)
                    act.activation(identb[:], piece("l0", "ident"), ACT.Copy).then_inc(identb_set, 1)
                elif kind == "turn":
                    name = ("lnT", step[1], h)
                    if step[1] == 6:
                        await_bank(act, name)
                        act.activation(xr[:, 0, half(h)], bank(name), ACT.Copy)
                    evac(name, xnT[:, half(h)])
                elif kind == "qk0":
                    for n, name in enumerate(("q0", "k0")):
                        await_bank(act, (name, h))
                        act.activation(relu[:, h, n, :], bank((name, h)), ACT.Square).then_inc(squares_ready, 1)
                        read_out(act.activation(wide[:, h, n, :], bank((name, h)), ACT.Copy), (name, h))
                elif kind == "rms0":
                    act.wait_ge(squares_summed, nth(*step))
                    act.activation(ssum[:, h, :, :], ssum[:, h, :, :], ACT.Sqrt, scale=1.0 / HD,
                                   bias=piece("l0", "eps")).then_inc(roots_ready, 1)
                elif kind == "qkT0":
                    evac(("qT0", h), qT[:, half(h)], scale=piece("l0", "qnw"))
                    evac(("kT0", h), kf[:, half(h)], scale=piece("l0", "knw"))
                elif kind == "v":
                    if step[1] == 0:
                        act.wait_ge(fill_set, 1)
                    values(("v%d" % step[1], h), h)
                elif kind == "exp":
                    act.wait_ge(shifted, nth("scores", step[1], h))
                    act.activation(sc[:, slot(h), :], sc[:, slot(h), :], ACT.Exp).then_inc(probs_ready, 1)
                elif kind == "weights":
                    if before(h) is not None:
                        await_bank(act, ("o", step[1], before(h)))
                    for g in range(2):
                        evac(("t", step[1], h, g), pT[:, h // TPH, 4 * g:4 * g + 4, :])
                elif kind == "ck0":
                    act.wait_ge(pack_loaded["ctx"], 16)
                    evac(step, k0T[:, half(h)], func=ACT.Identity, bias=piece("ctx", "bk0"))
                elif kind == "ck1":
                    evac(step, k1T[:, step[1], half(h)])
                elif kind == "cv0":
                    evac(step, v0[:, 2 * h:2 * h + 2, :, :])
                elif kind == "cv1":
                    evac(step, v1[:, 2 * h:2 * h + 2, :, :])
                elif kind == "xq0":
                    evac(step, rawq[:, half(h)], func=ACT.Identity, bias=piece("ctx", "bq0"))
                elif kind == "xs0":
                    await_read(act, ("xs0", h))
                    act.activation(xs[:, th(h), :], xs[:, th(h), :], ACT.Exp).then_inc(xprobs0, 1)
                elif kind == "xo0":
                    evac(("xt0", h), pT[:, h, 0:2, :], src=bank(("xt0", h))[:, 0:2 * P])
                elif kind == "enc":
                    if nth(*step) == 1:
                        act.wait_ge(pack_loaded["f0"], 16)
                        act.activation(halfb[:, 0:2], piece("f0", "benc"), ACT.Copy, scale=0.5)
                        link(act.activation(halfb[:, 2:4], piece("f0", "bc2s"), ACT.Copy, scale=0.5))
                    for c in range(2):
                        evac(("enc", h, c), spk[:, h, c, :], func=ACT.Tanh, scale=0.5, bias=halfb[:, c:c + 1])
                elif kind == "s2c":
                    evac(step, contT[:, half(h)], func=ACT.Identity, bias=piece("f0", "bs2c"))
                elif kind == "route":
                    act.wait_ge(logits_shifted, nth(*step))
                    n = (E0, E1)[step[1]]
                    act.activation(rl[:, th(h), 0:n], rl[:, th(h), 0:n], ACT.Exp).then_inc(exp_ready, 1)
                elif kind == "gates":
                    name = ("g%d" % step[1], h)
                    if step[1] == 0:
                        act.wait_ge(fill_set, 1)
                    evac(name, g3T[0:GW, half(h)], src=bank(name).bitcast(bf16)[0:GW, 0:HT])
                elif kind == "up0":
                    g, p = step[1], step[2]
                    for q in range(2):
                        if p > 0:
                            await_read(act, ("G0", g, p - 1, q))
                        evac(("z0", g, p, q), relu[:, g, q, :], func=ACT.Relu, bias=piece("f0", "b1")[:, 2 * p + q:2 * p + q + 1])
                elif kind == "down0" and h == E0 // 2 - 1:
                    evac(("y0", step[1]), accT[:, half(step[1])])
                elif kind == "c2s":
                    for c in range(2):
                        evac(("c2s", h, c), relu[:, h, c, :], func=ACT.Tanh, scale=0.5, bias=halfb[:, 2 + c:3 + c])
                elif kind == "qk1":
                    evac(("q1", h), qT[:, half(h)])
                    evac(("k1", h), kf[:, half(h)])
                elif kind == "proj1":
                    evac(("oT", h), rawq[:, half(h)])
                elif kind == "xq1":
                    for c in range(XC):
                        evac(("xq1", h, c), q1T[:, c, half(h)])
                elif kind == "xexp1":
                    await_read(act, ("xs1", h))
                    act.activation(sc[:, slot(h), 0:XH * S], sc[:, slot(h), 0:XH * S], ACT.Exp,
                                   scale=float(XD) ** -0.5).then_inc(xprobs1, 1)
                elif kind == "xw1":
                    if before(h) is not None:
                        await_bank(act, ("xo1", before(h), 1))
                    evac(("xt1", h), pT[:, h // TPH, 0:XC, :])
                elif kind == "xo1":
                    for q in range(2):
                        name = ("xo1", h, q)
                        evac(name, q1T[rows(q), :, tok(h)], src=bank(name)[rows(q), :].rearrange("p (c k) -> p c k", c=XC))
                elif kind == "experts":
                    experts()

        @block.vector
        def _(dve):
            link = chain(dve, dve_step)

            def stats_of(k, h):
                src = xn if k == 3 else x
                for t in tiles(h):
                    last = dve.bn_stats(stats[:, t, :], src[:, t, :])
                link(last)
                for t in tiles(h):
                    last = dve.bn_aggr(mv[:, t, :], stats[:, t, :])
                last.then_inc(stats_ready, 1)

            def normalise(k, h, dst):
                dve.wait_ge(rstd_ready, nth("stats", k, h))
                src = xn if k == 3 else x
                for t in tiles(h):
                    last = dve.tensor_scalar(dst[:, t, :], src[:, t, :], mv[:, t, 0:1], rstd[:, t:t + 1], ALU.subtract, ALU.mult)
                return last

            def scores(layer, t):
                name = ("s", layer, t)
                await_bank(dve, name)
                s = sc[:, slot(t), :]
                read_out(dve.scalar_tensor_tensor(s.rearrange("p (i n) -> p i n", i=NG), PS[:, 0:NG, 0:GRP * S],
                                                  float(HD) ** -0.5, masks[:, layer, :].rearrange("p (i n) -> p i n", i=NG),
                                                  ALU.mult, ALU.add), name)
                await_read(dve, name)
                dve.reduce_max(top[:, slot(t), :], s.rearrange("p (h k) -> p h k", h=NH), AX.X).then_inc(top_ready, 1)

            def heads(layer, t):
                name = ("o", layer, t)
                await_bank(dve, name)
                o = bank(name)[:, 0:NH * (HD + 1)].rearrange("p (h d) -> p h d", h=NH)
                link(dve.reciprocal(orec[:, slot(t), :], o[:, :, HD]))
                dst = oh[:, t, :].rearrange("p (h d) -> p h d", h=NH)
                read_out(dve.tensor_tensor(dst, o[:, :, 0:HD], bc(orec[:, slot(t), :].unsqueeze(2), [P, NH, HD]), ALU.mult), name)
                if layer == 0:
                    await_read(dve, name)
                    last = dve.tensor_tensor(x[:, t, :], x[:, t, :], oh[:, t, :], ALU.add)
                    if t % TPH == TPH - 1:
                        link(last)

            def route(layer, h):
                n = (E0, E1)[layer]
                name = ("rt%d" % layer, h)
                await_bank(dve, name)
                r, s4 = rl[:, th(h), 0:n], rsum[:, th(h)]
                src = bank(name)[:, 0:TPH * n].rearrange("p (t e) -> p t e", e=n)
                if layer == 0:
                    read_out(dve.tensor_tensor(r, src, bc(piece("f0", "br").unsqueeze(1), [P, TPH, n]), ALU.add), name)
                else:
                    read_out(dve.tensor_copy(r, src), name)
                await_read(dve, name)
                link(dve.reduce_max(s4, r, AX.X))
                dve.tensor_tensor(r, r, bc(s4.unsqueeze(2), [P, TPH, n]), ALU.subtract).then_inc(logits_shifted, 1)

            def pick_experts(layer, h):
                n, k = ((E0, K0), (E1, K1))[layer]
                r, s4 = rl[:, th(h), 0:n], rsum[:, th(h)]
                dve.wait_ge(exp_ready, nth("route", layer, h))
                link(dve.reduce_sum(s4, r, AX.X))
                link(dve.reciprocal(s4, s4))
                link(dve.tensor_tensor(r, r, bc(s4.unsqueeze(2), [P, TPH, n]), ALU.mult))
                for t in tiles(h):
                    last = dve.max(r8[:, t, :], rl[:, t, 0:n])
                link(last)
                for t in tiles(h):
                    last = dve.max_index(i8[:, t, :], r8[:, t, :], rl[:, t, 0:n])
                link(last)
                link(dve.tensor_copy(i8f[:, th(h), :], i8[:, th(h), :]))
                iota = piece("l0", "iota")
                for t in tiles(h):
                    last = dve.tensor_tensor(eq[:, t, 0:k, 0:n], bc(iota[:, 0:n].unsqueeze(1), [P, k, n]),
                                             bc(i8f[:, t, 0:k].unsqueeze(2), [P, k, n]), ALU.is_equal)
                link(last)
                link(dve.reduce_sum(pick[:, th(h), 0:n], eq[:, th(h), 0:k, 0:n].rearrange("p t k e -> p t e k"), AX.X))
                link(dve.tensor_tensor(r, r, pick[:, th(h), 0:n], ALU.mult))
                link(dve.reduce_sum(s4, r, AX.X))
                if layer == 1:
                    link(dve.tensor_scalar(s4, s4, 1e-12, None, ALU.max))
                link(dve.reciprocal(s4, s4))
                link(dve.tensor_tensor(r, r, bc(s4.unsqueeze(2), [P, TPH, n]), ALU.mult))
                if nth("pick", layer, h) == 1:
                    dve.wait_ge(fill_set, 1)
                link(dve.tensor_copy(ghi[:, th(h), 0:n], r))
                link(dve.tensor_tensor(r, r, ghi[:, th(h), 0:n], ALU.subtract))
                link(dve.tensor_copy(ghi[:, th(h), 32:32 + n], r))
                link(dve.tensor_tensor(r, r, ghi[:, th(h), 32:32 + n], ALU.subtract))
                dve.tensor_copy(ghi[:, th(h), 64:64 + n], r).then_inc(gates_ready, 1)

            def bias_parts(layer, src, n):
                link(dve.tensor_copy(b2s[:, layer, 0, 0:n], src))
                link(dve.tensor_tensor(b2r[:, 0:n], src, b2s[:, layer, 0, 0:n], ALU.subtract))
                link(dve.tensor_copy(b2s[:, layer, 1, 0:n], b2r[:, 0:n]))
                link(dve.tensor_tensor(b2r[:, 0:n], b2r[:, 0:n], b2s[:, layer, 1, 0:n], ALU.subtract))
                dve.tensor_copy(b2s[:, layer, 2, 0:n], b2r[:, 0:n]).then_inc(b2_split, 1)

            def experts():
                def pair_of_experts(i, first):
                    for u in range(4):
                        ub = u % 2
                        fresh = first and u < 2
                        dve.wait_ge(G_full, u + 1 if first else i * 4 + (u + 1))
                        for c in range(2):
                            if not fresh:
                                dve.wait_ge(high_ready, 2 * (u - 2) + c + 1 if first else i * 8 + (2 * (u - 2) + c + 1))
                            dve.wait_ge(relu_ready, 2 * u + c + 1 if first else i * 8 + (2 * u + c + 1))
                            dve.tensor_tensor(hid[:, ub, c, :], relu[:, ub, c, :], PS[:, 4 + ub, :], ALU.mult).then_inc(hid_ready, 1)
                        for c in range(2):
                            dve.wait_ge(high_ready, 2 * u + c + 1 if first else i * 8 + (2 * u + c + 1))
                            dve.tensor_tensor(hr[:, u, c, 1, :], hid[:, ub, c, :], hr[:, u, c, 0, :].bitcast(f32), ALU.subtract).then_inc(low_ready, 1)

                pair_of_experts(0, True)
                with dve.Fori(1, E1 // 2) as i:
                    pair_of_experts(i, False)
                for h in range(HALVES):
                    name = ("fin", h)
                    await_bank(dve, name)
                    dve.tensor_tensor(x[:, th(h), :], x[:, th(h), :], by_tile(bank(name)), ALU.add).then_inc(out_ready, 1)

            d4 = [P, TPH, D]
            for step in order:
                kind, h = step[0], step[-1]
                if kind == "fold":
                    dve.wait_ge(pack_loaded["l0"], 16)
                    for n, w in enumerate(("dq", "dk", "dm", "c", "v")):
                        name = ("fold", w)
                        await_bank(dve, name)
                        if w == "c":
                            read_out(dve.tensor_copy(fold_c[:], bank(name)[0:HD, 0:P]), name)
                        else:
                            read_out(dve.tensor_tensor(fold[:, min(n, 3), :], bank(name)[:, 0:P], piece("l0", "blocks"), ALU.mult), name)
                elif kind == "stats":
                    if step[1] == 0:
                        dve.wait_ge(x_loaded, 16 * h + 16)
                    stats_of(step[1], h)
                elif kind == "turn":
                    normalise(step[1], h, xn).then_inc(xn_ready, 1)
                elif kind == "rms0":
                    dve.wait_ge(squares_ready, 2 * nth("qk0", h))
                    dve.reduce_sum(ssum[:, h, :, :].rearrange("p n s -> p (n s)"),
                                   relu[:, h, :, :].rearrange("p n (s d) -> p (n s) d", d=HD), AX.X).then_inc(squares_summed, 1)
                    dve.wait_ge(roots_ready, nth(*step))
                    link(dve.reciprocal(ssum[:, h, :, :], ssum[:, h, :, :]))
                    await_read(dve, ("k0", h))
                    for n in range(2):
                        w = wide[:, h, n, :].rearrange("p (s d) -> p s d", d=HD)
                        dve.tensor_tensor(w, w, bc(ssum[:, h, n, :].unsqueeze(2), [P, TPH * NH, HD]), ALU.mult).then_inc(qk_normed, 1)
                elif kind == "expand":
                    if step[1] == 0:
                        await_read(dve, ("kT0", h))
                        await_bank(dve, ("m0", h))
                        read_out(dve.tensor_tensor(kf[:, half(h)], kf[:, half(h)], bank(("m0", h)), ALU.add), ("m0", h))
                        await_read(dve, ("m0", h))
                    else:
                        await_read(dve, ("k1", h))
                    for j in range(GRP):
                        last = dve.tensor_scalar(kexp[:, j, half(h)], kf[:, half(h)], piece("l0", "heads")[:, j:j + 1], None, ALU.mult)
                    last.then_inc(k_ready, 1)
                elif kind == "scores":
                    dve.wait_ge(masks_loaded, 16)
                    scores(step[1], h)
                elif kind == "values":
                    heads(step[1], h)
                elif kind == "xs0":
                    name = ("xs0", h)
                    await_bank(dve, name)
                    s = bank(name)[:, 0:TPH * S].rearrange("p (t k) -> p t k", k=S)
                    link(dve.reduce_max(xtop[:, th(h)], s, AX.X))
                    read_out(dve.tensor_tensor(xs[:, th(h), :], s, bc(xtop[:, th(h)].unsqueeze(2), [P, TPH, S]), ALU.subtract), name)
                    link(dve.tensor_tensor(x[:, th(h), :], x[:, th(h), :], bc(piece("ctx", "bv0").unsqueeze(1), d4), ALU.add))
                elif kind == "xo0":
                    dve.wait_ge(xprobs0, nth("xs0", h))
                    link(dve.reduce_sum(xrec[:, th(h)], xs[:, th(h), :], AX.X))
                    link(dve.reciprocal(xrec[:, th(h)], xrec[:, th(h)]))
                    for u in range(2):
                        name = ("xo0", h, u)
                        await_bank(dve, name)
                        for a in range(2):
                            t = TPH * h + 2 * a + u
                            last = dve.scalar_tensor_tensor(x[:, t, :], bank(name)[:, P * a:P * a + P], xrec[:, t:t + 1], x[:, t, :], ALU.mult, ALU.add)
                        read_out(last, name)
                    await_read(dve, ("xo0", h, 1))
                elif kind == "enc":
                    for c in range(2):
                        await_read(dve, ("enc", h, c))
                        dve.tensor_scalar(spk[:, h, c, :], spk[:, h, c, :], 0.5, 0.5, ALU.mult, ALU.add).then_inc(spikes_in, 1)
                elif kind == "s2c":
                    if nth(*step) == 1:
                        bias_parts(0, piece("f0", "b2"), M0)
                elif kind == "route":
                    if step[1] == 1:
                        await_read(dve, ("lnT", 6, h))
                        dve.tensor_tensor(xr[:, 1, half(h)], xnT[:, half(h)], xr[:, 0, half(h)].bitcast(f32), ALU.subtract).then_inc(x_split, 1)
                    route(step[1], h)
                elif kind == "pick":
                    pick_experts(step[1], h)
                elif kind == "up0":
                    g, p = step[1], step[2]
                    for q in range(2):
                        await_read(dve, ("z0", g, p, q))
                        await_bank(dve, ("G0", g, p, q))
                        if p > 0:
                            dve.wait_ge(hid0_used, 2 * nth("down0", g, p - 1) - 1 + q)
                        read_out(dve.tensor_tensor(wide[:, g, q, :], relu[:, g, q, :], bank(("G0", g, p, q)), ALU.mult), ("G0", g, p, q))
                elif kind == "c2s":
                    for c in range(2):
                        await_read(dve, ("c2s", h, c))
                        dve.tensor_scalar(relu[:, h, c, :], relu[:, h, c, :], 0.5, 0.5, ALU.mult, ALU.add).then_inc(spikes_out, 1)
                elif kind == "dec":
                    await_bank(dve, step)
                    read_out(dve.tensor_tensor(xn[:, th(h), :], by_tile(bank(step)), bc(piece("f0", "bdec").unsqueeze(1), d4), ALU.add), step)
                    await_read(dve, step)
                elif kind == "inner":
                    link(normalise(3, h, oh))
                    o = oh[:, th(h), :]
                    link(dve.tensor_tensor(o, o, bc(piece("f0", "lng").unsqueeze(1), d4), ALU.mult))
                    link(dve.tensor_tensor(o, o, bc(piece("f0", "lnb").unsqueeze(1), d4), ALU.add))
                    link(dve.tensor_tensor(x[:, th(h), :], x[:, th(h), :], o, ALU.add))
                elif kind == "qk1":
                    if nth(*step) == 1:
                        dve.wait_ge(pack_loaded["l1"], 16)
                        bias_parts(1, piece("l1", "fb2"), D)
                elif kind == "proj1":
                    name = ("pr", h)
                    await_bank(dve, name)
                    read_out(dve.tensor_tensor(x[:, th(h), :], x[:, th(h), :], by_tile(bank(name)), ALU.add), name)
                    await_read(dve, name)
                elif kind == "xs1":
                    s = PS[:, plan[("xs1", h)][0]:plan[("xs1", h)][0] + 2, 0:XC * S].rearrange("p q (c k) -> p q c k", c=XC)
                    await_bank(dve, step)
                    tp = top[:, slot(h), 0:XH].rearrange("p (q c) -> p q c", q=2)
                    link(dve.reduce_max(tp, s, AX.X))
                    w = sc[:, slot(h), 0:XH * S].rearrange("p (c q k) -> p q c k", q=2, k=S)
                    for q in range(2):
                        last = dve.tensor_tensor(w[:, q, :, :], s[:, q, :, :], bc(tp[:, q, :].unsqueeze(2), [P, XC, S]), ALU.subtract)
                    read_out(last, step)
                elif kind == "xexp1":
                    dve.wait_ge(xprobs1, nth(*step))
                    e = sc[:, slot(h), 0:XH * S].rearrange("p (h k) -> p h k", h=XH)
                    link(dve.reduce_sum(orec[:, slot(h), 0:XH], e, AX.X))
                    dve.reciprocal(orec[:, slot(h), 0:XH], orec[:, slot(h), 0:XH]).then_inc(xrec_ready, 1)
                elif kind == "xp1":
                    await_bank(dve, step)
                    link(dve.tensor_tensor(x[:, h, :], x[:, h, :], piece("l1", "xbo"), ALU.add))
                    read_out(dve.tensor_tensor(x[:, h, :], x[:, h, :], bank(step)[:, 0:P], ALU.add), step)
                    if h % TPH == TPH - 1:
                        await_read(dve, step)
                elif kind == "experts":
                    experts()


def _tile_cols(a, n):
    return np.tile(a, (1, n))


def _host_pieces(v):
    heads = np.arange(P) // HD
    rep = P // HD
    w2 = v["L0_ffn_W2"]
    b2 = np.zeros((GW, M0), np.float32)
    fb2 = np.zeros((GW, D), np.float32)
    for n in range(3):
        b2[32 * n:32 * n + E0] = v["L0_ffn_b2"]
        fb2[32 * n:32 * n + E1] = v["L1_ffn_b2"]

    def row(a):
        return np.broadcast_to(a[None, :], (P, a.shape[0]))

    def col(a):
        return a.reshape(-1, P).T

    def cols2(w):
        return w.reshape(-1, P, w.shape[1]).transpose(1, 0, 2).reshape(P, -1)

    s2c = v["L0_ffn_W_s2c"].reshape(2, P, M0).transpose(1, 0, 2)
    return {
        "ident": np.eye(P, dtype=np.float32),
        "blocks": (heads[:, None] == heads[None, :]).astype(np.float32),
        "heads": (heads[:, None] % GRP == np.arange(GRP)[None, :]).astype(np.float32),
        "eps": np.full((P, 1), RMS_EPS, np.float32),
        "qnw": np.tile(v["L0_attn_q_norm_w"], rep)[:, None], "knw": np.tile(v["L0_attn_k_norm_w"], rep)[:, None],
        "dq": _tile_cols(v["L0_attn_W_DQ"], rep), "uqT": _tile_cols(v["L0_attn_W_UQ"].T, rep),
        "dkv": _tile_cols(v["L0_attn_W_DKV"], rep), "ukT": _tile_cols(v["L0_attn_W_UKV"][:HD].T, rep),
        "uvT": v["L0_attn_W_UKV"][HD:].T, "kr": _tile_cols(v["L0_attn_W_KR"], rep),
        "qr": _tile_cols(v["L0_attn_W_QR"], rep), "oT": _tile_cols(v["L0_attn_W_O"].T, rep),
        "ctxT": v["ctx_768"].reshape(TOK, DC).T, "wk0": v["L0_xattn_Wk"], "wv0": v["L0_xattn_Wv"],
        "bk0": col(v["L0_xattn_bk"]), "bv0": row(v["L0_xattn_bv"]), "wq0": v["L0_xattn_Wq"], "bq0": col(v["L0_xattn_bq"]),
        "xk": v["L1_xattn_Wk"], "xv": v["L1_xattn_Wv"],
        "enc": v["L0_ffn_W_enc"], "benc": col(v["L0_ffn_b_enc"]),
        "s2c": np.concatenate([s2c, s2c], axis=2).reshape(P, 2 * P),
        "bs2c": np.tile(v["L0_ffn_b_s2c"], 2)[:, None], "wr": v["L0_ffn_Wr"], "br": row(v["L0_ffn_br"]),
        "iota": row(np.arange(E1, dtype=np.float32)),
        "w1": v["L0_ffn_W1"].reshape(E0 // 2, P, F0H).transpose(1, 0, 2).reshape(P, -1),
        "b1": v["L0_ffn_b1"].T, "w2": w2.transpose(1, 0, 2).reshape(P, -1), "b2": b2,
        "c2s": np.concatenate([v["L0_ffn_W_c2s"]] * 2, axis=0), "bc2s": col(v["L0_ffn_b_c2s"]),
        "dec": cols2(v["L0_ffn_W_dec"]), "bdec": row(v["L0_ffn_b_dec"]), "lng": row(v["L0_ffn_ln_g"]), "lnb": row(v["L0_ffn_ln_b"]),
        "qkv": v["L1_attn_w_qkv"], "proj": v["L1_attn_w_proj"], "xq": v["L1_xattn_Wq"], "xo": cols2(v["L1_xattn_Wo"]),
        "xbo": row(v["L1_xattn_bo"]), "gate": v["L1_ffn_gate"],
        "fb2": fb2,
    }


def _expert_rows(w1, w2, b1):
    w2 = w2.reshape(E1, 2, P, D).transpose(0, 2, 1, 3).reshape(E1, P, 2 * D)
    return np.ascontiguousarray(np.concatenate([w1, w2, b1.reshape(E1, 2, P).transpose(0, 2, 1)], axis=2))


def _masks():
    q = (np.arange(P) % S)[:, None, None]
    k = np.arange(S)[None, None, :]
    first = 2.0 ** (-(2.0 ** -(np.log2(NH) - 3)))
    slopes = np.array([first * first ** n for n in range(NH)], np.float32)[None, :, None]
    keep = np.broadcast_to(k <= q, (P, NH, S))
    causal = np.where(keep, np.float32(0), np.float32(MASKED))
    alibi = np.where(keep, slopes * k.astype(np.float32), np.float32(MASKED))
    return np.stack([causal, alibi], axis=1).astype(np.float32).reshape(P, 2, NH * S)


def kernel(**inputs):
    import concourse.bacc as bacc
    from concourse import mybir
    from concourse.bass_utils import run_bass_kernel_spmd

    v = {k: np.asarray(a) for k, a in inputs.items()}
    pieces = _host_pieces(v)
    arrays = {"x": np.ascontiguousarray(v["x"].reshape(TOK, D)), "masks": _masks(),
              "experts": _expert_rows(v["L1_ffn_W1"], v["L1_ffn_W2"], v["L1_ffn_b1"])}
    for k, parts in PACKS.items():
        packed = np.zeros((P, WIDTH[k]), np.float32)
        for name, rows, cols in parts:
            r, at, c = LAYOUT[k][name]
            packed[:r, at:at + c] = pieces[name]
        arrays[k] = packed
    nc = bacc.Bacc("TRN2", target_bir_lowering=False, num_devices=1)
    dram = {k: nc.dram_tensor(f"in_{k}", a.shape, mybir.dt.float32, kind="ExternalInput").ap() for k, a in arrays.items()}
    out = nc.dram_tensor("out", (TOK, D), mybir.dt.float32, kind="ExternalOutput").ap()
    build(nc, dram, out)
    r = run_bass_kernel_spmd(nc, [{f"in_{k}": a for k, a in arrays.items()}], core_ids=[0])
    return r.results[0]["out"].reshape(B, S, D)
```

```python
import numpy as np

B, S, D, DC = 16, 64, 128, 96
P = 128
TOK = B * S
TILES = TOK // P
HALVES = 2
TPH = TILES // HALVES
HT = TOK // HALVES
PAIR = P // S
LN_EPS = 1e-5
RMS_EPS = 1.1920929e-07
NH, HD = 16, 8
GRP = 4
NG = NH // GRP
XH, XD = 8, 64
XC = XH // 2
E0, K0, M0, F0H = 8, 2, 64, 128
E1, K1, F1H = 16, 3, 256
GW = 96
EXPERT = F1H + 2 * D + 2
MASKED = -1e30
RESIDUAL_BIAS = {1: ("ctx", "bv0"), 2: ("f0", "lnb"), 5: ("l1", "xbo")}
PARTS = ((0, 0), (0, 1), (1, 0))


def _pack_layout(parts):
    at, out = 0, {}
    for name, rows, cols in parts:
        out[name] = (rows, at, cols)
        at += cols
    return out, at


PACKS = {
    "l0": [("ident", P, P), ("iota", P, E1), ("blocks", P, P), ("heads", P, GRP), ("eps", P, 1), ("qnw", P, 1), ("knw", P, 1),
           ("dq", 64, P), ("uqT", 64, P), ("dkv", P, P), ("ukT", P, P), ("uvT", P, HD), ("kr", 64, P),
           ("qr", 64, P), ("oT", HD, P)],
    "ctx": [("ctxT", DC, TOK), ("wk0", DC, P), ("wv0", DC, P), ("bk0", P, 1), ("bv0", P, P), ("wq0", P, P),
            ("bq0", P, 1), ("xk", DC, XH * XD), ("xv", DC, XH * XD)],
    "f0": [("enc", P, 256), ("benc", P, 2), ("s2c", P, 2 * P), ("bs2c", P, 1), ("wr", M0, E0), ("br", P, E0),
           ("b1", P, E0), ("w2", P, E0 * M0), ("b2", GW, M0),
           ("c2s", P, 256), ("bc2s", P, 2), ("dec", P, 2 * P), ("bdec", P, P), ("lng", P, P), ("lnb", P, P)],
    "w0": [("w1", P, E0 * F0H)],
    "l1": [("qkv", P, 3 * P), ("proj", P, P), ("xq", P, XH * XD), ("xo", P, XC * P), ("xbo", P, P),
           ("gate", P, E1), ("fb2", GW, P)],
}
LAYOUT = {k: _pack_layout(v)[0] for k, v in PACKS.items()}
WIDTH = {k: _pack_layout(v)[1] for k, v in PACKS.items()}


ORDER = """
    stats.0.0 stats.0.1 norm.0.0 norm.0.1 fold turn.0.0 qk0.0 turn.0.1 rms0.0 qk0.1 qkT0.0 warm.2 rms0.1
    qkT0.1 expand.0.0 expand.0.1 v.0.0 scores.0.0 v.0.1 warm.8 scores.0.4 scores.0.5 exp.0.4 scores.0.1
    exp.0.0 weights.0.0 weights.0.4 values.0.0 ck1.0.0 ck0.1 exp.0.1 scores.0.2 cv0.0 ck1.0.1 weights.0.1
    values.0.4 exp.0.5 ck1.2.0 cv0.1 ck1.1.1 ck1.1.0 values.0.1 warm.8 scores.0.6 weights.0.5 ck0.0
    scores.0.3 exp.0.2 weights.0.2 values.0.5 exp.0.6 scores.0.7 weights.0.6 ck1.2.1 values.0.6 values.0.2
    warm.2 exp.0.3 exp.0.7 weights.0.3 ck1.3.0 weights.0.7 warm.4 values.0.3 stats.1.0 warm.1 values.0.7
    stats.1.1 warm.11 ck1.3.1 norm.1.0 turn.1.0 xq0.0 norm.1.1 turn.1.1 xs0.0 xq0.1 xt0.0 xs0.1 warm.4 xo0.0
    xt0.1 warm.4 warm.3 split0 stats.2.0 xo0.1 warm.6 norm.2.0 stats.2.1 turn.2.0 enc.0 norm.2.1 s2c.0
    turn.2.1 enc.1 route.0.0 pick.0.0.0 s2c.1 route.0.1 pick.0.1.1 gates.0.0 up0.0.0 down0.0.0 gates.0.1
    up0.0.1 up0.1.0 down0.0.1 up0.0.2 up0.1.1 down0.0.2 down0.1.0 up0.1.2 down0.1.1 up0.0.3 down0.1.2
    down0.0.3 up0.1.3 c2s.0 down0.1.3 dec.0 stats.3.0 c2s.1 inner.3.0 warm.3 stats.4.0 dec.1 stats.3.1
    inner.3.1 warm.4 norm.4.0 stats.4.1 turn.4.0 qk1.0 norm.4.1 turn.4.1 qk1.1 expand.1.0 scores.1.0
    expand.1.1 warm.16 exp.1.0 scores.1.1 v.1.0 v.1.1 scores.1.4 cv1.1 weights.1.0 cv1.0 scores.1.5 warm.1
    values.1.0 scores.1.2 exp.1.4 weights.1.4 cv1.4 exp.1.1 warm.8 values.1.4 scores.1.6 exp.1.5 weights.1.1
    cv1.5 weights.1.5 values.1.1 scores.1.3 values.1.5 exp.1.6 cv1.3 warm.1 scores.1.7 exp.1.2 cv1.7 cv1.2
    weights.1.6 weights.1.2 values.1.2 values.1.6 exp.1.3 exp.1.7 weights.1.3 weights.1.7 warm.1 values.1.3
    oT.0 values.1.7 pr.0 stats.5.0 oT.1 pr.1 warm.1 stats.5.1 norm.5.0 cv1.6 turn.5.0 norm.5.1 turn.5.1
    xq1.0 xs1.0 xexp1.0 xq1.1 xs1.4 xw1.0 xexp1.4 xs1.1 xo1.0 xs1.5 xw1.4 xp1.0 xexp1.1 xs1.2 warm.1 xo1.4
    xw1.1 xp1.4 xexp1.5 xo1.1 xs1.6 xw1.5 xp1.1 xexp1.2 xo1.5 xs1.3 warm.3 xw1.2 xp1.5 xexp1.6 xo1.2 xs1.7
    xp1.2 xexp1.3 xw1.6 xo1.6 xw1.3 xp1.6 xexp1.7 xo1.3 xw1.7 xp1.3 stats.6.0 xo1.7 xp1.7 warm.7 stats.6.1
    norm.6.0 warm.8 norm.6.1 warm.1 turn.6.0 turn.6.1 route.1.0 route.1.1 pick.1.0.1 hidden warm.8 gates.1.1
    gates.1.0 experts
"""


def schedule():
    return [tuple(int(a) if a.isdigit() else a for a in word.split(".")) for word in ORDER.split()]


def bank_plan(order):
    held, counts, plan, turn, kept = {}, {}, {}, list(range(4, 8)), set()

    def lend(name, *banks):
        before = []
        for b in banks:
            if b in held and held[b] not in before:
                before.append(held[b])
        counts[banks[0]] = counts.get(banks[0], 0) + 1
        for b in banks:
            held[b] = (banks[0], counts[banks[0]])
        plan[name] = (banks[0], counts[banks[0]], before, banks)

    def any_bank(name, keep=False):
        b = next(b for b in turn if b not in kept)
        turn.remove(b)
        turn.append(b)
        if keep:
            kept.add(b)
        lend(name, b)
        return b

    n = 0
    for at, step in enumerate(order):
        kind = step[0]
        h = step[-1]
        if kind == "warm":
            b = next(b for b in turn if b not in kept)
            plan[("warm", at)] = (b, None, [held[b]] if b in held else [], (b,))
        elif kind == "fold":
            for i, w in enumerate(("dq", "dk", "dm", "c")):
                lend(("fold", w), i)
            lend(("fold", "v"), 4)
        elif kind == "turn":
            any_bank(("lnT", step[1], h))
        elif kind in ("qk0", "qk1"):
            any_bank(("q" + kind[2], h))
            any_bank(("k" + kind[2], h))
        elif kind == "qkT0":
            for w in ("qT0", "kT0", "m0"):
                any_bank((w, h))
        elif kind == "v":
            any_bank(("v%d" % step[1], h))
        elif kind == "scores":
            lend(("s", step[1], h), 0, 1, 2, 3)
        elif kind == "weights":
            for g in range(2):
                any_bank(("t", step[1], h, g))
        elif kind == "values":
            any_bank(("o", step[1], h))
        elif kind in ("ck0", "cv0", "ck1", "cv1"):
            any_bank(step)
        elif kind in ("xq0", "xs0", "s2c", "dec", "xp1"):
            any_bank(step)
        elif kind == "xt0":
            any_bank(step)
        elif kind == "xo0":
            for u in range(2):
                any_bank(("xo0", h, u))
        elif kind in ("enc", "c2s"):
            for c in range(2):
                any_bank((kind, h, c))
        elif kind == "route":
            any_bank(("rt%d" % step[1], h))
        elif kind == "gates":
            any_bank(("g%d" % step[1], h))
        elif kind == "up0":
            if h == 0:
                any_bank(("y0", step[1]), keep=True)
            for q in range(2):
                lend(("z0", step[1], h, q), n % 4)
                lend(("G0", step[1], h, q), (n + 1) % 4)
                n += 2
        elif kind == "down0" and h == E0 // 2 - 1:
            kept.discard(plan[("y0", step[1])][0])
        elif kind in ("oT", "pr"):
            any_bank(step)
        elif kind == "xq1":
            for c in range(XC):
                any_bank(("xq1", h, c))
        elif kind == "xs1":
            lend(("xs1", h), 2 * (h // TPH), 2 * (h // TPH) + 1)
        elif kind == "xw1":
            any_bank(("xt1", h))
        elif kind == "xo1":
            for q in range(2):
                any_bank(("xo1", h, q))
        elif kind == "hidden":
            lend(("hidden",), 0, 1, 2, 3)
        elif kind == "experts":
            lend(("gate_rows",), 4, 5)
            for i in range(HALVES):
                lend(("y1", i), 6 + i)
            for i in range(HALVES):
                lend(("fin", i), 6 + i)
    return plan


def build(nc, dram, out):
    import concourse.bass as bass
    from concourse import mybir
    from contextlib import ExitStack

    f32, f32r, bf16, u32 = mybir.dt.float32, mybir.dt.float32r, mybir.dt.bfloat16, mybir.dt.uint32
    ALU, ACT, AX = mybir.AluOpType, mybir.ActivationFunctionType, mybir.AxisListType
    order = schedule()
    plan = bank_plan(order)

    def nth(*step):
        return [s for s in order if s[0] == step[0]].index(step) + 1

    with ExitStack() as ctx:
        def sb(name, shape, dt=f32):
            return ctx.enter_context(nc.sbuf_tensor(name, shape, dt))

        def sem(name):
            return ctx.enter_context(nc.semaphore(name))

        PS = ctx.enter_context(nc.psum_tensor("banks", [P, 8, 512], f32))

        x = sb("x", [P, TILES, D])
        xn = sb("xn", [P, TILES, D])
        xnT = sb("xnT", [P, TOK])
        kf = sb("kf", [P, TOK])
        stats = sb("stats", [P, TILES, 6])
        mv = sb("mv", [P, TILES, 2])
        veps = sb("veps", [P, TILES])
        half_neg = sb("half_neg", [P, TPH])
        zero = sb("zero", [P, 1])
        rstd = sb("rstd", [P, TILES])
        rl = sb("rl", [P, TILES, E1])
        r8 = sb("r8", [P, TILES, 8])
        i8 = sb("i8", [P, TILES, 8], u32)
        i8f = sb("i8f", [P, TILES, 8])
        eq = sb("eq", [P, TILES, K1, E1])
        pick = sb("pick", [P, TILES, E1])
        rsum = sb("rsum", [P, TILES])
        ghi = sb("ghi", [P, TILES, GW], bf16)
        g3T = sb("g3T", [P, TOK], bf16)
        sel = sb("sel", [P, E1, P], bf16)
        identb = sb("identb", [P, P], bf16)
        ones = sb("ones", [P, 512], bf16)
        b2s = sb("b2s", [GW, 2, 3, P], bf16)
        b2r = sb("b2r", [GW, P])
        ws = sb("ws", [P, 2, EXPERT])
        relu = sb("relu", [P, 2, 2, HT])
        packs = {k: sb(f"pack_{k}", [P, WIDTH[k]]) for k in ("l0", "l1")}

        early = ExitStack()

        def eb(name, shape, dt=f32):
            return early.enter_context(nc.sbuf_tensor(name, shape, dt))

        packs.update({k: eb(f"pack_{k}", [P, WIDTH[k]]) for k in ("ctx", "f0")})
        masks = eb("masks", [P, 2, NH * S])
        fold = eb("fold", [P, 4, P])
        fold_c = eb("fold_c", [HD, P])
        wide = eb("wide", [P, HALVES, 2, HT])
        ssum = eb("ssum", [P, HALVES, 2, TPH * NH])
        rawq = eb("rawq", [P, TOK])
        contT = eb("contT", [P, TOK])
        kexp = eb("kexp", [P, GRP, TOK])
        vx = eb("vx", [P, B, NH // 2, 2 * (HD + 1)])
        pT = eb("pT", [P, HALVES, NH // 2, P])
        top = eb("top", [P, 2 * HALVES, NH])
        orec = eb("orec", [P, 2 * HALVES, NH])
        oh = eb("oh", [P, TILES, D])
        k0T = eb("k0T", [P, TOK])
        v0 = eb("v0", [P, TILES // 2, PAIR, D])
        k1T = eb("k1T", [P, XC, TOK])
        v1 = eb("v1", [P, B, XC, XD])
        xs = eb("xs", [P, TILES, S])
        xtop = eb("xtop", [P, TILES])
        xrec = eb("xrec", [P, TILES])
        halfb = eb("halfb", [P, 4])
        spk = wide
        q1T = kexp
        with ExitStack() as attention:
            qT = attention.enter_context(nc.sbuf_tensor("qT", [P, TOK], f32))
            sc = attention.enter_context(nc.sbuf_tensor("sc", [P, 2 * HALVES, NH * S], f32))
        contr = eb("contr", [P, TOK], f32r)
        w0 = eb("w0", [P, E0 * F0H])
        w0r = [eb("w0_high", [P, E0 * F0H], f32r), eb("w0_low", [M0, E0 * F0H], f32r)]
        early.close()
        hid = sb("hid", [P, 2, 2, HT])
        bias1 = sb("bias1", [P, 2, 2])
        w1r = sb("w1r", [P, 2, 2, F1H], f32r)
        w2r = sb("w2r", [P, 2, 2, 2 * D], f32r)
        xr = sb("xr", [P, 2, TOK], f32r)
        hr = sb("hr", [P, 4, 2, 2, HT], f32r)
        accT = kf

        def piece(pack, name):
            rows, at, cols = LAYOUT[pack][name]
            return packs[pack][0:rows, at:at + cols]

        bank_full = [sem(f"bank_full{b}") for b in range(8)]
        bank_read = [sem(f"bank_read{b}") for b in range(8)]
        x_loaded, masks_loaded = [sem(f"x_loaded{h}") for h in range(HALVES)], sem("masks_loaded")
        pack_loaded = {k: sem(f"pack_{k}_loaded") for k in PACKS}
        ones_set, fill_set, identb_set, b2_split = (sem(n) for n in ("ones_set", "fill_set", "identb_set", "b2_split"))
        stats_ready, rstd_ready, xn_ready = sem("stats_ready"), sem("rstd_ready"), sem("xn_ready")
        squares_ready, squares_summed, roots_ready, qk_normed = (sem(n) for n in ("squares_ready", "squares_summed", "roots_ready", "qk_normed"))
        k_ready = sem("k_ready")
        top_ready, shifted, probs_ready = sem("top_ready"), sem("shifted"), sem("probs_ready")
        xprobs0, xprobs1, xrec_ready, xnorm = sem("xprobs0"), sem("xprobs1"), sem("xrec_ready"), sem("xnorm")
        spikes_in, spikes_out, hid0_used = sem("spikes_in"), sem("spikes_out"), sem("hid0_used")
        logits_shifted, exp_ready, gates_ready = sem("logits_shifted"), sem("exp_ready"), sem("gates_ready")
        dve_step, act_step, pool_step = sem("dve_step"), sem("act_step"), sem("pool_step")
        w_loaded = [sem(f"w_loaded{n}") for n in range(2)]
        part_high = sem("part_high")
        w1_split, w2_split, x_split = sem("w1_split"), sem("w2_split"), sem("x_split")
        w0_high, w0_split, cont_split = sem("w0_high"), sem("w0_split"), sem("cont_split")
        z_full, G_full, acc_done = sem("z_full"), sem("G_full"), sem("acc_done")
        relu_ready, hid_ready, high_ready, low_ready = (sem(n) for n in ("relu_ready", "hid_ready", "high_ready", "low_ready"))
        biased = sem("biased")
        out_ready, stored = sem("out_ready"), sem("stored")

        def await_bias(eng, layernorm, h):
            steps = [s for s in order if s[0] == "norm" and s[1] in RESIDUAL_BIAS]
            eng.wait_ge(biased, steps.index(("norm", layernorm, h)) + 1)

        def filled(ins, name):
            ins.then_inc(bank_full[plan[name][0]], 1)

        def await_bank(eng, name):
            eng.wait_ge(bank_full[plan[name][0]], plan[name][1])

        def read_out(ins, name):
            ins.then_inc(bank_read[plan[name][0]], 1)

        def await_read(eng, name):
            eng.wait_ge(bank_read[plan[name][0]], plan[name][1])

        def chain(eng, signal):
            n = [0]

            def link(ins):
                n[0] += 1
                ins.then_inc(signal, 1)
                eng.wait_ge(signal, n[0])
            return link

        def bank(name, i=0):
            return PS[:, plan[name][3][i], :]

        def tok(t, j=None):
            return slice(P * t, P * t + P) if j is None else slice(P * t + S * j, P * t + S * j + S)

        def rows(j):
            return slice(S * j, S * j + S)

        def half(h):
            return slice(HT * h, HT * h + HT)

        def tiles(h):
            return range(TPH * h, TPH * h + TPH)

        def th(h):
            return slice(TPH * h, TPH * h + TPH)

        def slot(t):
            return 2 * (t // TPH) + t % 2

        def before(t, n=1):
            return t - n if t - n >= TPH * (t // TPH) else None

        def bc(ap, shape):
            return ap.broadcast_to(shape)

        def by_tile(ap):
            return ap.rearrange("p (t d) -> p t d", t=TPH)

        block = ctx.enter_context(nc.Block())

        @block.sync
        def _(sp):
            xv = dram["x"].rearrange("(t p) d -> p t d", p=P)
            sp.dma_start(x[:, th(0), :], xv[:, th(0), :]).then_inc(x_loaded[0], 16)
            sp.dma_start(packs["l0"][:], dram["l0"]).then_inc(pack_loaded["l0"], 16)
            sp.dma_start(x[:, th(1), :], xv[:, th(1), :]).then_inc(x_loaded[1], 16)
            sp.dma_start(masks[:], dram["masks"]).then_inc(masks_loaded, 16)
            for k in ("ctx", "f0", "l1"):
                sp.dma_start(packs[k][:], dram[k]).then_inc(pack_loaded[k], 16)

            def load_expert(e, slot):
                sp.dma_start(ws[:, slot, :], dram["experts"][e, :, :]).then_inc(w_loaded[slot], 16)

            for e in range(2):
                load_expert(e, e)
            for h in range(HALVES):
                for t in tiles(h)[-2:]:
                    await_read(sp, ("t", 0, t, 1))
            sp.dma_start(w0[:], dram["w0"]).then_inc(pack_loaded["w0"], 16)
            with sp.Fori(1, E1 // 2) as i:
                for n in range(2):
                    sp.wait_ge(w2_split, i * 2 + (n - 1))
                    load_expert(i * 2 + n, n)
            o = out.rearrange("(t p) d -> p t d", p=P)
            for n in range(TILES // 2):
                sp.wait_ge(out_ready, n + 1)
                sp.dma_start(o[:, 2 * n:2 * n + 2, :], x[:, 2 * n:2 * n + 2, :]).then_inc(stored, 16)
            sp.wait_ge(stored, 16 * (TILES // 2))

        @block.gpsimd
        def _(pool):
            link = chain(pool, pool_step)
            link(pool.memset(half_neg[:], -0.5))
            link(pool.memset(zero[:], 0.0))

            def rsqrt(k, h):
                pool.wait_ge(stats_ready, nth("stats", k, h))
                link(pool.tensor_scalar(veps[:, th(h)], mv[:, th(h), 1], LN_EPS, None, ALU.add))
                pool.tensor_tensor(rstd[:, th(h)], veps[:, th(h)], half_neg[:], ALU.pow).then_inc(rstd_ready, 1)

            def fill():
                link(pool.memset(vx[:], 0.0))
                for q in range(2):
                    link(pool.memset(vx[rows(q), :, :, 9 * q + 8:9 * q + 9], 1.0))
                link(pool.memset(ghi[:], 0.0))
                link(pool.memset(g3T[:], 0.0))
                link(pool.memset(sel[:], 0.0))
                for part in range(3):
                    ins = pool.affine_select(out=sel[:], in_=sel[:], compare_op=ALU.not_equal, fill=1.0, base=-32 * part,
                                             pattern=[[-1, E1], [0, P]], channel_multiplier=1)
                    if part < 2:
                        link(ins)
                ins.then_inc(fill_set, 1)

            def copied(o, a):
                return pool.tensor_tensor(o, a, bc(zero[:, 0:1], [P, a.shape[1]]), ALU.add)

            def split_weights(i, n, first):
                pool.wait_ge(w_loaded[n], 16 if first else i * 16 + 16)
                if not first:
                    pool.wait_ge(relu_ready, i * 8 + (4 * n - 4))
                copied(bias1[:, n, :], ws[:, n, 2 * F1H:2 * F1H + 2])
                copied(w1r[:, n, 0, :], ws[:, n, 0:F1H]).then_inc(part_high, 1)
                pool.wait_ge(part_high, 2 * n + 1 if first else i * 4 + (2 * n + 1))
                pool.tensor_tensor(w1r[:, n, 1, :], ws[:, n, 0:F1H], w1r[:, n, 0, :].bitcast(f32), ALU.subtract).then_inc(w1_split, 1)
                if not first:
                    pool.wait_ge(acc_done, i * 4 + (2 * n - 2))
                copied(w2r[:, n, 0, :], ws[:, n, F1H:F1H + 2 * D]).then_inc(part_high, 1)
                pool.wait_ge(part_high, 2 * n + 2 if first else i * 4 + (2 * n + 2))
                pool.tensor_tensor(w2r[:, n, 1, :], ws[:, n, F1H:F1H + 2 * D], w2r[:, n, 0, :].bitcast(f32), ALU.subtract).then_inc(w2_split, 1)

            for step in order:
                kind, h = step[0], step[-1]
                if kind == "norm" and step[1] in RESIDUAL_BIAS:
                    pack, name = RESIDUAL_BIAS[step[1]]
                    pool.wait_ge(pack_loaded[pack], 16)
                    pool.wait_ge(xn_ready, nth(*step))
                    pool.tensor_tensor(x[:, th(h), :], x[:, th(h), :], bc(piece(pack, name).unsqueeze(1), [P, TPH, D]),
                                       ALU.add).then_inc(biased, 1)
                elif kind == "stats":
                    rsqrt(step[1], h)
                    if step == ("stats", 0, HALVES - 1):
                        fill()
                elif kind == "split0":
                    pool.wait_ge(w0_high, 1)
                    pool.tensor_tensor(w0r[1][:], w0[0:M0, :], w0r[0][0:M0, :].bitcast(f32), ALU.subtract).then_inc(w0_split, 1)
                elif kind == "scores":
                    pool.wait_ge(top_ready, nth(*step))
                    s = sc[:, slot(h), :].rearrange("p (h k) -> p h k", h=NH)
                    pool.tensor_tensor(s, s, bc(top[:, slot(h), :].unsqueeze(2), [P, NH, S]), ALU.subtract).then_inc(shifted, 1)
                elif kind == "xexp1":
                    pool.wait_ge(xrec_ready, nth(*step))
                    e = sc[:, slot(h), 0:XH * S].rearrange("p (h k) -> p h k", h=XH)
                    pool.tensor_tensor(e, e, bc(orec[:, slot(h), 0:XH].unsqueeze(2), [P, XH, S]), ALU.mult).then_inc(xnorm, 1)
                elif kind == "experts":
                    for n in range(2):
                        split_weights(0, n, True)
                    with pool.Fori(1, E1 // 2) as i:
                        for n in range(2):
                            split_weights(i, n, False)

        @block.tensor
        def _(pe):
            def claim(name):
                for key, count in plan[name][2]:
                    pe.wait_ge(bank_read[key], count)
                return bank(name)

            def mm(o, w, m, start=True, stop=True, **kw):
                return pe.matmul(o, w, m, start=start, stop=stop, **kw)

            ident = piece("l0", "ident")

            def product(name, w, m):
                b = claim(name)
                filled(mm(b[0:w.shape[1], :], w, m), name)

            def turned(name, src, h, identity=ident):
                b = claim(name)
                for i in range(TPH):
                    last = pe.transpose(b[:, P * i:P * i + P], src[:, P * i:P * i + P], identity)
                filled(last, name)

            def fold_weights():
                pe.wait_ge(pack_loaded["l0"], 16)
                for name, a, c in (("dq", "dq", "uqT"), ("dk", "dkv", "ukT"), ("dm", "kr", "qr"), ("c", "uvT", "dkv")):
                    b = claim(("fold", name))
                    w, m = piece("l0", a), piece("l0", c)
                    filled(mm(b[0:w.shape[1], 0:P], w, m), ("fold", name))
                b = claim(("fold", "v"))
                await_read(pe, ("fold", "c"))
                filled(mm(b[:, 0:P], fold_c[:], piece("l0", "oT")), ("fold", "v"))
                await_read(pe, ("fold", "v"))

            def values(name, h, w):
                b = claim(name)
                wv = w.rearrange("p (c q d) -> p q c d", q=2, d=HD)
                for n in range(B // HALVES):
                    for q in range(2):
                        last = mm(b[rows(q), 64 * n:64 * n + 64], xnT[:, HT * h + S * n:HT * h + S * n + S], wv[:, q, :, :])
                filled(last, name)

            def context(name):
                pe.wait_ge(pack_loaded["ctx"], 16)
                ctxT = piece("ctx", "ctxT")
                if name[0] == "ck0":
                    product(name, piece("ctx", "wk0"), ctxT[:, half(name[1])])
                elif name[0] == "ck1":
                    product(name, piece("ctx", "xk")[:, P * name[1]:P * name[1] + P], ctxT[:, half(name[2])])
                elif name[0] == "cv0":
                    b = claim(name)
                    for a in range(2):
                        for j in range(PAIR):
                            for u in range(2):
                                last = mm(b[rows(u), P * (2 * a + j):P * (2 * a + j) + P],
                                          ctxT[:, tok(TPH * name[1] + 2 * a + u, j)], piece("ctx", "wv0"))
                    filled(last, name)
                else:
                    b = claim(name)
                    w = piece("ctx", "xv").rearrange("p (c q d) -> p q c d", q=2, d=XD)
                    for n in range(2):
                        for q in range(2):
                            s0 = S * (2 * name[1] + n)
                            last = mm(b[rows(q), 256 * n:256 * n + 256], ctxT[:, s0:s0 + S], w[:, q, :, :])
                    filled(last, name)

            def scores(layer, t):
                claim(("s", layer, t))
                if layer == 1:
                    await_read(pe, ("q1", t // TPH))
                else:
                    await_read(pe, ("qT0", t // TPH))
                pe.wait_ge(k_ready, nth("expand", layer, t // TPH))
                for i in range(NG):
                    g = slice(32 * i, 32 * i + 32)
                    for j in range(PAIR):
                        last = mm(PS[rows(j), i, 0:GRP * S], qT[g, tok(t, j)], kexp[g, :, tok(t, j)])
                filled(last, ("s", layer, t))

            def turn_weights(layer, t):
                pe.wait_ge(probs_ready, nth("exp", layer, t))
                for g in range(2):
                    b = claim(("t", layer, t, g))
                    for c in range(4):
                        k0 = P * (4 * g + c)
                        last = pe.transpose(b[:, P * c:P * c + P], sc[:, slot(t), k0:k0 + P], ident)
                    filled(last, ("t", layer, t, g))

            def heads(layer, t):
                b = claim(("o", layer, t))
                await_read(pe, ("v%d" % layer, t // TPH))
                for g in range(2):
                    await_read(pe, ("t", layer, t, g))
                for c in range(NH // 2):
                    for j in range(PAIR):
                        last = mm(b[rows(j), 18 * c:18 * c + 18], pT[:, t // TPH, c, rows(j)], vx[:, 2 * t + j, c, :])
                filled(last, ("o", layer, t))

            def hidden_product(i, u, c, first):
                if u % 2 == 0 and c == 0:
                    pe.wait_ge(w1_split, u // 2 + 1 if first else i * 2 + (u // 2 + 1))
                if not (first and u < 2):
                    pe.wait_ge(relu_ready, 2 * (u - 2) + c + 1 if first else i * 8 + (2 * (u - 2) + c + 1))
                for k, (a, b) in enumerate(PARTS):
                    last = mm(PS[:, 2 * (u % 2) + c, :], w1r[:, u // 2, a, P * c:P * c + P], xr[:, b, half(u % 2)],
                              start=(k == 0), stop=(k == len(PARTS) - 1))
                last.then_inc(z_full, 1)

            def experts():
                for name in (("gate_rows",), ("y1", 0), ("y1", 1)):
                    claim(name)
                pe.wait_ge(b2_split, 2)
                for h in range(HALVES):
                    await_read(pe, ("g1", h))
                    for n in range(3):
                        mm(bank(("y1", h)), b2s[:, 1, n, :], g3T[0:GW, half(h)], start=(n == 0), stop=False, skip_group_check=True)

                def down(i, u, first, last=False):
                    n, h = (u % 4) // 2, u % 2
                    if h == 0:
                        pe.wait_ge(w2_split, u // 2 + 1 if first else i * 2 + (u // 2 + 1))
                    for c in range(2):
                        pe.wait_ge(low_ready, 2 * u + c + 1 if first else i * 8 + (2 * u + c + 1))
                        for k, (a, b) in enumerate(PARTS):
                            ins = mm(bank(("y1", h)), w2r[:, n, a, P * c:P * c + P], hr[:, u % 4, c, b, :],
                                     start=False, stop=(last and c == 1 and k == len(PARTS) - 1), skip_group_check=True)
                    if not last:
                        ins.then_inc(acc_done, 1)
                    return ins

                def pair_of_experts(i, first):
                    for u in range(4):
                        n, h, ub = u // 2, u % 2, u % 2
                        fresh = first and u < 2
                        if not fresh:
                            pe.wait_ge(hid_ready, 2 * (u - 2) + 2 if first else i * 8 + (2 * (u - 2) + 2))
                        mm(PS[:, 4 + ub, :], sel[:, (n if first else i * 2 + n), :], g3T[:, half(h)]).then_inc(G_full, 1)
                        if not fresh:
                            for c in range(2):
                                hidden_product(i, u, c, first)
                            down(i, u - 2, first)

                pair_of_experts(0, True)
                with pe.Fori(1, E1 // 2) as i:
                    pair_of_experts(i, False)
                for u in (2 * E1 - 2, 2 * E1 - 1):
                    h = u % 2
                    filled(down(0, u, True, last=True), ("y1", h))
                for h in range(HALVES):
                    await_read(pe, ("y1", h))
                    turned(("fin", h), accT[:, half(h)], h)

            pe.wait_ge(ones_set, 1)
            for at, step in enumerate(order):
                kind, h = step[0], step[-1]
                if kind == "warm":
                    b = claim(("warm", at))
                    for _ in range(step[1]):
                        mm(b, ones[:, 0:P], ones[:])
                elif kind == "fold":
                    fold_weights()
                elif kind == "turn":
                    pe.wait_ge(xn_ready, nth("norm", step[1], h))
                    turned(("lnT", step[1], h), xn[:, th(h), :].rearrange("p t d -> p (t d)"), h)
                elif kind == "qk0":
                    await_read(pe, ("lnT", 0, h))
                    for n, name in enumerate(("q0", "k0")):
                        b = claim((name, h))
                        for i, t in enumerate(tiles(h)):
                            last = mm(b[:, P * i:P * i + P], xnT[:, tok(t)], fold[:, n, :])
                        filled(last, (name, h))
                elif kind == "qkT0":
                    for n, name in enumerate(("qT0", "kT0")):
                        pe.wait_ge(qk_normed, 2 * nth("rms0", h) - 1 + n)
                        turned((name, h), wide[:, h, n, :], h)
                    product(("m0", h), fold[:, 2, :], xnT[:, half(h)])
                elif kind == "v":
                    await_read(pe, ("lnT", (0, 4)[step[1]], h))
                    values(("v%d" % step[1], h), h, fold[:, 3, :] if step[1] == 0 else piece("l1", "qkv")[:, 2 * P:3 * P])
                elif kind == "scores":
                    scores(step[1], h)
                elif kind == "weights":
                    turn_weights(step[1], h)
                elif kind == "values":
                    heads(step[1], h)
                elif kind in ("ck0", "ck1", "cv0", "cv1"):
                    context(step)
                elif kind == "xq0":
                    await_read(pe, ("lnT", 1, h))
                    product(("xq0", h), piece("ctx", "wq0"), xnT[:, half(h)])
                elif kind == "xs0":
                    b = claim(("xs0", h))
                    await_read(pe, ("xq0", h))
                    await_read(pe, ("ck0", h))
                    for i, t in enumerate(tiles(h)):
                        for j in range(PAIR):
                            last = mm(b[rows(j), S * i:S * i + S], rawq[:, tok(t, j)], k0T[:, tok(t, j)])
                    filled(last, ("xs0", h))
                elif kind == "xt0":
                    b = claim(step)
                    pe.wait_ge(xprobs0, nth("xs0", h))
                    for a in range(2):
                        t = TPH * h + 2 * a
                        last = pe.transpose(b[:, P * a:P * a + P], xs[:, t:t + 2, :], ident)
                    filled(last, step)
                elif kind == "xo0":
                    await_read(pe, ("xt0", h))
                    await_read(pe, ("cv0", h))
                    for u in range(2):
                        b = claim(("xo0", h, u))
                        for a in range(2):
                            for j in range(PAIR):
                                last = mm(b[rows(j), P * a:P * a + P], pT[rows(u), h, a, rows(j)],
                                          v0[rows(u), 2 * h + a, j, :])
                        filled(last, ("xo0", h, u))
                elif kind == "enc":
                    pe.wait_ge(pack_loaded["f0"], 16)
                    await_read(pe, ("lnT", 2, h))
                    for c in range(2):
                        product(("enc", h, c), piece("f0", "enc")[:, P * c:P * c + P], xnT[:, half(h)])
                elif kind == "s2c":
                    b = claim(("s2c", h))
                    for c in range(2):
                        pe.wait_ge(spikes_in, 2 * nth("enc", h) - 1 + c)
                        last = mm(b, piece("f0", "s2c")[:, P * c:P * c + P], spk[:, h, c, :], start=(c == 0), stop=(c == 1))
                    filled(last, ("s2c", h))
                elif kind == "route":
                    n = (E0, E1)[step[1]]
                    name = ("rt%d" % step[1], h)
                    b = claim(name)
                    await_read(pe, ("s2c", h) if step[1] == 0 else ("lnT", 6, h))
                    for i, t in enumerate(tiles(h)):
                        w, m = (contT[0:M0, tok(t)], piece("f0", "wr")) if step[1] == 0 else (xnT[:, tok(t)], piece("l1", "gate"))
                        last = mm(b[:, n * i:n * i + n], w, m)
                    filled(last, name)
                elif kind == "gates":
                    name = ("g%d" % step[1], h)
                    b = claim(name).bitcast(bf16)
                    pe.wait_ge(identb_set, 1)
                    pe.wait_ge(gates_ready, nth(*next(s for s in order if s[0:2] == ("pick", step[1]) and s[2] <= h <= s[3])))
                    for i, t in enumerate(tiles(h)):
                        last = pe.transpose(b[0:GW, P * i:P * i + P], ghi[:, t, :], identb[:])
                    filled(last, name)
                elif kind == "up0":
                    g, p = step[1], step[2]
                    if p == 0:
                        pe.wait_ge(w0_split, 1)
                        pe.wait_ge(cont_split, nth("pick", 0, g, g))
                        pe.wait_ge(fill_set, 1)
                        await_read(pe, ("g0", g))
                    for q in range(2):
                        b, e = claim(("z0", g, p, q)), 2 * p + q
                        mm(b, w0r[0][:, F0H * e:F0H * e + F0H], contr[:, half(g)], stop=False)
                        filled(mm(b, w0r[1][:, F0H * e:F0H * e + F0H], contr[0:M0, half(g)], start=False), ("z0", g, p, q))
                        product(("G0", g, p, q), sel[:, 2 * p + q, :], g3T[:, half(g)])
                elif kind == "down0":
                    g, p = step[1], step[2]
                    b = claim(("y0", g)) if p == 0 else bank(("y0", g))
                    for q in range(2):
                        e = 2 * p + q
                        await_read(pe, ("G0", g, p, q))
                        mm(b[rows(q), :], piece("f0", "w2")[:, M0 * e:M0 * e + M0], wide[:, g, q, :],
                           start=(p == 0), stop=(q == 1 and p == E0 // 2 - 1), skip_group_check=True).then_inc(hid0_used, 1)
                    if p == E0 // 2 - 1:
                        pe.wait_ge(b2_split, 1)
                        for n in range(3):
                            last = mm(b[rows(0), :], b2s[:, 0, n, 0:M0], g3T[0:GW, half(g)],
                                      start=False, stop=True, skip_group_check=True)
                        filled(last, ("y0", g))
                elif kind == "c2s":
                    await_read(pe, ("y0", h))
                    for c in range(2):
                        product(("c2s", h, c), piece("f0", "c2s")[:, P * c:P * c + P], accT[:, half(h)])
                elif kind == "dec":
                    b = claim(("dec", h))
                    pe.wait_ge(spikes_out, 2 * nth("c2s", h))
                    for i in range(TPH):
                        for c in range(2):
                            last = mm(b[:, P * i:P * i + P], relu[:, h, c, P * i:P * i + P], piece("f0", "dec")[:, P * c:P * c + P],
                                      start=(c == 0), stop=(c == 1))
                    filled(last, ("dec", h))
                elif kind == "qk1":
                    await_read(pe, ("lnT", 4, h))
                    pe.wait_ge(pack_loaded["l1"], 16)
                    product(("q1", h), piece("l1", "qkv")[:, 0:P], xnT[:, half(h)])
                    product(("k1", h), piece("l1", "qkv")[:, P:2 * P], xnT[:, half(h)])
                elif kind == "oT":
                    await_read(pe, ("o", 1, TPH * h + TPH - 1))
                    turned(("oT", h), oh[:, th(h), :].rearrange("p t d -> p (t d)"), h)
                elif kind == "pr":
                    b = claim(("pr", h))
                    await_read(pe, ("oT", h))
                    for i, t in enumerate(tiles(h)):
                        last = mm(b[:, P * i:P * i + P], rawq[:, tok(t)], piece("l1", "proj"))
                    filled(last, ("pr", h))
                elif kind == "xq1":
                    await_read(pe, ("lnT", 5, h))
                    for c in range(XC):
                        product(("xq1", h, c), piece("l1", "xq")[:, P * c:P * c + P], xnT[:, half(h)])
                elif kind == "xs1":
                    claim(("xs1", h))
                    for c in range(XC):
                        await_read(pe, ("xq1", h // TPH, c))
                        await_read(pe, ("ck1", c, h // TPH))
                    for c in range(XC):
                        for q in range(2):
                            for j in range(PAIR):
                                last = mm(bank(("xs1", h), q)[rows(j), S * c:S * c + S], q1T[rows(q), c, tok(h, j)],
                                          k1T[rows(q), c, tok(h, j)])
                    filled(last, ("xs1", h))
                elif kind == "xw1":
                    pe.wait_ge(xnorm, nth("xexp1", h))
                    b = claim(("xt1", h))
                    for c in range(XC):
                        last = pe.transpose(b[:, P * c:P * c + P], sc[:, slot(h), P * c:P * c + P], ident)
                    filled(last, ("xt1", h))
                elif kind == "xo1":
                    bs = [claim(("xo1", h, q)) for q in range(2)]
                    await_read(pe, ("xt1", h))
                    await_read(pe, ("cv1", h))
                    last = [None, None]
                    for c in range(XC):
                        for q in range(2):
                            for j in range(PAIR):
                                last[q] = mm(bs[q][rows(q), P * c + S * j:P * c + S * j + S],
                                             v1[rows(q), 2 * h + j, c, :], pT[rows(q), h // TPH, c, rows(j)])
                    for q in range(2):
                        filled(last[q], ("xo1", h, q))
                elif kind == "xp1":
                    b = claim(("xp1", h))
                    for q in range(2):
                        await_read(pe, ("xo1", h, q))
                    for c in range(XC):
                        last = mm(b[:, 0:P], q1T[:, c, tok(h)], piece("l1", "xo")[:, P * c:P * c + P],
                                  start=(c == 0), stop=(c == XC - 1))
                    filled(last, ("xp1", h))
                elif kind == "hidden":
                    claim(("hidden",))
                    for u in range(2):
                        pe.wait_ge(x_split, u + 1)
                        for c in range(2):
                            hidden_product(0, u, c, True)
                elif kind == "experts":
                    experts()

        @block.scalar
        def _(act):
            link = chain(act, act_step)

            def evac(name, dst, src=None, func=ACT.Copy, **kw):
                await_bank(act, name)
                read_out(act.activation(dst, bank(name) if src is None else src, func, **kw), name)

            def values(name, h):
                await_bank(act, name)
                src = bank(name).rearrange("p (n d) -> p n d", d=HD)
                dst = vx[:, 8 * h:8 * h + 8, :, :].rearrange("p b c d -> p (b c) d")
                act.activation(dst[rows(0), :, 0:HD], src[rows(0), :, :], ACT.Copy)
                read_out(act.activation(dst[rows(1), :, HD + 1:2 * HD + 1], src[rows(1), :, :], ACT.Copy), name)

            def hidden_relu(i, u, c, first):
                act.wait_ge(z_full, 2 * u + c + 1 if first else i * 8 + (2 * u + c + 1))
                if not (first and u < 2):
                    act.wait_ge(hid_ready, 2 * (u - 2) + c + 1 if first else i * 8 + (2 * (u - 2) + c + 1))
                act.activation(relu[:, u % 2, c, :], PS[:, 2 * (u % 2) + c, :], ACT.Relu,
                               bias=bias1[:, u // 2, c:c + 1]).then_inc(relu_ready, 1)

            def experts():
                def pair_of_experts(i, first):
                    for u in range(4):
                        ub = u % 2
                        if not (first and u < 2):
                            for c in range(2):
                                hidden_relu(i, u, c, first)
                        if not first:
                            act.wait_ge(acc_done, i * 4 + (u - 3))
                        for c in range(2):
                            act.wait_ge(hid_ready, 2 * u + c + 1 if first else i * 8 + (2 * u + c + 1))
                            act.activation(hr[:, u, c, 0, :], hid[:, ub, c, :], ACT.Copy).then_inc(high_ready, 1)

                pair_of_experts(0, True)
                with act.Fori(1, E1 // 2) as i:
                    pair_of_experts(i, False)
                for h in range(HALVES):
                    evac(("y1", h), accT[:, half(h)])

            for step in order:
                kind, h = step[0], step[-1]
                if kind == "fold":
                    act.wait_ge(pack_loaded["l0"], 16)
                    act.activation(identb[:], piece("l0", "ident"), ACT.Copy).then_inc(identb_set, 1)
                elif kind == "turn":
                    name = ("lnT", step[1], h)
                    if step[1] == 6:
                        await_bank(act, name)
                        act.activation(xr[:, 0, half(h)], bank(name), ACT.Copy)
                    evac(name, xnT[:, half(h)])
                elif kind == "qk0":
                    for n, name in enumerate(("q0", "k0")):
                        await_bank(act, (name, h))
                        act.activation(relu[:, h, n, :], bank((name, h)), ACT.Square).then_inc(squares_ready, 1)
                        read_out(act.activation(wide[:, h, n, :], bank((name, h)), ACT.Copy), (name, h))
                elif kind == "rms0":
                    act.wait_ge(squares_summed, nth(*step))
                    act.activation(ssum[:, h, :, :], ssum[:, h, :, :], ACT.Sqrt, scale=1.0 / HD,
                                   bias=piece("l0", "eps")).then_inc(roots_ready, 1)
                elif kind == "qkT0":
                    evac(("qT0", h), qT[:, half(h)], scale=piece("l0", "qnw"))
                    evac(("kT0", h), kf[:, half(h)], scale=piece("l0", "knw"))
                elif kind == "v":
                    if step[1] == 0:
                        act.wait_ge(fill_set, 1)
                    values(("v%d" % step[1], h), h)
                elif kind == "exp":
                    act.wait_ge(shifted, nth("scores", step[1], h))
                    act.activation(sc[:, slot(h), :], sc[:, slot(h), :], ACT.Exp).then_inc(probs_ready, 1)
                elif kind == "weights":
                    if before(h) is not None:
                        await_bank(act, ("o", step[1], before(h)))
                    for g in range(2):
                        evac(("t", step[1], h, g), pT[:, h // TPH, 4 * g:4 * g + 4, :])
                elif kind == "ck0":
                    act.wait_ge(pack_loaded["ctx"], 16)
                    evac(step, k0T[:, half(h)], func=ACT.Identity, bias=piece("ctx", "bk0"))
                elif kind == "ck1":
                    evac(step, k1T[:, step[1], half(h)])
                elif kind == "cv0":
                    evac(step, v0[:, 2 * h:2 * h + 2, :, :])
                elif kind == "cv1":
                    evac(step, v1[:, 2 * h:2 * h + 2, :, :])
                elif kind == "xq0":
                    evac(step, rawq[:, half(h)], func=ACT.Identity, bias=piece("ctx", "bq0"))
                elif kind == "xs0":
                    await_read(act, ("xs0", h))
                    act.activation(xs[:, th(h), :], xs[:, th(h), :], ACT.Exp).then_inc(xprobs0, 1)
                elif kind == "xt0":
                    evac(("xt0", h), pT[:, h, 0:2, :], src=bank(("xt0", h))[:, 0:2 * P])
                elif kind == "enc":
                    if nth(*step) == 1:
                        act.wait_ge(pack_loaded["f0"], 16)
                        act.activation(halfb[:, 0:2], piece("f0", "benc"), ACT.Copy, scale=0.5)
                        link(act.activation(halfb[:, 2:4], piece("f0", "bc2s"), ACT.Copy, scale=0.5))
                    for c in range(2):
                        evac(("enc", h, c), spk[:, h, c, :], func=ACT.Tanh, scale=0.5, bias=halfb[:, c:c + 1])
                elif kind == "split0":
                    act.wait_ge(pack_loaded["w0"], 16)
                    act.activation(w0r[0][:], w0[:], ACT.Copy).then_inc(w0_high, 1)
                elif kind == "s2c":
                    await_bank(act, step)
                    act.activation(contr[:, half(h)], bank(step), ACT.Identity, bias=piece("f0", "bs2c"))
                    evac(step, contT[:, half(h)], func=ACT.Identity, bias=piece("f0", "bs2c"))
                elif kind == "route":
                    act.wait_ge(logits_shifted, nth(*step))
                    n = (E0, E1)[step[1]]
                    act.activation(rl[:, th(h), 0:n], rl[:, th(h), 0:n], ACT.Exp).then_inc(exp_ready, 1)
                elif kind == "gates":
                    name = ("g%d" % step[1], h)
                    if step[1] == 0:
                        act.wait_ge(fill_set, 1)
                    evac(name, g3T[0:GW, half(h)], src=bank(name).bitcast(bf16)[0:GW, 0:HT])
                elif kind == "up0":
                    g, p = step[1], step[2]
                    for q in range(2):
                        if p > 0:
                            await_read(act, ("G0", g, p - 1, q))
                        evac(("z0", g, p, q), relu[:, g, q, :], func=ACT.Relu, bias=piece("f0", "b1")[:, 2 * p + q:2 * p + q + 1])
                elif kind == "down0" and h == E0 // 2 - 1:
                    evac(("y0", step[1]), accT[:, half(step[1])])
                elif kind == "c2s":
                    for c in range(2):
                        evac(("c2s", h, c), relu[:, h, c, :], func=ACT.Tanh, scale=0.5, bias=halfb[:, 2 + c:3 + c])
                elif kind == "qk1":
                    evac(("q1", h), qT[:, half(h)])
                    evac(("k1", h), kf[:, half(h)])
                elif kind == "oT":
                    evac(("oT", h), rawq[:, half(h)])
                elif kind == "xq1":
                    for c in range(XC):
                        evac(("xq1", h, c), q1T[:, c, half(h)])
                elif kind == "xexp1":
                    await_read(act, ("xs1", h))
                    act.activation(sc[:, slot(h), 0:XH * S], sc[:, slot(h), 0:XH * S], ACT.Exp,
                                   scale=float(XD) ** -0.5).then_inc(xprobs1, 1)
                elif kind == "xw1":
                    if before(h) is not None:
                        await_bank(act, ("xo1", before(h), 1))
                    evac(("xt1", h), pT[:, h // TPH, 0:XC, :])
                elif kind == "xo1":
                    for q in range(2):
                        name = ("xo1", h, q)
                        evac(name, q1T[rows(q), :, tok(h)], src=bank(name)[rows(q), :].rearrange("p (c k) -> p c k", c=XC))
                elif kind == "hidden":
                    for u in range(2):
                        for c in range(2):
                            hidden_relu(0, u, c, True)
                elif kind == "experts":
                    experts()

        @block.vector
        def _(dve):
            link = chain(dve, dve_step)
            dve.memset(ones[:], 1.0).then_inc(ones_set, 1)

            def stats_of(k, h):
                src = xn if k == 3 else x
                for t in tiles(h):
                    last = dve.bn_stats(stats[:, t, :], src[:, t, :])
                link(last)
                for t in tiles(h):
                    last = dve.bn_aggr(mv[:, t, :], stats[:, t, :])
                last.then_inc(stats_ready, 1)

            def normalise(k, h, dst):
                dve.wait_ge(rstd_ready, nth("stats", k, h))
                src = xn if k == 3 else x
                for t in tiles(h):
                    last = dve.tensor_scalar(dst[:, t, :], src[:, t, :], mv[:, t, 0:1], rstd[:, t:t + 1], ALU.subtract, ALU.mult)
                return last

            def scores(layer, t):
                name = ("s", layer, t)
                await_bank(dve, name)
                s = sc[:, slot(t), :]
                read_out(dve.scalar_tensor_tensor(s.rearrange("p (i n) -> p i n", i=NG), PS[:, 0:NG, 0:GRP * S],
                                                  float(HD) ** -0.5, masks[:, layer, :].rearrange("p (i n) -> p i n", i=NG),
                                                  ALU.mult, ALU.add), name)
                await_read(dve, name)
                dve.reduce_max(top[:, slot(t), :], s.rearrange("p (h k) -> p h k", h=NH), AX.X).then_inc(top_ready, 1)

            def heads(layer, t):
                name = ("o", layer, t)
                await_bank(dve, name)
                o = bank(name)[:, 0:NH * (HD + 1)].rearrange("p (h d) -> p h d", h=NH)
                link(dve.reciprocal(orec[:, slot(t), :], o[:, :, HD]))
                dst = oh[:, t, :].rearrange("p (h d) -> p h d", h=NH)
                read_out(dve.tensor_tensor(dst, o[:, :, 0:HD], bc(orec[:, slot(t), :].unsqueeze(2), [P, NH, HD]), ALU.mult), name)
                if layer == 0:
                    await_read(dve, name)
                    last = dve.tensor_tensor(x[:, t, :], x[:, t, :], oh[:, t, :], ALU.add)
                    if t % TPH == TPH - 1:
                        link(last)

            def route(layer, h):
                n = (E0, E1)[layer]
                name = ("rt%d" % layer, h)
                await_bank(dve, name)
                r, s4 = rl[:, th(h), 0:n], rsum[:, th(h)]
                src = bank(name)[:, 0:TPH * n].rearrange("p (t e) -> p t e", e=n)
                if layer == 0:
                    read_out(dve.tensor_tensor(r, src, bc(piece("f0", "br").unsqueeze(1), [P, TPH, n]), ALU.add), name)
                else:
                    read_out(dve.tensor_copy(r, src), name)
                await_read(dve, name)
                link(dve.reduce_max(s4, r, AX.X))
                dve.tensor_tensor(r, r, bc(s4.unsqueeze(2), [P, TPH, n]), ALU.subtract).then_inc(logits_shifted, 1)

            def pick_experts(layer, h0, h1):
                n, k = ((E0, K0), (E1, K1))[layer]
                some = slice(TPH * h0, TPH * h1 + TPH)
                r, s4, shape = rl[:, some, 0:n], rsum[:, some], [P, some.stop - some.start, n]
                dve.wait_ge(exp_ready, max(nth("route", layer, h) for h in (h0, h1)))
                link(dve.reduce_sum(s4, r, AX.X))
                link(dve.reciprocal(s4, s4))
                link(dve.tensor_tensor(r, r, bc(s4.unsqueeze(2), shape), ALU.mult))
                for t in range(some.start, some.stop):
                    last = dve.max(r8[:, t, :], rl[:, t, 0:n])
                link(last)
                for t in range(some.start, some.stop):
                    last = dve.max_index(i8[:, t, :], r8[:, t, :], rl[:, t, 0:n])
                link(last)
                link(dve.tensor_copy(i8f[:, some, :], i8[:, some, :]))
                iota = piece("l0", "iota")
                for t in range(some.start, some.stop):
                    last = dve.tensor_tensor(eq[:, t, 0:k, 0:n], bc(iota[:, 0:n].unsqueeze(1), [P, k, n]),
                                             bc(i8f[:, t, 0:k].unsqueeze(2), [P, k, n]), ALU.is_equal)
                link(last)
                link(dve.reduce_sum(pick[:, some, 0:n], eq[:, some, 0:k, 0:n].rearrange("p t k e -> p t e k"), AX.X))
                link(dve.tensor_tensor(r, r, pick[:, some, 0:n], ALU.mult))
                link(dve.reduce_sum(s4, r, AX.X))
                if layer == 1:
                    link(dve.tensor_scalar(s4, s4, 1e-12, None, ALU.max))
                link(dve.reciprocal(s4, s4))
                link(dve.tensor_tensor(r, r, bc(s4.unsqueeze(2), shape), ALU.mult))
                if nth("pick", layer, h0, h1) == 1:
                    dve.wait_ge(fill_set, 1)
                link(dve.tensor_copy(ghi[:, some, 0:n], r))
                link(dve.tensor_tensor(r, r, ghi[:, some, 0:n], ALU.subtract))
                link(dve.tensor_copy(ghi[:, some, 32:32 + n], r))
                link(dve.tensor_tensor(r, r, ghi[:, some, 32:32 + n], ALU.subtract))
                dve.tensor_copy(ghi[:, some, 64:64 + n], r).then_inc(gates_ready, 1)

            def bias_parts(layer, src, n):
                link(dve.tensor_copy(b2s[:, layer, 0, 0:n], src))
                link(dve.tensor_tensor(b2r[:, 0:n], src, b2s[:, layer, 0, 0:n], ALU.subtract))
                link(dve.tensor_copy(b2s[:, layer, 1, 0:n], b2r[:, 0:n]))
                link(dve.tensor_tensor(b2r[:, 0:n], b2r[:, 0:n], b2s[:, layer, 1, 0:n], ALU.subtract))
                dve.tensor_copy(b2s[:, layer, 2, 0:n], b2r[:, 0:n]).then_inc(b2_split, 1)

            def experts():
                def pair_of_experts(i, first):
                    for u in range(4):
                        ub = u % 2
                        fresh = first and u < 2
                        dve.wait_ge(G_full, u + 1 if first else i * 4 + (u + 1))
                        for c in range(2):
                            if not fresh:
                                dve.wait_ge(high_ready, 2 * (u - 2) + c + 1 if first else i * 8 + (2 * (u - 2) + c + 1))
                            dve.wait_ge(relu_ready, 2 * u + c + 1 if first else i * 8 + (2 * u + c + 1))
                            dve.tensor_tensor(hid[:, ub, c, :], relu[:, ub, c, :], PS[:, 4 + ub, :], ALU.mult).then_inc(hid_ready, 1)
                        for c in range(2):
                            dve.wait_ge(high_ready, 2 * u + c + 1 if first else i * 8 + (2 * u + c + 1))
                            dve.tensor_tensor(hr[:, u, c, 1, :], hid[:, ub, c, :], hr[:, u, c, 0, :].bitcast(f32), ALU.subtract).then_inc(low_ready, 1)

                pair_of_experts(0, True)
                with dve.Fori(1, E1 // 2) as i:
                    pair_of_experts(i, False)
                for h in range(HALVES):
                    name = ("fin", h)
                    await_bank(dve, name)
                    for i in range(0, TPH, 2):
                        t = slice(TPH * h + i, TPH * h + i + 2)
                        dve.tensor_tensor(x[:, t, :], x[:, t, :], by_tile(bank(name))[:, i:i + 2, :], ALU.add).then_inc(out_ready, 1)

            d4 = [P, TPH, D]
            for step in order:
                kind, h = step[0], step[-1]
                if kind == "fold":
                    dve.wait_ge(pack_loaded["l0"], 16)
                    for n, w in enumerate(("dq", "dk", "dm", "c", "v")):
                        name = ("fold", w)
                        await_bank(dve, name)
                        if w == "c":
                            read_out(dve.tensor_copy(fold_c[:], bank(name)[0:HD, 0:P]), name)
                        else:
                            read_out(dve.tensor_tensor(fold[:, min(n, 3), :], bank(name)[:, 0:P], piece("l0", "blocks"), ALU.mult), name)
                elif kind == "stats":
                    if step[1] == 0:
                        dve.wait_ge(x_loaded[h], 16)
                    stats_of(step[1], h)
                elif kind == "norm":
                    normalise(step[1], h, xn).then_inc(xn_ready, 1)
                elif kind == "rms0":
                    dve.wait_ge(squares_ready, 2 * nth("qk0", h))
                    dve.reduce_sum(ssum[:, h, :, :].rearrange("p n s -> p (n s)"),
                                   relu[:, h, :, :].rearrange("p n (s d) -> p (n s) d", d=HD), AX.X).then_inc(squares_summed, 1)
                    dve.wait_ge(roots_ready, nth(*step))
                    link(dve.reciprocal(ssum[:, h, :, :], ssum[:, h, :, :]))
                    await_read(dve, ("k0", h))
                    for n in range(2):
                        w = wide[:, h, n, :].rearrange("p (s d) -> p s d", d=HD)
                        dve.tensor_tensor(w, w, bc(ssum[:, h, n, :].unsqueeze(2), [P, TPH * NH, HD]), ALU.mult).then_inc(qk_normed, 1)
                elif kind == "expand":
                    if step[1] == 0:
                        await_read(dve, ("kT0", h))
                        await_bank(dve, ("m0", h))
                        read_out(dve.tensor_tensor(kf[:, half(h)], kf[:, half(h)], bank(("m0", h)), ALU.add), ("m0", h))
                        await_read(dve, ("m0", h))
                    else:
                        await_read(dve, ("k1", h))
                    for j in range(GRP):
                        last = dve.tensor_scalar(kexp[:, j, half(h)], kf[:, half(h)], piece("l0", "heads")[:, j:j + 1], None, ALU.mult)
                    last.then_inc(k_ready, 1)
                elif kind == "scores":
                    dve.wait_ge(masks_loaded, 16)
                    scores(step[1], h)
                elif kind == "values":
                    heads(step[1], h)
                elif kind == "xs0":
                    name = ("xs0", h)
                    await_bank(dve, name)
                    s = bank(name)[:, 0:TPH * S].rearrange("p (t k) -> p t k", k=S)
                    link(dve.reduce_max(xtop[:, th(h)], s, AX.X))
                    read_out(dve.tensor_tensor(xs[:, th(h), :], s, bc(xtop[:, th(h)].unsqueeze(2), [P, TPH, S]), ALU.subtract), name)
                elif kind == "xo0":
                    await_bias(dve, 1, h)
                    dve.wait_ge(xprobs0, nth("xs0", h))
                    link(dve.reduce_sum(xrec[:, th(h)], xs[:, th(h), :], AX.X))
                    link(dve.reciprocal(xrec[:, th(h)], xrec[:, th(h)]))
                    for u in range(2):
                        name = ("xo0", h, u)
                        await_bank(dve, name)
                        for a in range(2):
                            t = TPH * h + 2 * a + u
                            last = dve.scalar_tensor_tensor(x[:, t, :], bank(name)[:, P * a:P * a + P], xrec[:, t:t + 1], x[:, t, :], ALU.mult, ALU.add)
                        read_out(last, name)
                    await_read(dve, ("xo0", h, 1))
                elif kind == "enc":
                    for c in range(2):
                        await_read(dve, ("enc", h, c))
                        dve.tensor_scalar(spk[:, h, c, :], spk[:, h, c, :], 0.5, 0.5, ALU.mult, ALU.add).then_inc(spikes_in, 1)
                elif kind == "s2c":
                    if nth(*step) == 1:
                        bias_parts(0, piece("f0", "b2"), M0)
                elif kind == "route":
                    route(step[1], h)
                elif kind == "pick":
                    if step[1] == 1:
                        for i in range(step[2], h + 1):
                            await_read(dve, ("lnT", 6, i))
                            dve.tensor_tensor(xr[:, 1, half(i)], xnT[:, half(i)], xr[:, 0, half(i)].bitcast(f32), ALU.subtract).then_inc(x_split, 1)
                    else:
                        for i in range(step[2], h + 1):
                            await_read(dve, ("s2c", i))
                            low = slice(M0, P)
                            dve.tensor_tensor(contr[low, half(i)], contT[low, half(i)], contr[low, half(i)].bitcast(f32), ALU.subtract).then_inc(cont_split, 1)
                    pick_experts(*step[1:])
                elif kind == "up0":
                    g, p = step[1], step[2]
                    for q in range(2):
                        await_read(dve, ("z0", g, p, q))
                        await_bank(dve, ("G0", g, p, q))
                        if p > 0:
                            dve.wait_ge(hid0_used, 2 * nth("down0", g, p - 1) - 1 + q)
                        read_out(dve.tensor_tensor(wide[:, g, q, :], relu[:, g, q, :], bank(("G0", g, p, q)), ALU.mult), ("G0", g, p, q))
                elif kind == "c2s":
                    for c in range(2):
                        await_read(dve, ("c2s", h, c))
                        dve.tensor_scalar(relu[:, h, c, :], relu[:, h, c, :], 0.5, 0.5, ALU.mult, ALU.add).then_inc(spikes_out, 1)
                elif kind == "dec":
                    await_bank(dve, step)
                    read_out(dve.tensor_tensor(xn[:, th(h), :], by_tile(bank(step)), bc(piece("f0", "bdec").unsqueeze(1), d4), ALU.add), step)
                    await_read(dve, step)
                elif kind == "inner":
                    dve.wait_ge(stats_ready, nth("stats", 3, h))
                    for t in tiles(h):
                        last = dve.scalar_tensor_tensor(oh[:, t, :], xn[:, t, :], mv[:, t, 0:1], piece("f0", "lng"), ALU.subtract, ALU.mult)
                    link(last)
                    await_bias(dve, 2, h)
                    dve.wait_ge(rstd_ready, nth("stats", 3, h))
                    for t in tiles(h):
                        last = dve.scalar_tensor_tensor(x[:, t, :], oh[:, t, :], rstd[:, t:t + 1], x[:, t, :], ALU.mult, ALU.add)
                    link(last)
                elif kind == "qk1":
                    if nth(*step) == 1:
                        dve.wait_ge(pack_loaded["l1"], 16)
                        bias_parts(1, piece("l1", "fb2"), D)
                elif kind == "pr":
                    name = ("pr", h)
                    await_bank(dve, name)
                    read_out(dve.tensor_tensor(x[:, th(h), :], x[:, th(h), :], by_tile(bank(name)), ALU.add), name)
                    await_read(dve, name)
                elif kind == "xs1":
                    s = PS[:, plan[("xs1", h)][0]:plan[("xs1", h)][0] + 2, 0:XC * S].rearrange("p q (c k) -> p q c k", c=XC)
                    await_bank(dve, step)
                    tp = top[:, slot(h), 0:XH].rearrange("p (q c) -> p q c", q=2)
                    link(dve.reduce_max(tp, s, AX.X))
                    w = sc[:, slot(h), 0:XH * S].rearrange("p (c q k) -> p q c k", q=2, k=S)
                    for q in range(2):
                        last = dve.tensor_tensor(w[:, q, :, :], s[:, q, :, :], bc(tp[:, q, :].unsqueeze(2), [P, XC, S]), ALU.subtract)
                    read_out(last, step)
                elif kind == "xexp1":
                    dve.wait_ge(xprobs1, nth(*step))
                    e = sc[:, slot(h), 0:XH * S].rearrange("p (h k) -> p h k", h=XH)
                    link(dve.reduce_sum(orec[:, slot(h), 0:XH], e, AX.X))
                    dve.reciprocal(orec[:, slot(h), 0:XH], orec[:, slot(h), 0:XH]).then_inc(xrec_ready, 1)
                elif kind == "xp1":
                    await_bank(dve, step)
                    await_bias(dve, 5, h // TPH)
                    read_out(dve.tensor_tensor(x[:, h, :], x[:, h, :], bank(step)[:, 0:P], ALU.add), step)
                    if h % TPH == TPH - 1:
                        await_read(dve, step)
                elif kind == "experts":
                    experts()


def _tile_cols(a, n):
    return np.tile(a, (1, n))


def _host_pieces(v):
    heads = np.arange(P) // HD
    rep = P // HD
    w2 = v["L0_ffn_W2"]
    b2 = np.zeros((GW, M0), np.float32)
    fb2 = np.zeros((GW, D), np.float32)
    for n in range(3):
        b2[32 * n:32 * n + E0] = v["L0_ffn_b2"]
        fb2[32 * n:32 * n + E1] = v["L1_ffn_b2"]

    def row(a):
        return np.broadcast_to(a[None, :], (P, a.shape[0]))

    def col(a):
        return a.reshape(-1, P).T

    def cols2(w):
        return w.reshape(-1, P, w.shape[1]).transpose(1, 0, 2).reshape(P, -1)

    s2c = v["L0_ffn_W_s2c"].reshape(2, P, M0).transpose(1, 0, 2)
    return {
        "ident": np.eye(P, dtype=np.float32),
        "blocks": (heads[:, None] == heads[None, :]).astype(np.float32),
        "heads": (heads[:, None] % GRP == np.arange(GRP)[None, :]).astype(np.float32),
        "eps": np.full((P, 1), RMS_EPS, np.float32),
        "qnw": np.tile(v["L0_attn_q_norm_w"], rep)[:, None], "knw": np.tile(v["L0_attn_k_norm_w"], rep)[:, None],
        "dq": _tile_cols(v["L0_attn_W_DQ"], rep), "uqT": _tile_cols(v["L0_attn_W_UQ"].T, rep),
        "dkv": _tile_cols(v["L0_attn_W_DKV"], rep), "ukT": _tile_cols(v["L0_attn_W_UKV"][:HD].T, rep),
        "uvT": v["L0_attn_W_UKV"][HD:].T, "kr": _tile_cols(v["L0_attn_W_KR"], rep),
        "qr": _tile_cols(v["L0_attn_W_QR"], rep), "oT": _tile_cols(v["L0_attn_W_O"].T, rep),
        "ctxT": v["ctx_768"].reshape(TOK, DC).T, "wk0": v["L0_xattn_Wk"], "wv0": v["L0_xattn_Wv"],
        "bk0": col(v["L0_xattn_bk"]), "bv0": row(v["L0_xattn_bv"]), "wq0": v["L0_xattn_Wq"], "bq0": col(v["L0_xattn_bq"]),
        "xk": v["L1_xattn_Wk"], "xv": v["L1_xattn_Wv"],
        "enc": v["L0_ffn_W_enc"], "benc": col(v["L0_ffn_b_enc"]),
        "s2c": np.concatenate([s2c, s2c], axis=2).reshape(P, 2 * P),
        "bs2c": np.tile(v["L0_ffn_b_s2c"], 2)[:, None], "wr": v["L0_ffn_Wr"], "br": row(v["L0_ffn_br"]),
        "iota": row(np.arange(E1, dtype=np.float32)),
        "w1": np.concatenate([v["L0_ffn_W1"].transpose(1, 0, 2).reshape(M0, -1)] * 2, axis=0),
        "b1": v["L0_ffn_b1"].T, "w2": w2.transpose(1, 0, 2).reshape(P, -1), "b2": b2,
        "c2s": np.concatenate([v["L0_ffn_W_c2s"]] * 2, axis=0), "bc2s": col(v["L0_ffn_b_c2s"]),
        "dec": cols2(v["L0_ffn_W_dec"]), "bdec": row(v["L0_ffn_b_dec"]), "lng": row(v["L0_ffn_ln_g"]), "lnb": row(v["L0_ffn_ln_b"]),
        "qkv": v["L1_attn_w_qkv"], "proj": v["L1_attn_w_proj"], "xq": v["L1_xattn_Wq"], "xo": cols2(v["L1_xattn_Wo"]),
        "xbo": row(v["L1_xattn_bo"]), "gate": v["L1_ffn_gate"],
        "fb2": fb2,
    }


def _expert_rows(w1, w2, b1):
    w2 = w2.reshape(E1, 2, P, D).transpose(0, 2, 1, 3).reshape(E1, P, 2 * D)
    return np.ascontiguousarray(np.concatenate([w1, w2, b1.reshape(E1, 2, P).transpose(0, 2, 1)], axis=2))


def _masks():
    q = (np.arange(P) % S)[:, None, None]
    k = np.arange(S)[None, None, :]
    first = 2.0 ** (-(2.0 ** -(np.log2(NH) - 3)))
    slopes = np.array([first * first ** n for n in range(NH)], np.float32)[None, :, None]
    keep = np.broadcast_to(k <= q, (P, NH, S))
    causal = np.where(keep, np.float32(0), np.float32(MASKED))
    alibi = np.where(keep, slopes * k.astype(np.float32), np.float32(MASKED))
    return np.stack([causal, alibi], axis=1).astype(np.float32).reshape(P, 2, NH * S)


def kernel(**inputs):
    import concourse.bacc as bacc
    from concourse import mybir
    from concourse.bass_utils import run_bass_kernel_spmd

    v = {k: np.asarray(a) for k, a in inputs.items()}
    pieces = _host_pieces(v)
    arrays = {"x": np.ascontiguousarray(v["x"].reshape(TOK, D)), "masks": _masks(),
              "experts": _expert_rows(v["L1_ffn_W1"], v["L1_ffn_W2"], v["L1_ffn_b1"])}
    for k, parts in PACKS.items():
        packed = np.zeros((P, WIDTH[k]), np.float32)
        for name, rows, cols in parts:
            r, at, c = LAYOUT[k][name]
            packed[:r, at:at + c] = pieces[name]
        arrays[k] = packed
    nc = bacc.Bacc("TRN2", target_bir_lowering=False, num_devices=1)
    dram = {k: nc.dram_tensor(f"in_{k}", a.shape, mybir.dt.float32, kind="ExternalInput").ap() for k, a in arrays.items()}
    out = nc.dram_tensor("out", (TOK, D), mybir.dt.float32, kind="ExternalOutput").ap()
    build(nc, dram, out)
    r = run_bass_kernel_spmd(nc, [{f"in_{k}": a for k, a in arrays.items()}], core_ids=[0])
    return r.results[0]["out"].reshape(B, S, D)
```
